# Optimizing a Trainium2 kernel written in Bass

```python
import numpy as np
import jax
import jax.numpy as jnp

def _softmax(x, axis=-1):
    return jax.nn.softmax(x, axis=axis)

def _gelu(x):
    return jax.nn.gelu(x, approximate=True)

def _silu(x):
    return jax.nn.silu(x)

def _sigmoid(x):
    return jax.nn.sigmoid(x)

def _layernorm(x, axis=-1, eps=1e-05):
    m = jnp.mean(x, axis=axis, keepdims=True)
    v = jnp.var(x, axis=axis, keepdims=True)
    return (x - m) / jnp.sqrt(v + eps)

def _scatter_add(tgt, idx, src, axis=0):
    return tgt.at[idx].add(src)

def _segment_sum(src, seg, n):
    return jax.ops.segment_sum(src, seg, n)
kernel_name = 'mk_conv_preact_d2_conv_nhwc768_r2_c73782'

def setup_inputs(seed: int=0):
    np.random.seed(seed)
    _w = jnp.asarray

    def _rec_inputs():
        import jax
        import jax.numpy as jnp
        _gk = jax.random.key(seed)
        x = -0.0005058 + 1 * jax.random.normal(jax.random.fold_in(_gk, 1), (2, 48, 48, 384), jnp.float32)
        return x
    x = _rec_inputs()

    def _L0_conv_setup():
        import jax, jax.numpy as jnp
        import numpy as np
        D_MODEL = 384
        D_HEAD = 32
        N_HEADS = D_MODEL // D_HEAD
        KERNEL = 7
        NEG_INF = -1e+30

        def make_neighbourhood_mask(kernel_h, kernel_w, canvas_h, canvas_w):
            h_ramp = jnp.arange(canvas_h)
            w_ramp = jnp.arange(canvas_w)
            h_pos, w_pos = jnp.meshgrid(h_ramp, w_ramp, indexing='ij')
            start_h = jnp.clip(h_pos - kernel_h // 2, 0, canvas_h - kernel_h)[..., None, None]
            end_h = start_h + kernel_h
            start_w = jnp.clip(w_pos - kernel_w // 2, 0, canvas_w - kernel_w)[..., None, None]
            end_w = start_w + kernel_w
            h_range = h_ramp.reshape(1, 1, canvas_h, 1)
            w_range = w_ramp.reshape(1, 1, 1, canvas_w)
            mask = (h_range >= start_h) & (h_range < end_h) & (w_range >= start_w) & (w_range < end_w)
            return mask.reshape(canvas_h * canvas_w, canvas_h * canvas_w)
        key = jax.random.key(seed)
        k1, k2, k3, k4, k5, k6 = jax.random.split(key, 6)
        x = jax.random.normal(k1, (2, 48, 48, D_MODEL), dtype=jnp.float32)
        registers = jax.random.normal(k2, (16, D_MODEL), dtype=jnp.float32)
        scale = 1.0 / np.sqrt(D_MODEL)
        qkv_w = jax.random.normal(k3, (3 * D_MODEL, D_MODEL), dtype=jnp.float32) * scale
        qkv_b = jax.random.normal(k4, (3 * D_MODEL,), dtype=jnp.float32) * 0.01
        out_w = jax.random.normal(k5, (D_MODEL, D_MODEL), dtype=jnp.float32) * scale
        out_b = jax.random.normal(k6, (D_MODEL,), dtype=jnp.float32) * 0.01
        return {'x': x, 'registers': registers, 'qkv_w': qkv_w, 'qkv_b': qkv_b, 'out_w': out_w, 'out_b': out_b}
    _L0_conv_all = _L0_conv_setup()
    _L0_conv_in = {k: v for k, v in _L0_conv_all.items() if k in ('registers', 'qkv_w', 'qkv_b', 'out_w', 'out_b')}
    del _L0_conv_all

    def _L1_conv_setup():
        import jax, jax.numpy as jnp
        import numpy as np
        NUM_HEADS = 12

        def _rel_pos_table(rel_pos, size):
            coords = jnp.arange(size)[:, None] - jnp.arange(size)[None, :] + (size - 1)
            return rel_pos[coords]
        key = jax.random.key(seed)
        ks = jax.random.split(key, 7)
        B, H, W, C = (8, 32, 32, 384)
        hd = C // NUM_HEADS
        return {'x': jax.random.normal(ks[0], (B, H, W, C), jnp.float32), 'qkv_w': jax.random.normal(ks[1], (3 * C, C), jnp.float32) * 0.02, 'qkv_b': jax.random.normal(ks[2], (3 * C,), jnp.float32) * 0.02, 'proj_w': jax.random.normal(ks[3], (C, C), jnp.float32) * 0.02, 'proj_b': jax.random.normal(ks[4], (C,), jnp.float32) * 0.02, 'rel_pos_h': jax.random.normal(ks[5], (2 * H - 1, hd), jnp.float32) * 0.02, 'rel_pos_w': jax.random.normal(ks[6], (2 * W - 1, hd), jnp.float32) * 0.02}
    _L1_conv_all = _L1_conv_setup()
    _L1_conv_in = {k: v for k, v in _L1_conv_all.items() if k in ('qkv_w', 'qkv_b', 'proj_w', 'proj_b', 'rel_pos_h', 'rel_pos_w')}
    del _L1_conv_all
    return {'x': x, 'L0_conv_registers': _L0_conv_in['registers'], 'L0_conv_qkv_w': _L0_conv_in['qkv_w'], 'L0_conv_qkv_b': _L0_conv_in['qkv_b'], 'L0_conv_out_w': _L0_conv_in['out_w'], 'L0_conv_out_b': _L0_conv_in['out_b'], 'L1_conv_qkv_w': _L1_conv_in['qkv_w'], 'L1_conv_qkv_b': _L1_conv_in['qkv_b'], 'L1_conv_proj_w': _L1_conv_in['proj_w'], 'L1_conv_proj_b': _L1_conv_in['proj_b'], 'L1_conv_rel_pos_h': _L1_conv_in['rel_pos_h'], 'L1_conv_rel_pos_w': _L1_conv_in['rel_pos_w']}

def reference(x, L0_conv_registers, L0_conv_qkv_w, L0_conv_qkv_b, L0_conv_out_w, L0_conv_out_b, L1_conv_qkv_w, L1_conv_qkv_b, L1_conv_proj_w, L1_conv_proj_b, L1_conv_rel_pos_h, L1_conv_rel_pos_w):
    import jax
    import jax.numpy as jnp

    def _L0_conv_ref(x, registers, qkv_w, qkv_b, out_w, out_b):
        import jax, jax.numpy as jnp
        import numpy as np
        D_MODEL = 384
        D_HEAD = 32
        N_HEADS = D_MODEL // D_HEAD
        KERNEL = 7
        NEG_INF = -1e+30

        def make_neighbourhood_mask(kernel_h, kernel_w, canvas_h, canvas_w):
            h_ramp = jnp.arange(canvas_h)
            w_ramp = jnp.arange(canvas_w)
            h_pos, w_pos = jnp.meshgrid(h_ramp, w_ramp, indexing='ij')
            start_h = jnp.clip(h_pos - kernel_h // 2, 0, canvas_h - kernel_h)[..., None, None]
            end_h = start_h + kernel_h
            start_w = jnp.clip(w_pos - kernel_w // 2, 0, canvas_w - kernel_w)[..., None, None]
            end_w = start_w + kernel_w
            h_range = h_ramp.reshape(1, 1, canvas_h, 1)
            w_range = w_ramp.reshape(1, 1, 1, canvas_w)
            mask = (h_range >= start_h) & (h_range < end_h) & (w_range >= start_w) & (w_range < end_w)
            return mask.reshape(canvas_h * canvas_w, canvas_h * canvas_w)
        n, h, w, _ = x.shape
        nh, e = (N_HEADS, D_HEAD)
        s = h * w
        r = registers.shape[0]
        qkv = x @ qkv_w.T + qkv_b
        qkv = qkv.reshape(n, h, w, 3, nh, e)
        qkv = qkv.transpose(3, 0, 4, 1, 2, 5).reshape(3, n, nh, s, e)
        q, k, v = (qkv[0], qkv[1], qkv[2])
        reg_kv = registers @ qkv_w[D_MODEL:].T + qkv_b[D_MODEL:]
        reg_kv = reg_kv.reshape(r, 2, nh, e).transpose(1, 2, 0, 3)
        reg_k = jnp.broadcast_to(reg_kv[0][None], (n, nh, r, e))
        reg_v = jnp.broadcast_to(reg_kv[1][None], (n, nh, r, e))
        k_cat = jnp.concatenate([k, reg_k], axis=-2)
        v_cat = jnp.concatenate([v, reg_v], axis=-2)
        mask = make_neighbourhood_mask(KERNEL, KERNEL, h, w)
        mask_cat = jnp.concatenate([mask, jnp.ones((s, r), dtype=bool)], axis=-1)
        scale = 1.0 / jnp.sqrt(jnp.asarray(e, dtype=x.dtype))
        scores = jnp.einsum('bnqe,bnke->bnqk', q, k_cat) * scale
        scores = jnp.where(mask_cat[None, None], scores, NEG_INF)
        attn = jax.nn.softmax(scores, axis=-1)
        o = jnp.einsum('bnqk,bnke->bnqe', attn, v_cat)
        o = o.transpose(0, 2, 1, 3).reshape(n, h, w, nh * e)
        return o @ out_w.T + out_b

    def _L1_conv_ref(x, qkv_w, qkv_b, proj_w, proj_b, rel_pos_h, rel_pos_w):
        import jax, jax.numpy as jnp
        import numpy as np
        NUM_HEADS = 12

        def _rel_pos_table(rel_pos, size):
            coords = jnp.arange(size)[:, None] - jnp.arange(size)[None, :] + (size - 1)
            return rel_pos[coords]
        B, H, W, C = x.shape
        nh = NUM_HEADS
        hd = C // nh
        scale = hd ** (-0.5)
        N = H * W
        qkv = jnp.einsum('bhwc,oc->bhwo', x, qkv_w) + qkv_b
        qkv = qkv.reshape(B, N, 3, nh, hd).transpose(2, 0, 3, 1, 4)
        qkv = qkv.reshape(3, B * nh, N, hd)
        q, k, v = (qkv[0], qkv[1], qkv[2])
        q = q * scale
        attn = jnp.einsum('bqd,bkd->bqk', q, k)
        Rh = _rel_pos_table(rel_pos_h, H)
        Rw = _rel_pos_table(rel_pos_w, W)
        r_q = q.reshape(B * nh, H, W, hd)
        rel_h = jnp.einsum('bhwc,hkc->bhwk', r_q, Rh)
        rel_w = jnp.einsum('bhwc,wkc->bhwk', r_q, Rw)
        attn = (attn.reshape(B * nh, H, W, H, W) + rel_h[:, :, :, :, None] + rel_w[:, :, :, None, :]).reshape(B * nh, N, N)
        attn = jax.nn.softmax(attn, axis=-1)
        out = jnp.einsum('bqk,bkd->bqd', attn, v)
        out = out.reshape(B, nh, H, W, hd).transpose(0, 2, 3, 1, 4).reshape(B, H, W, C)
        out = jnp.einsum('bhwc,oc->bhwo', out, proj_w) + proj_b
        return out

    def _gn(v, G=32, eps=1e-05):
        B_, H_, W_, C_ = v.shape
        g = v.reshape(B_, H_, W_, G, C_ // G)
        m = jnp.mean(g, axis=(1, 2, 4), keepdims=True)
        s = jnp.var(g, axis=(1, 2, 4), keepdims=True)
        return ((g - m) / jnp.sqrt(s + eps)).reshape(v.shape)

    def _ln_c(v, eps=1e-06):
        m = jnp.mean(v, axis=-1, keepdims=True)
        s = jnp.var(v, axis=-1, keepdims=True)
        return (v - m) / jnp.sqrt(s + eps)

    def _ln_t(v, eps=1e-05):
        m = jnp.mean(v, axis=-1, keepdims=True)
        s = jnp.var(v, axis=-1, keepdims=True)
        return (v - m) / jnp.sqrt(s + eps)

    def _to_tokens(v):
        B_, H_, W_, C_ = v.shape
        return v.reshape(B_, H_ * W_, C_)

    def _from_tokens(t, like):
        return t.reshape(like.shape)
    x = x + _L0_conv_ref(_gn(x), L0_conv_registers, L0_conv_qkv_w, L0_conv_qkv_b, L0_conv_out_w, L0_conv_out_b)
    x = x + _L1_conv_ref(_gn(x), L1_conv_qkv_w, L1_conv_qkv_b, L1_conv_proj_w, L1_conv_proj_b, L1_conv_rel_pos_h, L1_conv_rel_pos_w)
    return x

_drawn_inputs = setup_inputs


def setup_inputs(seed=0):
    import zlib

    import numpy as np

    out = dict(_drawn_inputs(seed))
    spreads = {}
    factors = {'L0_conv_qkv_b': 6.238,
     'L0_conv_out_b': 5.218,
     'L1_conv_qkv_w': 4.283,
     'L1_conv_qkv_b': 7.631,
     'L1_conv_proj_w': 3.289,
     'L1_conv_proj_b': 2.91,
     'L1_conv_rel_pos_h': 8.0,
     'L1_conv_rel_pos_w': 8.0}
    for name, (base, spread) in spreads.items():
        noise = np.random.default_rng([zlib.crc32(name.encode()), seed]).standard_normal(out[name].shape)
        drawn = base * np.exp(spread * noise) if base else spread * noise
        out[name] = jnp.asarray(drawn.astype(out[name].dtype))
    for name, factor in factors.items():
        out[name] = (out[name] * factor).astype(out[name].dtype)
    return out
```

```python
from contextlib import ExitStack

import numpy as np
import concourse.bass as bass
from concourse import mybir

F32 = mybir.dt.float32
F16 = mybir.dt.float16
BF16 = mybir.dt.bfloat16
ACT = mybir.ActivationFunctionType
ALU = mybir.AluOpType
AX = mybir.AxisListType

B, SIDE, C = 2, 48, 384
TOK = SIDE * SIDE
ALL = B * TOK
HEADS, D = 12, 32
REGS, WINDOW = 16, 7
CT = C // 128
GROUPS = 32
HPT = 128 // D
EPS = 1e-5
Q_SCALE = float(D) ** -0.5

KR, KC = 8, 16
NA, NS = SIDE // KR, SIDE // KC
TILES = NA * NS
STRIP = SIDE * KC
UNIT = KR * SIDE
PIECE = 384
PIECES = TOK // PIECE
QT = UNIT // 128
HALO = WINDOW // 2
VW = 3 * D
BIG = 32768.0
STAGES = HEADS * B

B_ROWS = 2 * SIDE + 1
M_ROW = 2 * SIDE


def window_of(tile, size, limit):
    return max(0, tile * size - HALO), min(limit, (tile + 1) * size + HALO)


def rects(a):
    out = []
    for c in range(NS):
        lo, hi = window_of(c, KC, SIDE)
        at = 0
        for ka, r0, r1 in ((a, 0, KR), (a - 1, 0, HALO), (a + 1, KR - HALO, KR)):
            if 0 <= ka < NA:
                out.append((c, ka, r0, r1, lo, hi, at))
                at += (r1 - r0) * (hi - lo)
    return out


def rect_width(a, c):
    return sum((r1 - r0) * (hi - lo) for s, _, r0, r1, lo, hi, _ in rects(a) if s == c)


def shape_constants():
    t = np.arange(TOK)
    strip, row, col = t // STRIP, (t % STRIP) // KC, t % KC
    one_a = np.zeros((32, TOK + REGS), np.float16)
    for i in range(KC):
        one_a[i, :TOK] = one_a[KC + i, :TOK] = col == i
    one_b = np.zeros((B_ROWS, NA + 1, 128), np.float16)
    for a in range(NA):
        for k in range(128):
            one_b[a * KR + k // KC, a, k] = one_b[SIDE + a * KR + k // KC, a, k] = 1
    one_m = np.zeros((2 * SIDE, TOK + REGS), np.float16)
    one_m[t // SIDE, t] = 1
    one_m[SIDE + t % SIDE, t] = 1
    pos = np.arange(SIDE)
    start = np.clip(pos - HALO, 0, SIDE - WINDOW)
    outside = ~((pos[:, None] >= start[None]) & (pos[:, None] < start[None] + WINDOW))
    far = np.where(outside, -BIG, 0.0).astype(np.float16)
    far_row = far[:, t // SIDE]
    far_col = far[:, t % SIDE]
    mask_a = np.zeros((32, NS, TOK), np.float16)
    for c in range(NS):
        mask_a[:KC, c] = far_col[c * KC:(c + 1) * KC]
    mask_b = np.concatenate([far_row, np.zeros_like(far_row)])
    by_strip = row * SIDE + strip * KC + col
    mask_m = np.concatenate([far_row, far_col])[:, by_strip]
    ones_row = np.zeros((B_ROWS, NA + 1, 128), np.float16)
    ones_row[M_ROW] = 1
    group = np.arange(C) // (C // GROUPS)
    share = (group[:, None] == group[None]).astype(np.float32) / (C // GROUPS)
    share = share.reshape(CT, 128, C).transpose(1, 0, 2).copy()
    big = np.float16(BIG)
    return {
        "one_a0": one_a * big, "one_a1": one_a, "one_b0": one_b * big + ones_row,
        "one_b1": one_b + ones_row, "one_m0": one_m * big, "one_m1": one_m,
        "mask_a": mask_a, "mask_b": mask_b, "mask_m": mask_m, "share": share,
        "ident": np.eye(128, dtype=np.float16),
    }


def group_norm(nc, ctx, x, layer, dram, sem):
    stats = ctx.enter_context(nc.sbuf_tensor(f"stats{layer}", [128, CT * B * NA, 6], F32))
    chan = ctx.enter_context(nc.sbuf_tensor(f"chan{layer}", [128, CT * B, 2], F32))
    share = ctx.enter_context(nc.sbuf_tensor(f"share{layer}", [128, CT, C], F32))
    means = ctx.enter_context(nc.sbuf_tensor(f"means{layer}", [128, CT, B], F32))
    second = ctx.enter_context(nc.sbuf_tensor(f"second{layer}", [128, CT, B], F32))
    off = ctx.enter_context(nc.sbuf_tensor(f"off{layer}", [128, CT, B], F32))
    gmean = ctx.enter_context(nc.sbuf_tensor(f"gmean{layer}", [128, CT, B], F32))
    gvar = ctx.enter_context(nc.sbuf_tensor(f"gvar{layer}", [128, CT, B], F32))
    sd = ctx.enter_context(nc.sbuf_tensor(f"sd{layer}", [128, CT, B], F32))
    rstd = ctx.enter_context(nc.sbuf_tensor(f"rstd{layer}", [128, CT, B], F32))
    sums = ctx.enter_context(nc.psum_tensor(f"sums{layer}", [128, 2, 512], F32))
    x_in = [sem(f"x_in{layer}_{i}") for i in range(CT * B)]
    share_in = sem(f"share_in{layer}")
    chain = sem(f"gn_chain{layer}")
    second_ready = sem(f"second_ready{layer}")
    means_ready = sem(f"means_ready{layer}")
    mean_sum = sem(f"mean_sum{layer}")
    var_sum = sem(f"var_sum{layer}")
    var_ready = sem(f"var_ready{layer}")
    sd_ready = sem(f"sd_ready{layer}")

    with nc.Block() as block:
        @block.sync
        def _(sp):
            if layer == 0:
                for i in range(CT * B):
                    t, b = i // B, i % B
                    sp.dma_start(x[:, t, b * TOK:(b + 1) * TOK],
                                 dram["x"][t * 128:(t + 1) * 128, b * TOK:(b + 1) * TOK]).then_inc(x_in[i], 16)
            sp.dma_start(share[:, :, :], dram["share"]).then_inc(share_in, 16)

        @block.vector
        def _(dve):
            steps = [0]

            def link(ins):
                steps[0] += 1
                ins.then_inc(chain, 1)
                dve.wait_ge(chain, steps[0])

            for i in range(CT * B):
                t, b = i // B, i % B
                if layer == 0:
                    dve.wait_ge(x_in[i], 16)
                for a in range(NA):
                    at = b * TOK + a * UNIT
                    last = nc.vector.bn_stats(stats[:, i * NA + a, :], x[:, t, at:at + UNIT])
            link(last)
            for i in range(CT * B):
                last = nc.vector.bn_aggr(chan[:, i, :], stats[:, i * NA:(i + 1) * NA, :])
            link(last)
            by_chan = chan[:, :, :].rearrange("p (t b) s -> p t b s", b=B)
            nc.vector.tensor_copy(means[:, :, :], by_chan[:, :, :, 0]).then_inc(means_ready, 1)
            dve.wait_ge(mean_sum, 1)
            link(nc.vector.tensor_copy(gmean[:, :, :], sums[:, 0, 0:CT * B].rearrange("p (t b) -> p t b", b=B)))
            link(nc.vector.tensor_tensor(off[:, :, :], by_chan[:, :, :, 0], gmean[:, :, :], ALU.subtract))
            link(nc.vector.tensor_tensor(off[:, :, :], off[:, :, :], off[:, :, :], ALU.mult))
            nc.vector.tensor_tensor(second[:, :, :], off[:, :, :], by_chan[:, :, :, 1],
                                    ALU.add).then_inc(second_ready, 1)
            dve.wait_ge(var_sum, 1)
            nc.vector.tensor_scalar(gvar[:, :, :], sums[:, 1, 0:CT * B].rearrange("p (t b) -> p t b", b=B),
                                    EPS, None, ALU.add).then_inc(var_ready, 1)
            dve.wait_ge(sd_ready, 1)
            link(nc.vector.reciprocal(rstd[:, :, :], sd[:, :, :]))
            for i in range(CT * B):
                t, b = i // B, i % B
                nc.vector.tensor_scalar(x[:, t, b * TOK:(b + 1) * TOK], x[:, t, b * TOK:(b + 1) * TOK],
                                        gmean[:, t, b:b + 1], rstd[:, t, b:b + 1], ALU.subtract, ALU.mult)

        @block.tensor
        def _(pe):
            pe.wait_ge(share_in, 16)
            for ready, done, src, bank in ((means_ready, mean_sum, means, 0), (second_ready, var_sum, second, 1)):
                pe.wait_ge(ready, 1)
                for to in range(CT):
                    for t in range(CT):
                        last = nc.tensor.matmul(sums[:, bank, to * B:(to + 1) * B],
                                                share[:, t, to * 128:(to + 1) * 128], src[:, t, :],
                                                start=(t == 0), stop=(t == CT - 1))
                last.then_inc(done, 1)

        @block.scalar
        def _(act):
            act.wait_ge(var_ready, 1)
            nc.scalar.activation(sd[:, :, :], gvar[:, :, :], ACT.Sqrt).then_inc(sd_ready, 1)


def project(nc, ctx, x, values, layer, dram, sem):
    regs = REGS if layer == 0 else 0
    w = ctx.enter_context(nc.sbuf_tensor(f"w{layer}", [128, CT, 3 * C], F32))
    bias = ctx.enter_context(nc.sbuf_tensor(f"bias{layer}", [128, 2 * CT], F32))
    q_bias = ctx.enter_context(nc.sbuf_tensor(f"q_bias{layer}", [128, CT], F32))
    v_bias = ctx.enter_context(nc.sbuf_tensor(f"v_bias{layer}", [128, C], F32))
    full = ctx.enter_context(nc.sbuf_tensor(f"full{layer}", [128, 3, UNIT], F32))
    v_full = ctx.enter_context(nc.sbuf_tensor(f"v_full{layer}", [128, 3, C], F32))
    high = ctx.enter_context(nc.sbuf_tensor(f"high{layer}", [128, 2, TOK + REGS], F16))
    low = ctx.enter_context(nc.sbuf_tensor(f"low{layer}", [128, 2, TOK + REGS], F16))
    other = ctx.enter_context(nc.sbuf_tensor(f"other{layer}", [128, 2, TOK + REGS], F16))
    acc = ctx.enter_context(nc.psum_tensor(f"acc{layer}", [128, 8, 512], F32))
    w_in = sem(f"w_in{layer}")
    acc_ready = sem(f"acc_ready{layer}")
    full_ready = sem(f"full_ready{layer}")
    bias_ready = sem(f"bias_ready{layer}")
    high_ready = sem(f"high_ready{layer}")
    low_ready = sem(f"low_ready{layer}")
    other_ready = sem(f"other_ready{layer}")
    stored = [sem(f"stored{layer}_{i}") for i in range(2)]
    v_acc_ready = sem(f"v_acc_ready{layer}")
    v_full_ready = sem(f"v_full_ready{layer}")
    v_high_ready = sem(f"v_high_ready{layer}")
    v_low_ready = sem(f"v_low_ready{layer}")

    blocks = [(m, b) for m in range(2 * CT) for b in range(B)]

    def chunks(m, b):
        return NA + (1 if regs and m >= CT and b == 0 else 0)

    def width(a):
        return UNIT if a < NA else regs

    def source(b, a):
        return (b * TOK + a * UNIT) if a < NA else ALL

    def by_strip(buf, a):
        return buf[:, TOK:TOK + REGS] if a == NA else buf[:, a * UNIT:(a + 1) * UNIT]

    def by_row(buf, a):
        if a == NA:
            return buf[:, TOK:TOK + REGS]
        rows = UNIT // KC
        c, r = a * rows // SIDE, a * rows % SIDE
        return buf[:, 0:TOK].rearrange("p (r c s) -> p c r s", c=NS, s=KC)[:, c, r:r + rows]

    def as_rows(ap, a):
        return ap if a == NA else ap.rearrange("p (r s) -> p r s", s=KC)

    def store_count(i):
        out = 0
        for j in range(i % 2, i + 1, 2):
            m, b = blocks[j]
            out += 16 * 3 * (2 if chunks(m, b) > NA else 1)
        return out

    v_tiles = [(b, j) for b in range(B) for j in range(TILES)] + ([(B, 0)] if regs else [])
    total = sum(chunks(m, b) for m, b in blocks)

    with nc.Block() as block:
        @block.sync
        def _(sp):
            sp.dma_start(w[:, :, :], dram[f"w{layer}"].rearrange("(t p) n -> p t n", p=128)).then_inc(w_in, 16)
            sp.dma_start(bias[:, :], dram[f"b{layer}"][:, 0:2 * CT]).then_inc(w_in, 16)
            sp.dma_start(v_bias[:, :], dram[f"vb{layer}"]).then_inc(w_in, 16)
            if regs:
                sp.dma_start(x[:, :, ALL:ALL + REGS],
                             dram["registers"].rearrange("(t p) n -> p t n", p=128)).then_inc(w_in, 16)
            done = 0
            for i, (m, b) in enumerate(blocks):
                done += chunks(m, b)
                sp.wait_ge(high_ready, done)
                sp.wait_ge(low_ready, done)
                par = i % 2
                rows = slice((m % CT) * 128, (m % CT + 1) * 128)
                n = TOK + (regs if chunks(m, b) > NA else 0)
                sp.wait_ge(other_ready, done)
                which = "q" if m < CT else "k"
                for name, buf in ((which + "_high", high), (which + "_low", low), (which + "_other", other)):
                    sp.dma_start(dram[name][rows, b, 0:TOK], buf[:, par, 0:TOK]).then_inc(stored[par], 16)
                    if n > TOK:
                        sp.dma_start(dram[name + "_regs"][rows, :], buf[:, par, TOK:n]).then_inc(stored[par], 16)
            for par in range(2):
                sp.wait_ge(stored[par], store_count(len(blocks) - 2 + par))

        @block.tensor
        def _(pe):
            pe.wait_ge(w_in, 16 * (4 if regs else 3))
            n = 0
            for m, b in blocks:
                for a in range(chunks(m, b)):
                    if n >= 4:
                        pe.wait_ge(full_ready, n - 3)
                    at = source(b, a)
                    for t in range(CT):
                        last = nc.tensor.matmul(acc[:, n % 4, 0:width(a)], w[:, t, m * 128:(m + 1) * 128],
                                                x[:, t, at:at + width(a)], start=(t == 0), stop=(t == CT - 1))
                    last.then_inc(acc_ready, 1)
                    n += 1
            for n, (b, j) in enumerate(v_tiles):
                if n >= 4:
                    pe.wait_ge(v_full_ready, n - 3)
                for t in range(CT):
                    if b < B:
                        at = b * TOK + j * 128
                        keys = x[:, t, at:at + 128]
                        dst = acc[:, 4 + n % 4, 0:C]
                    else:
                        keys = x[:, t, ALL:ALL + REGS]
                        dst = acc[0:REGS, 4 + n % 4, 0:C]
                    last = nc.tensor.matmul(dst, keys, w[:, t, 2 * C:3 * C], start=(t == 0), stop=(t == CT - 1))
                last.then_inc(v_acc_ready, 1)

        @block.scalar
        def _(act):
            act.wait_ge(w_in, 16 * (4 if regs else 3))
            nc.scalar.activation(q_bias[:, :], bias[:, 0:CT], ACT.Identity, scale=Q_SCALE).then_inc(bias_ready, 1)
            act.wait_ge(bias_ready, 1)
            n = 0
            for m, b in blocks:
                for a in range(chunks(m, b)):
                    act.wait_ge(acc_ready, n + 1)
                    if n >= 3:
                        act.wait_ge(low_ready, n - 2)
                        act.wait_ge(other_ready, n - 2)
                    col = q_bias[:, m:m + 1] if m < CT else bias[:, m:m + 1]
                    nc.scalar.activation(full[:, n % 3, 0:width(a)], acc[:, n % 4, 0:width(a)], ACT.Identity,
                                         bias=col, scale=Q_SCALE if m < CT else 1.0).then_inc(full_ready, 1)
                    n += 1
            for n, (b, j) in enumerate(v_tiles):
                act.wait_ge(v_full_ready, n + 1)
                p = 128 if b < B else REGS
                tile = b * TILES + j
                nc.scalar.activation(values[0:p, tile, :, 0:D],
                                     v_full[0:p, n % 3, :].rearrange("p (h d) -> p h d", d=D),
                                     ACT.Identity).then_inc(v_high_ready, 1)

        @block.vector
        def _(dve):
            n = 0
            for i, (m, b) in enumerate(blocks):
                par = i % 2
                if i >= 2:
                    dve.wait_ge(stored[par], store_count(i - 2))
                for a in range(chunks(m, b)):
                    src = full[:, n % 3, 0:width(a)]
                    if m < CT:
                        src = as_rows(src, a)
                        hi, lo = by_row(high[:, par, :], a), by_row(low[:, par, :], a)
                    else:
                        hi, lo = by_strip(high[:, par, :], a), by_strip(low[:, par, :], a)
                    dve.wait_ge(full_ready, n + 1)
                    nc.vector.tensor_copy(hi, src).then_inc(high_ready, 1)
                    dve.wait_ge(high_ready, n + 1)
                    nc.vector.tensor_tensor(lo, src, hi, ALU.subtract).then_inc(low_ready, 1)
                    n += 1
            for n, (b, j) in enumerate(v_tiles):
                p = 128 if b < B else REGS
                tile = b * TILES + j
                dve.wait_ge(v_acc_ready, n + 1)
                if n >= 3:
                    dve.wait_ge(v_low_ready, n - 2)
                nc.vector.tensor_tensor(v_full[0:p, n % 3, :], acc[0:p, 4 + n % 4, 0:C], v_bias[0:p, :],
                                        ALU.add).then_inc(v_full_ready, 1)

        @block.gpsimd
        def _(pool):
            n = 0
            for i, (m, b) in enumerate(blocks):
                par = i % 2
                for a in range(chunks(m, b)):
                    if a == 0 and i >= 2:
                        pool.wait_ge(stored[par], store_count(i - 2))
                    pool.wait_ge(full_ready, n + 1)
                    src = full[:, n % 3, 0:width(a)]
                    if m < CT:
                        dst = by_strip(other[:, par, :], a)
                    else:
                        dst, src = by_row(other[:, par, :], a), as_rows(src, a)
                    nc.gpsimd.tensor_copy(dst, src).then_inc(other_ready, 1)
                    n += 1
            for n, (b, j) in enumerate(v_tiles):
                p = 128 if b < B else REGS
                tile = b * TILES + j
                pool.wait_ge(v_high_ready, n + 1)
                nc.gpsimd.tensor_tensor(values[0:p, tile, :, D:2 * D],
                                        v_full[0:p, n % 3, :].rearrange("p (h d) -> p h d", d=D),
                                        values[0:p, tile, :, 0:D], ALU.subtract).then_inc(v_low_ready, 1)


def position_bias(nc, ctx, dram, sem):
    GQ = 4
    NG = SIDE // GQ
    table32 = ctx.enter_context(nc.sbuf_tensor("table32", [128, 2, 2 * SIDE], F32))
    table_hi = ctx.enter_context(nc.sbuf_tensor("table_hi", [128, 2, 2 * SIDE], F16))
    table = ctx.enter_context(nc.sbuf_tensor("table", [128, 2, 2 * SIDE], F16))
    q = ctx.enter_context(nc.sbuf_tensor("q_parts", [128, 2, B, TOK], F16))
    hi = ctx.enter_context(nc.sbuf_tensor("bias_hi", [SIDE, 2, B, TOK], F16))
    lo = ctx.enter_context(nc.sbuf_tensor("bias_lo", [SIDE, 2, B, TOK], F16))
    acc = ctx.enter_context(nc.psum_tensor("bias_acc", [128, 8, 512], F32))
    tables_in = sem("tables_in")
    table_hi_ready = sem("table_hi_ready")
    table_ready = sem("table_ready")
    q_in = [sem(f"q_in{i}") for i in range(2)]
    acc_ready = sem("bias_acc_ready")
    hi_ready = sem("bias_hi_ready")
    lo_ready = sem("bias_lo_ready")
    stored = [sem(f"bias_stored{i}") for i in range(2)]

    def groups():
        return [(axis, g) for axis in range(2) for g in range(NG)]

    def banked(n, axis):
        v = acc[0:SIDE, n % 8, 0:B * GQ * SIDE].rearrange("p (b g x) -> p b g x", b=B, g=GQ)
        return v if axis == 0 else v.rearrange("p b g x -> p b x g")

    def placed(buf, axis, g):
        if axis == 0:
            return buf[:, axis, :, g * GQ * SIDE:(g + 1) * GQ * SIDE].rearrange("p b (g x) -> p b g x", g=GQ)
        return buf[:, axis, :, :].rearrange("p b (x w) -> p b x w", w=SIDE)[:, :, :, g * GQ:(g + 1) * GQ]

    with nc.Block() as block:
        @block.sync
        def _(sp):
            for part in range(3):
                sp.dma_start(table32[part * D:(part + 1) * D, :, 0:2 * SIDE - 1], dram["tables"]).then_inc(tables_in, 16)

            def load(h, par):
                for part, name in enumerate(("q_high", "q_high", "q_low")):
                    sp.dma_start(q[part * D:(part + 1) * D, par], dram[name][bass.ds(h * D, D)]).then_inc(q_in[par], 16)

            def store(h, axis):
                sp.wait_ge(lo_ready, h * 2 * NG + (axis + 1) * NG)
                if axis == 0:
                    sp.dma_start(dram["row_bias"][bass.ds(h, 1), 0:SIDE].rearrange("o p b n -> (o p) b n"),
                                 hi[:, 0]).then_inc(stored[0], 16)
                    sp.dma_start(dram["row_bias"][bass.ds(h, 1), SIDE:2 * SIDE].rearrange("o p b n -> (o p) b n"),
                                 lo[:, 0]).then_inc(stored[0], 16)
                else:
                    for c in range(NS):
                        for part, buf in enumerate((hi, lo)):
                            sp.dma_start(
                                dram["col_bias"][bass.ds(h, 1), part * KC:(part + 1) * KC, c]
                                .rearrange("o p b n -> (o p) b n"),
                                buf[c * KC:(c + 1) * KC, 1]).then_inc(stored[1], 16)

            def two_heads(h, more):
                sp.wait_ge(acc_ready, h * 2 * NG)
                load(h + 1, 1)
                for axis in range(2):
                    store(h, axis)
                if more:
                    load(h + 2, 0)
                for axis in range(2):
                    store(h + 1, axis)

            load(0, 0)
            with sp.Fori(0, HEADS // 2 - 1) as pair:
                two_heads(pair * 2, True)
            two_heads(HEADS - 2, False)
            for axis, n in ((0, 2), (1, 2 * NS)):
                sp.wait_ge(stored[axis], 16 * n * HEADS)

        @block.tensor
        def _(pe):
            pe.wait_ge(table_ready, 2)
            with pe.Fori(0, HEADS // 2) as pair:
                for par in range(2):
                    h = pair * 2 + par
                    pe.wait_ge(q_in[par], (pair + 1) * 48)
                    for n, (axis, g) in enumerate(groups()):
                        if par == 0 and n < 8:
                            pe.wait_ge(lo_ready, pair * 4 * NG)
                        else:
                            pe.wait_ge(lo_ready, h * 2 * NG + n - 7)
                        for j in range(GQ):
                            x = g * GQ + j
                            dst = acc[0:SIDE, n % 8, 0:B * GQ * SIDE] \
                                .rearrange("p (b g x) -> p b g x", b=B, g=GQ)[:, :, j]
                            src = q[0:3 * D, par].rearrange("p b (r w) -> p b r w", w=SIDE)
                            src = src[:, :, x, :] if axis == 0 else src[:, :, :, x]
                            last = nc.tensor.matmul(dst, table[0:3 * D, axis, SIDE - 1 - x:2 * SIDE - 1 - x], src,
                                                    start=True, stop=True)
                        last.then_inc(acc_ready, 1)

        @block.scalar
        def _(act):
            with act.Fori(0, HEADS) as h:
                for n, (axis, g) in enumerate(groups()):
                    if g == 0:
                        act.wait_ge(stored[axis], h * (32 if axis == 0 else 32 * NS))
                    act.wait_ge(acc_ready, h * 2 * NG + n + 1)
                    nc.scalar.activation(placed(hi, axis, g), banked(n, axis), ACT.Identity).then_inc(hi_ready, 1)

        @block.vector
        def _(dve):
            dve.wait_ge(tables_in, 48)
            used = table32[0:3 * D, :, 0:2 * SIDE - 1]
            parts = table_hi[0:3 * D, :, 0:2 * SIDE - 1]
            nc.vector.tensor_copy(parts, used).then_inc(table_hi_ready, 1)
            dve.wait_ge(table_hi_ready, 1)
            nc.vector.tensor_copy(table[0:3 * D, :, 0:2 * SIDE - 1], parts).then_inc(table_hi_ready, 1)
            dve.wait_ge(table_hi_ready, 2)
            nc.vector.tensor_tensor(table[D:2 * D, :, 0:2 * SIDE - 1], table32[D:2 * D, :, 0:2 * SIDE - 1],
                                    table_hi[D:2 * D, :, 0:2 * SIDE - 1], ALU.subtract).then_inc(table_ready, 2)
            with dve.Fori(0, HEADS) as h:
                for n, (axis, g) in enumerate(groups()):
                    dve.wait_ge(hi_ready, h * 2 * NG + n + 1)
                    nc.vector.tensor_tensor(placed(lo, axis, g), banked(n, axis), placed(hi, axis, g),
                                            ALU.subtract).then_inc(lo_ready, 1)


def attention(nc, ctx, values, layer, dram, sem):
    local = layer == 0
    keys_n = TOK + (REGS if local else 0)
    key_tiles = TILES + (1 if local else 0)
    SLOT = 4 * UNIT if local else 2 * UNIT
    RING = 2 if local else 3
    q_a = ctx.enter_context(nc.sbuf_tensor(f"q_a{layer}", [128, 2, NS, TOK], F16))
    q_b = ctx.enter_context(nc.sbuf_tensor(f"q_b{layer}", [B_ROWS, 2, TOK], F16))
    k_a = ctx.enter_context(nc.sbuf_tensor(f"k_a{layer}", [128, 2, keys_n], F16))
    k_b = ctx.enter_context(nc.sbuf_tensor(f"k_b{layer}", [B_ROWS, NA + 1, 128], F16))
    q_m = ctx.enter_context(nc.sbuf_tensor(f"q_m{layer}", [128, 2, TOK], F16))
    k_m = ctx.enter_context(nc.sbuf_tensor(f"k_m{layer}", [128, 2, keys_n], F16))
    v = ctx.enter_context(nc.sbuf_tensor(f"v{layer}", [128, 2, key_tiles, VW], F16))
    ident = ctx.enter_context(nc.sbuf_tensor(f"ident{layer}", [128, 128], F16))
    prob = ctx.enter_context(nc.sbuf_tensor(f"prob{layer}", [128, RING, SLOT], F32))
    prob_low = ctx.enter_context(nc.sbuf_tensor(f"prob_low{layer}", [128, RING, SLOT], F16))
    part_max = ctx.enter_context(nc.sbuf_tensor(f"part_max{layer}", [128, QT, PIECES], F32))
    tile_max = ctx.enter_context(nc.sbuf_tensor(f"tile_max{layer}", [128, QT], F32))
    neg_max = ctx.enter_context(nc.sbuf_tensor(f"neg_max{layer}", [128, QT], F16))
    warm = ctx.enter_context(nc.sbuf_tensor(f"warm{layer}", [1, 1], F32))
    result = ctx.enter_context(nc.sbuf_tensor(f"result{layer}", [VW, 2, UNIT], F32))
    scores = ctx.enter_context(nc.psum_tensor(f"scores{layer}", [128, 4, 512], F32))
    max_acc = ctx.enter_context(nc.psum_tensor(f"max_acc{layer}", [128, 2, 512], F32))
    max_row = ctx.enter_context(nc.psum_tensor(f"max_row{layer}", [128, 512], F32))
    out_acc = ctx.enter_context(nc.psum_tensor(f"out_acc{layer}", [128, 512], F32))

    consts_in = sem(f"consts_in{layer}")
    main_in = [sem(f"main_in{layer}_{i}") for i in range(2)]
    max_in = [sem(f"max_in{layer}_{i}") for i in range(2)]
    v_ready = sem(f"v_ready{layer}")
    score_ready = sem(f"score_ready{layer}")
    prob_ready = sem(f"prob_ready{layer}")
    low_by_dve = sem(f"low_by_dve{layer}")
    low_by_pool = sem(f"low_by_pool{layer}")
    prob_used = sem(f"prob_used{layer}")
    piece_ready = sem(f"piece_ready{layer}")
    piece_done = sem(f"piece_done{layer}")
    tile_done = sem(f"tile_done{layer}")
    neg_ready = sem(f"neg_ready{layer}")
    row_ready = sem(f"row_ready{layer}")
    row_written = sem(f"row_written{layer}")
    result_ready = sem(f"result_ready{layer}")
    result_out = [sem(f"result_out{layer}_{i}") for i in range(2)]

    PAIRS = TILES // 2
    STEPS = NA if local else NA * PAIRS
    STEP_PIECES = QT if local else 2
    MAXP = STEPS * STEP_PIECES
    SCORES = NA * (NS + 1) if local else STEPS

    def sources(stage_h, b):
        return lambda name: dram[name][bass.ds(stage_h * D, D), b]

    def piece_rhs(p, i):
        r0, r1 = window_of(p, KR, SIDE)
        c0, c1 = window_of(i, KC, SIDE)
        return r0, r1, c0, c1

    with nc.Block() as block:
        @block.sync
        def _(sp):
            sp.dma_start(k_b[:, :, :], dram[f"one_b{layer}"]).then_inc(consts_in, 16)
            sp.dma_start(ident[:, :], dram["ident"]).then_inc(consts_in, 16)
            for par in range(2):
                sp.dma_start(k_a[96:128, par], dram[f"one_a{layer}"][:, 0:keys_n]).then_inc(consts_in, 16)
                sp.dma_start(k_m[32:128, par], dram[f"one_m{layer}"][:, 0:keys_n]).then_inc(consts_in, 16)
                if local:
                    sp.dma_start(q_a[96:128, par], dram["mask_a"]).then_inc(consts_in, 16)
                    sp.dma_start(q_b[0:2 * SIDE, par], dram["mask_b"]).then_inc(consts_in, 16)
                    sp.dma_start(q_m[32:128, par], dram["mask_m"]).then_inc(consts_in, 16)

            def load_main(h, b):
                src = sources(h, b)
                for part, name in enumerate(("q_high", "q_high", "q_low")):
                    rows = slice(part * D, (part + 1) * D)
                    sp.dma_start(q_a[rows, b], src(name).unsqueeze(1).to_broadcast((D, NS, TOK))) \
                        .then_inc(main_in[b], 16)
                for part, name in enumerate(("k_high", "k_low", "k_high")):
                    rows = slice(part * D, (part + 1) * D)
                    sp.dma_start(k_a[rows, b, 0:TOK], src(name)).then_inc(main_in[b], 16)
                if local:
                    for part, name in enumerate(("k_high", "k_low", "k_high")):
                        rows = slice(part * D, (part + 1) * D)
                        sp.dma_start(k_a[rows, b, TOK:keys_n],
                                     dram[name + "_regs"][bass.ds(h * D, D)]).then_inc(main_in[b], 16)
                else:
                    sp.dma_start(q_a[96:128, b],
                                 dram["col_bias"][bass.ds(h, 1), :, :, b].rearrange("o p c n -> (o p) c n")) \
                        .then_inc(main_in[b], 16)
                    sp.dma_start(q_b[0:2 * SIDE, b],
                                 dram["row_bias"][bass.ds(h, 1), :, b].rearrange("o p n -> (o p) n")) \
                        .then_inc(main_in[b], 16)

            def load_max(h, b):
                src = sources(h, b)
                sp.dma_start(q_m[0:D, b], src("q_other" if local else "q_high")).then_inc(max_in[b], 16)
                sp.dma_start(k_m[0:D, b, 0:TOK], src("k_other")).then_inc(max_in[b], 16)
                if local:
                    sp.dma_start(k_m[0:D, b, TOK:keys_n],
                                 dram["k_other_regs"][bass.ds(h * D, D)]).then_inc(max_in[b], 16)
                else:
                    sp.dma_start(q_m[D:D + SIDE, b],
                                 dram["row_bias"][bass.ds(h, 1), 0:SIDE, b].rearrange("o p n -> (o p) n")) \
                        .then_inc(max_in[b], 16)
                    for c in range(NS):
                        at = D + SIDE + c * KC
                        sp.dma_start(q_m[at:at + KC, b],
                                     dram["col_bias"][bass.ds(h, 1), 0:KC, c, b].rearrange("o p n -> (o p) n")) \
                            .then_inc(max_in[b], 16)

            def store(h, b, a):
                sp.wait_ge(result_ready, (h * B + b) * NA + a + 1)
                sp.dma_start(dram["result"][bass.ds(h * B + b, 1)].rearrange("o p (c n) -> (o p) c n", c=NS)
                             [:, :, a * 128:(a + 1) * 128],
                             result[:, a % 2].rearrange("p (c n) -> p c n", c=NS)).then_inc(result_out[a % 2], 16)

            load_max(0, 0)
            load_max(0, 1)
            load_main(0, 0)

            def stage(h, b, more):
                n = h * B + b
                if more or b == 0:
                    sp.wait_ge(prob_used, n * STEPS)
                    load_main(h + b, 1 - b)
                if more:
                    sp.wait_ge(row_written, (n + 1) * NA)
                    load_max(h + 1, b)
                for a in range(NA):
                    store(h, b, a)

            with sp.Fori(0, HEADS - 1) as h:
                for b in range(B):
                    stage(h, b, True)
            for b in range(B):
                stage(HEADS - 1, b, False)
            for i in range(2):
                sp.wait_ge(result_out[i], 16 * STAGES * NA // 2)

        MAIN = 16 * (9 if local else 8)
        MAXL = 16 * (3 if local else 6)
        CONSTS = 16 * (2 + 2 * (5 if local else 2))

        @block.tensor
        def _(pe):
            def max_pieces(k, b, base):
                for j in range(STEP_PIECES):
                    i = k * STEP_PIECES + j
                    if isinstance(base, int):
                        if base + i >= 2:
                            pe.wait_ge(piece_done, base + i - 1)
                    else:
                        pe.wait_ge(piece_done, base + (i - 1))
                    bank = max_acc[:, i % 2]
                    if local:
                        r0, r1, c0, c1 = piece_rhs(k, j)
                        n = (r1 - r0) * (c1 - c0)
                        at = j * STRIP + k * 128
                        queries = q_m[:, b, at:at + 128]
                        keys = k_m[:, b, 0:TOK].rearrange("p (r w) -> p r w", w=SIDE)[:, r0:r1, c0:c1]
                        nc.tensor.matmul(bank[:, 0:n], queries, keys, start=True, stop=True)
                        last = nc.tensor.matmul(bank[:, n:n + REGS], queries, k_m[:, b, TOK:keys_n],
                                                start=True, stop=True)
                    else:
                        tile, piece = i // PIECES, i % PIECES
                        last = nc.tensor.matmul(bank[:, 0:PIECE], q_m[:, b, tile * 128:(tile + 1) * 128],
                                                k_m[:, b, piece * PIECE:(piece + 1) * PIECE],
                                                start=True, stop=True)
                    last.then_inc(piece_ready, 1)

            def row_of_max(count):
                pe.wait_ge(neg_ready, count + 1)
                if not isinstance(count, int) or count > 0:
                    pe.wait_ge(row_written, count)
                for i in range(QT):
                    last = nc.tensor.matmul(max_row[0:1, i * 128:(i + 1) * 128], neg_max[:, i:i + 1], ident[:, :],
                                            start=True, stop=True)
                last.then_inc(row_ready, 1)

            pe.wait_ge(consts_in, CONSTS)
            pe.wait_ge(max_in[0], MAXL)
            per_unit = STEPS // NA
            for a in range(NA):
                for k in range(a * per_unit, (a + 1) * per_unit):
                    max_pieces(k, 0, 0)
                row_of_max(a)

            def key_product(bank, rows, tile, queries_a, queries_b, b):
                keys = k_a[:, b, tile * 128:min((tile + 1) * 128, keys_n)]
                nc.tensor.matmul(bank, keys, queries_a, start=True, stop=False)
                return nc.tensor.matmul(bank, k_b[:, tile % NA if tile < TILES else NA, 0:rows], queries_b,
                                        start=False, stop=True)

            def scores_full(n, b, p):
                a, k = p // PAIRS, p % PAIRS
                if k == 0:
                    pe.wait_ge(row_written, n * NA + a + 1)
                if p < 2:
                    pe.wait_ge(prob_ready, n * STEPS)
                else:
                    pe.wait_ge(prob_ready, n * STEPS + p - 1)
                for j in range(2):
                    tile = 2 * k + j
                    last = key_product(scores[:, 2 * (p % 2) + j, 0:UNIT], 128, tile,
                                       q_a[:, b, tile // NA, a * UNIT:(a + 1) * UNIT],
                                       q_b[:, b, a * UNIT:(a + 1) * UNIT], b)
                last.then_inc(score_ready, 1)

            def weighted_full(n, b, p):
                a, k = p // PAIRS, p % PAIRS
                if p % 3 == 2:
                    pe.wait_ge(low_by_pool, n * (STEPS // 3) + p // 3 + 1)
                else:
                    pe.wait_ge(low_by_dve, n * (STEPS // 3 * 2) + p // 3 * 2 + p % 3 + 1)
                if k == 0:
                    pe.wait_ge(result_ready, n * NA + a)
                for j in range(2):
                    tile = 2 * k + j
                    top = prob[:, p % RING, :].bitcast(BF16)[:, 1::2][:, j * UNIT:(j + 1) * UNIT]
                    nc.tensor.matmul(out_acc[0:VW, 0:UNIT], v[:, b, tile, :], top,
                                     start=(tile == 0), stop=False)
                    last = nc.tensor.matmul(out_acc[0:VW, 0:UNIT], v[:, b, tile, :],
                                            prob_low[:, p % RING, j * UNIT:(j + 1) * UNIT],
                                            start=False, stop=(tile == TILES - 1))
                last.then_inc(prob_used, 1)

            def scores_local(n, b, a):
                pe.wait_ge(row_written, n * NA + a + 1)
                for c in range(NS + 1):
                    if a == 0:
                        pe.wait_ge(prob_ready, n * SCORES)
                    else:
                        pe.wait_ge(prob_ready, n * SCORES + (a - 1) * (NS + 1) + c + 1)
                    if c == NS:
                        last = key_product(scores[0:REGS, c, 0:UNIT], REGS, TILES,
                                           q_a[:, b, 0, a * UNIT:(a + 1) * UNIT],
                                           q_b[:, b, a * UNIT:(a + 1) * UNIT], b)
                    else:
                        for s, ka, r0, r1, lo, hi, at in rects(a):
                            if s != c:
                                continue
                            qa = q_a[:, b, c, a * UNIT:(a + 1) * UNIT].rearrange("p (r w) -> p r w", w=SIDE)
                            qb = q_b[:, b, a * UNIT:(a + 1) * UNIT].rearrange("p (r w) -> p r w", w=SIDE)
                            w = (r1 - r0) * (hi - lo)
                            last = key_product(scores[:, c, at:at + w], 128, c * NA + ka,
                                               qa[:, r0:r1, lo:hi], qb[:, r0:r1, lo:hi], b)
                    last.then_inc(score_ready, 1)

            def weighted_local(n, b, a):
                pe.wait_ge(low_by_dve, n * NA + a + 1)
                pe.wait_ge(result_ready, n * NA + a)
                tops = prob[:, a % RING, :].bitcast(BF16)[:, 1::2]
                at = NS * UNIT
                nc.tensor.matmul(out_acc[0:VW, 0:UNIT], v[0:REGS, b, TILES, :], tops[0:REGS, at:at + UNIT],
                                 start=True, stop=False)
                nc.tensor.matmul(out_acc[0:VW, 0:UNIT], v[0:REGS, b, TILES, :],
                                 prob_low[0:REGS, a % RING, at:at + UNIT], start=False, stop=False)
                todo = rects(a)
                for i, (c, ka, r0, r1, lo, hi, at) in enumerate(todo):
                    w = (r1 - r0) * (hi - lo)
                    dst = out_acc[0:VW, 0:UNIT].rearrange("p (r w) -> p r w", w=SIDE)[:, r0:r1, lo:hi]
                    at += c * UNIT
                    nc.tensor.matmul(dst, v[:, b, c * NA + ka, :], tops[:, at:at + w], start=False, stop=False)
                    last = nc.tensor.matmul(dst, v[:, b, c * NA + ka, :], prob_low[:, a % RING, at:at + w],
                                            start=False, stop=(i == len(todo) - 1))
                last.then_inc(prob_used, 1)

            compute, use, lag = (scores_local, weighted_local, 1) if local else (scores_full, weighted_full, 2)

            def stage(h, b, more):
                n = h * B + b
                pe.wait_ge(main_in[b], (h + 1) * MAIN)
                if more:
                    pe.wait_ge(max_in[1 - b], (h + 1 + b) * MAXL)
                pe.wait_ge(v_ready, n + 1)
                for k in range(STEPS):
                    compute(n, b, k)
                    if more:
                        max_pieces(k, 1 - b, (n + 1) * MAXP)
                    if k >= lag:
                        use(n, b, k - lag)
                    if more and k >= per_unit and k % per_unit == min(2, per_unit - 1):
                        row_of_max((n + 1) * NA + k // per_unit - 1)
                for k in range(STEPS - lag, STEPS):
                    use(n, b, k)
                if more:
                    row_of_max((n + 1) * NA + NA - 1)

            with pe.Fori(0, HEADS - 1) as h:
                for b in range(B):
                    stage(h, b, True)
            stage(HEADS - 1, 0, True)
            stage(HEADS - 1, 1, False)

        @block.scalar
        def _(act):
            per_unit = STEPS // NA

            def write_row(count, a, b):
                act.wait_ge(row_ready, count + 1)
                dst = q_b[M_ROW:M_ROW + 1, b, a * UNIT:(a + 1) * UNIT]
                src = max_row[0:1, 0:UNIT]
                if local:
                    dst = dst.rearrange("p (r c s) -> p c r s", c=NS, s=KC)
                    src = src.rearrange("p (c r s) -> p c r s", c=NS, s=KC)
                nc.scalar.activation(dst, src, ACT.Identity).then_inc(row_written, 1)

            def take_result(n, a):
                act.wait_ge(prob_used, n * STEPS + (a + 1) * per_unit)
                if not isinstance(n, int) or n * NA + a >= 2:
                    act.wait_ge(result_out[a % 2], (n * (NA // 2) + a // 2) * 16)
                nc.scalar.activation(result[:, a % 2].rearrange("p (c r s) -> p c r s", c=NS, s=KC),
                                     out_acc[0:VW, 0:UNIT].rearrange("p (r c s) -> p c r s", c=NS, s=KC),
                                     ACT.Identity).then_inc(result_ready, 1)

            act.wait_ge(consts_in, CONSTS)
            nc.scalar.activation(warm[:, :], ident[0:1, 0:1], ACT.Exp)
            for a in range(NA):
                write_row(a, a, 0)

            def exps(n, k):
                if local:
                    for c in range(NS + 1):
                        act.wait_ge(score_ready, n * SCORES + k * (NS + 1) + c + 1)
                        if c == 0 and k >= RING:
                            act.wait_ge(prob_used, n * STEPS + k - RING + 1)
                        p = 128 if c < NS else REGS
                        w = rect_width(k, c) if c < NS else UNIT
                        nc.scalar.activation(prob[0:p, k % RING, c * UNIT:c * UNIT + w], scores[0:p, c, 0:w],
                                             ACT.Exp).then_inc(prob_ready, 1)
                else:
                    act.wait_ge(score_ready, n * STEPS + k + 1)
                    if k >= RING:
                        act.wait_ge(prob_used, n * STEPS + k - RING + 1)
                    nc.scalar.activation(prob[:, k % RING, :].rearrange("p (j n) -> p j n", j=2),
                                         scores[:, 2 * (k % 2):2 * (k % 2) + 2, 0:UNIT],
                                         ACT.Exp).then_inc(prob_ready, 1)

            def stage(h, b, more):
                n = h * B + b
                lag = 1 if local else 2
                for k in range(STEPS):
                    exps(n, k)
                    u = k // per_unit - 1
                    if u >= 0 and k % per_unit == lag - 1:
                        take_result(n, u)
                    if more and u >= 0 and k % per_unit == min(3, per_unit - 1):
                        write_row((n + 1) * NA + u, u, 1 - b)
                take_result(n, NA - 1)
                if more:
                    write_row((n + 1) * NA + NA - 1, NA - 1, 1 - b)

            with act.Fori(0, HEADS - 1) as h:
                for b in range(B):
                    stage(h, b, True)
            stage(HEADS - 1, 0, True)
            stage(HEADS - 1, 1, False)

        @block.vector
        def _(dve):
            per_unit = STEPS // NA

            def maxima(k, count):
                for j in range(STEP_PIECES):
                    i = k * STEP_PIECES + j
                    dve.wait_ge(piece_ready, count + (i + 1))
                    if local:
                        r0, r1, c0, c1 = piece_rhs(k, j)
                        w = (r1 - r0) * (c1 - c0) + REGS
                        dst = tile_max[:, j:j + 1]
                    else:
                        w = PIECE
                        u = i % (QT * PIECES)
                        dst = part_max[:, u // PIECES, u % PIECES:u % PIECES + 1]
                    nc.vector.reduce_max(dst, max_acc[:, i % 2, 0:w], axis=AX.X).then_inc(piece_done, 1)

            def unit_max(unit, pieces):
                dve.wait_ge(piece_done, pieces)
                if not local:
                    nc.vector.reduce_max(tile_max[:, :], part_max[:, :, :], axis=AX.X).then_inc(tile_done, 1)
                    dve.wait_ge(tile_done, unit + 1)
                if not isinstance(unit, int) or unit > 0:
                    dve.wait_ge(row_ready, unit)
                nc.vector.tensor_scalar(neg_max[:, :], tile_max[:, :], -1.0, None, ALU.mult).then_inc(neg_ready, 1)
                dve.wait_ge(neg_ready, unit + 1)

            def low_part(n, k):
                if local:
                    dve.wait_ge(prob_ready, n * SCORES + (k + 1) * (NS + 1))
                    for c in range(NS + 1):
                        p = 128 if c < NS else REGS
                        w = rect_width(k, c) if c < NS else UNIT
                        at = c * UNIT
                        if c < NS:
                            last = nc.vector.tensor_tensor(
                                prob_low[0:p, k % RING, at:at + w], prob[0:p, k % RING, at:at + w],
                                prob[0:p, k % RING, :].bitcast(BF16)[:, 1::2][:, at:at + w], ALU.subtract)
                        else:
                            last = nc.vector.tensor_tensor(
                                prob_low[0:p, k % RING, at:at + w], prob[0:p, k % RING, at:at + w],
                                prob[0:p, k % RING, :].bitcast(BF16)[:, 1::2][:, at:at + w], ALU.subtract)
                    last.then_inc(low_by_dve, 1)
                elif k % 3 != 2:
                    dve.wait_ge(prob_ready, n * STEPS + k + 1)
                    nc.vector.tensor_tensor(prob_low[:, k % RING, :], prob[:, k % RING, :],
                                            prob[:, k % RING, :].bitcast(BF16)[:, 1::2],
                                            ALU.subtract).then_inc(low_by_dve, 1)

            for a in range(NA):
                for k in range(a * per_unit, (a + 1) * per_unit):
                    maxima(k, 0)
                unit_max(a, (a + 1) * per_unit * STEP_PIECES)

            def stage(h, b, more):
                n = h * B + b
                for k in range(STEPS):
                    if more:
                        maxima(k, (n + 1) * MAXP)
                    if not local and k > 0:
                        low_part(n, k - 1)
                    if local:
                        low_part(n, k)
                    if more and k % per_unit == per_unit - 1:
                        unit_max((n + 1) * NA + k // per_unit, (n + 1) * MAXP + (k + 1) * STEP_PIECES)
                if not local:
                    low_part(n, STEPS - 1)

            with dve.Fori(0, HEADS - 1) as h:
                for b in range(B):
                    stage(h, b, True)
            stage(HEADS - 1, 0, True)
            stage(HEADS - 1, 1, False)

        @block.gpsimd
        def _(pool):
            for par in range(2):
                last = nc.gpsimd.memset(v[:, par, :, 2 * D:VW], 1.0)
            pool.drain()

            def copy_values(h, b):
                cols = values[:, b * TILES:(b + 1) * TILES, bass.ds(h, 1)].rearrange("p t o n -> p t (o n)")
                if local:
                    nc.gpsimd.tensor_copy(v[:, b, 0:TILES, 0:2 * D], cols)
                    regs = values[0:REGS, B * TILES:B * TILES + 1, bass.ds(h, 1)].rearrange("p t o n -> p t (o n)")
                    nc.gpsimd.tensor_copy(v[0:REGS, b, TILES:TILES + 1, 0:2 * D], regs).then_inc(v_ready, 1)
                else:
                    nc.gpsimd.tensor_copy(v[:, b, 0:TILES, 0:2 * D], cols).then_inc(v_ready, 1)

            copy_values(0, 0)

            def stage(h, b, more):
                n = h * B + b
                if more:
                    pool.wait_ge(prob_used, n * STEPS)
                    copy_values(h + b, 1 - b)
                if not local:
                    for k in range(2, STEPS, 3):
                        pool.wait_ge(prob_ready, n * STEPS + k + 1)
                        nc.gpsimd.tensor_tensor(prob_low[:, k % RING, :], prob[:, k % RING, :],
                                                prob[:, k % RING, :].bitcast(BF16)[:, 1::2],
                                                ALU.subtract).then_inc(low_by_pool, 1)

            with pool.Fori(0, HEADS - 1) as h:
                for b in range(B):
                    stage(h, b, True)
            stage(HEADS - 1, 0, True)
            stage(HEADS - 1, 1, False)


def mix(nc, ctx, x, layer, dram, sem):
    w = ctx.enter_context(nc.sbuf_tensor(f"ow{layer}", [128, CT, C], F32))
    bias = ctx.enter_context(nc.sbuf_tensor(f"ob{layer}", [128, CT], F32))
    parts = ctx.enter_context(nc.sbuf_tensor(f"parts{layer}", [128, 2, 3, CT, UNIT], F32))
    inv = ctx.enter_context(nc.sbuf_tensor(f"inv{layer}", [128, 2, CT, UNIT], F32))
    heads = ctx.enter_context(nc.sbuf_tensor(f"heads{layer}", [128, 2, CT, UNIT], F32))
    normed = ctx.enter_context(nc.sbuf_tensor(f"normed{layer}", [128, 2, CT, UNIT], F32))
    acc = ctx.enter_context(nc.psum_tensor(f"mix_acc{layer}", [128, 2, 4, 512], F32))
    w_in = sem(f"ow_in{layer}")
    x_back = sem(f"x_back{layer}")
    parts_in = [sem(f"parts_in{layer}_{i}") for i in range(2)]
    inv_ready = sem(f"inv_ready{layer}")
    heads_ready = sem(f"heads_ready{layer}")
    normed_ready = sem(f"normed_ready{layer}")
    mixed = sem(f"mixed{layer}")
    added = sem(f"added{layer}")
    out_done = sem(f"out_done{layer}")
    UNITS = B * NA
    src_x = dram["x"] if layer == 0 else dram["x1"]
    dst_x = dram["x1"] if layer == 0 else dram["out"]

    with nc.Block() as block:
        @block.sync
        def _(sp):
            sp.dma_start(w[:, :, :], dram[f"ow{layer}"].rearrange("(t p) n -> p t n", p=128)).then_inc(w_in, 16)
            sp.dma_start(bias[:, :], dram[f"ob{layer}"]).then_inc(w_in, 16)
            for u in range(UNITS):
                b, a = u // NA, u % NA
                if u >= 2:
                    sp.wait_ge(normed_ready, u - 1)
                for kind in range(3):
                    for t in range(CT):
                        for i in range(HPT):
                            stage = (t * HPT + i) * B + b
                            sp.dma_start(parts[i * D:(i + 1) * D, u % 2, kind, t],
                                         dram["result"][stage, kind * D:(kind + 1) * D,
                                                        a * UNIT:(a + 1) * UNIT]).then_inc(parts_in[u % 2], 16)
                if u == 0:
                    sp.dma_start(x[:, :, 0:ALL], src_x.rearrange("(t p) n -> p t n", p=128)).then_inc(x_back, 16)
                if u >= 1:
                    v = u - 1
                    at = v * UNIT
                    sp.wait_ge(added, v + 1)
                    sp.dma_start(dst_x[:, at:at + UNIT].rearrange("(t p) n -> p t n", p=128),
                                 x[:, :, at:at + UNIT]).then_inc(out_done, 16)
            at = (UNITS - 1) * UNIT
            sp.wait_ge(added, UNITS)
            sp.dma_start(dst_x[:, at:at + UNIT].rearrange("(t p) n -> p t n", p=128),
                         x[:, :, at:at + UNIT]).then_inc(out_done, 16)
            sp.wait_ge(out_done, 16 * UNITS)

        @block.gpsimd
        def _(pool):
            for u in range(UNITS):
                pool.wait_ge(parts_in[u % 2], 16 * 3 * CT * HPT * (u // 2 + 1))
                if u >= 2:
                    pool.wait_ge(normed_ready, u - 1)
                nc.gpsimd.tensor_tensor(heads[:, u % 2], parts[:, u % 2, 0], parts[:, u % 2, 1],
                                        ALU.add).then_inc(heads_ready, 1)

        @block.vector
        def _(dve):
            def add(u):
                dve.wait_ge(mixed, u + 1)
                for to in range(CT):
                    dst = x[:, to, u * UNIT:(u + 1) * UNIT]
                    last = nc.vector.scalar_tensor_tensor(dst, acc[:, u % 2, to, 0:UNIT], bias[:, to:to + 1], dst,
                                                          ALU.add, ALU.add)
                last.then_inc(added, 1)

            dve.wait_ge(w_in, 32)
            for u in range(UNITS):
                dve.wait_ge(parts_in[u % 2], 16 * 3 * CT * HPT * (u // 2 + 1))
                nc.vector.reciprocal(inv[:, u % 2], parts[:, u % 2, 2]).then_inc(inv_ready, 1)
                dve.wait_ge(inv_ready, u + 1)
                dve.wait_ge(heads_ready, u + 1)
                if u >= 2:
                    dve.wait_ge(mixed, u - 1)
                nc.vector.tensor_tensor(normed[:, u % 2], heads[:, u % 2], inv[:, u % 2],
                                        ALU.mult).then_inc(normed_ready, 1)
                if u == 0:
                    dve.wait_ge(x_back, 16)
                else:
                    add(u - 1)
            add(UNITS - 1)

        @block.tensor
        def _(pe):
            pe.wait_ge(w_in, 32)
            for u in range(UNITS):
                pe.wait_ge(normed_ready, u + 1)
                if u >= 2:
                    pe.wait_ge(added, u - 1)
                for to in range(CT):
                    for t in range(CT):
                        last = nc.tensor.matmul(acc[:, u % 2, to, 0:UNIT], w[:, t, to * 128:(to + 1) * 128],
                                                normed[:, u % 2, t], start=(t == 0), stop=(t == CT - 1))
                last.then_inc(mixed, 1)


def build(nc, dram):
    def scratch(name, shape, dtype):
        dram[name] = nc.dram_tensor(name, shape, dtype, kind="Internal").ap()

    for name in ("q_high", "q_low", "q_other", "k_high", "k_low", "k_other"):
        scratch(name, (C, B, TOK), F16)
    for name in ("k_high_regs", "k_low_regs", "k_other_regs"):
        scratch(name, (C, REGS), F16)
    scratch("row_bias", (HEADS, 2 * SIDE, B, TOK), F16)
    scratch("col_bias", (HEADS, 2 * KC, NS, B, TOK), F16)
    scratch("result", (STAGES, VW, TOK), F32)
    scratch("x1", (C, ALL), F32)

    with ExitStack() as whole:
        x = whole.enter_context(nc.sbuf_tensor("x", [128, CT, ALL + REGS], F32))
        values = whole.enter_context(nc.sbuf_tensor("values", [128, B * TILES + 1, HEADS, 2 * D], F16))

        for layer in range(2):
            def phase(work, *args):
                with ExitStack() as ctx:
                    def sem(name):
                        return ctx.enter_context(nc.semaphore(name))

                    work(nc, ctx, *args, dram, sem)

            phase(group_norm, x, layer)
            phase(project, x, values, layer)
            if layer == 1:
                phase(position_bias)
            phase(attention, values, layer)
            phase(mix, x, layer)


def kernel(**inputs):
    import concourse.bacc as bacc
    from concourse.bass_utils import run_bass_kernel_spmd

    def array(name):
        return np.asarray(inputs[name])

    reach = np.minimum(2 * SIDE - 2 - np.arange(2 * SIDE - 1), array("L1_conv_rel_pos_h").shape[0] - 1)
    arrays = {
        "x": array("x").reshape(B, SIDE, NS, KC, C).transpose(4, 0, 2, 1, 3).reshape(C, ALL),
        "registers": array("L0_conv_registers").T,
        "w0": array("L0_conv_qkv_w").T, "b0": array("L0_conv_qkv_b").reshape(3 * CT, 128).T,
        "vb0": np.broadcast_to(array("L0_conv_qkv_b")[2 * C:], (128, C)),
        "ow0": array("L0_conv_out_w").T, "ob0": array("L0_conv_out_b").reshape(CT, 128).T,
        "w1": array("L1_conv_qkv_w").T, "b1": array("L1_conv_qkv_b").reshape(3 * CT, 128).T,
        "vb1": np.broadcast_to(array("L1_conv_qkv_b")[2 * C:], (128, C)),
        "ow1": array("L1_conv_proj_w").T, "ob1": array("L1_conv_proj_b").reshape(CT, 128).T,
        "tables": np.stack([array("L1_conv_rel_pos_h")[reach].T, array("L1_conv_rel_pos_w")[reach].T], axis=1),
        **shape_constants(),
    }
    arrays = {name: np.ascontiguousarray(a) for name, a in arrays.items()}

    nc = bacc.Bacc("TRN2", target_bir_lowering=False, num_devices=1)
    dram = {name: nc.dram_tensor("in_" + name, a.shape, mybir.dt.from_np(a.dtype), kind="ExternalInput").ap()
            for name, a in arrays.items()}
    dram["out"] = nc.dram_tensor("out_x", (C, ALL), F32, kind="ExternalOutput").ap()
    build(nc, dram)
    r = run_bass_kernel_spmd(nc, [{"in_" + name: a for name, a in arrays.items()}], core_ids=[0])
    return np.ascontiguousarray(r.results[0]["out_x"].reshape(C, B, NS, SIDE, KC).transpose(1, 3, 2, 4, 0)
                                .reshape(B, SIDE, SIDE, C))
```

```python
from contextlib import ExitStack

import numpy as np
import concourse.bass as bass
from concourse import mybir

F32 = mybir.dt.float32
F16 = mybir.dt.float16
BF16 = mybir.dt.bfloat16
ACT = mybir.ActivationFunctionType
ALU = mybir.AluOpType
AX = mybir.AxisListType

B, SIDE, C = 2, 48, 384
TOK = SIDE * SIDE
ALL = B * TOK
HEADS, D = 12, 32
REGS, WINDOW = 16, 7
CT = C // 128
GROUPS = 32
HPT = 128 // D
EPS = 1e-5
Q_SCALE = float(D) ** -0.5

KR, KC = 8, 16
NA, NS = SIDE // KR, SIDE // KC
TILES = NA * NS
STRIP = SIDE * KC
UNIT = KR * SIDE
PIECE = 384
PIECES = TOK // PIECE
QT = UNIT // 128
HALO = WINDOW // 2
VW = 2 * D + 1
BIG = 32768.0
STAGES = HEADS * B

B_ROWS = 2 * SIDE + 1
M_ROW = 2 * SIDE


def due(count):
    return not isinstance(count, int) or count > 0


def each_stage(engine, stage):
    for b in range(B):
        stage(0, b)
    with engine.Fori(1, HEADS - 1) as h:
        for b in range(B):
            stage(h, b)
    for b in range(B):
        stage(HEADS - 1, b)


def window_of(tile, size, limit):
    return max(0, tile * size - HALO), min(limit, (tile + 1) * size + HALO)


def rects(a):
    out = []
    for c in range(NS):
        lo, hi = window_of(c, KC, SIDE)
        at = 0
        for ka, r0, r1 in ((a, 0, KR), (a - 1, 0, HALO), (a + 1, KR - HALO, KR)):
            if 0 <= ka < NA:
                out.append((c, ka, r0, r1, lo, hi, at))
                at += (r1 - r0) * (hi - lo)
    return out


def rect_width(a, c):
    return sum((r1 - r0) * (hi - lo) for s, _, r0, r1, lo, hi, _ in rects(a) if s == c)


def shape_constants():
    t = np.arange(TOK)
    strip, row, col = t // STRIP, (t % STRIP) // KC, t % KC
    one_a = np.zeros((32, TOK + REGS), np.float16)
    for i in range(KC):
        one_a[i, :TOK] = one_a[KC + i, :TOK] = col == i
    one_b = np.zeros((B_ROWS, NA + 1, 128), np.float16)
    for a in range(NA):
        for k in range(128):
            one_b[a * KR + k // KC, a, k] = one_b[SIDE + a * KR + k // KC, a, k] = 1
    one_m = np.zeros((2 * SIDE, TOK + REGS), np.float16)
    one_m[t // SIDE, t] = 1
    one_m[SIDE + t % SIDE, t] = 1
    pos = np.arange(SIDE)
    start = np.clip(pos - HALO, 0, SIDE - WINDOW)
    outside = ~((pos[:, None] >= start[None]) & (pos[:, None] < start[None] + WINDOW))
    far = np.where(outside, -BIG, 0.0).astype(np.float16)
    far_row = far[:, t // SIDE]
    far_col = far[:, t % SIDE]
    mask_a = np.zeros((32, NS, TOK), np.float16)
    for c in range(NS):
        mask_a[:KC, c] = far_col[c * KC:(c + 1) * KC]
    mask_b = np.concatenate([far_row, np.zeros_like(far_row)])
    by_strip = row * SIDE + strip * KC + col
    mask_m = np.concatenate([far_row, far_col])[:, by_strip]
    ones_row = np.zeros((B_ROWS, NA + 1, 128), np.float16)
    ones_row[M_ROW] = 1
    group = np.arange(C) // (C // GROUPS)
    share = (group[:, None] == group[None]).astype(np.float32) / (C // GROUPS)
    share = share.reshape(CT, 128, C).transpose(1, 0, 2).copy()
    spread = (np.arange(HEADS)[:, None] == np.arange(C)[None] % HEADS).astype(np.float32).reshape(HEADS, CT, 128)
    big = np.float16(BIG)
    return {
        "one_a0": one_a * big, "one_a1": one_a, "one_b0": one_b * big + ones_row,
        "one_b1": one_b + ones_row, "one_m0": one_m * big, "one_m1": one_m,
        "mask_a": mask_a, "mask_b": mask_b, "mask_m": mask_m, "share": share, "spread": spread,
        "ident": np.eye(128, dtype=np.float16),
    }


def group_norm(nc, ctx, x, layer, dram, sem):
    stats = ctx.enter_context(nc.sbuf_tensor(f"stats{layer}", [128, CT * B * NA, 6], F32))
    chan = ctx.enter_context(nc.sbuf_tensor(f"chan{layer}", [128, CT * B, 2], F32))
    share = ctx.enter_context(nc.sbuf_tensor(f"share{layer}", [128, CT, C], F32))
    means = ctx.enter_context(nc.sbuf_tensor(f"means{layer}", [128, CT, B], F32))
    second = ctx.enter_context(nc.sbuf_tensor(f"second{layer}", [128, CT, B], F32))
    off = ctx.enter_context(nc.sbuf_tensor(f"off{layer}", [128, CT, B], F32))
    gmean = ctx.enter_context(nc.sbuf_tensor(f"gmean{layer}", [128, CT, B], F32))
    gvar = ctx.enter_context(nc.sbuf_tensor(f"gvar{layer}", [128, CT, B], F32))
    sd = ctx.enter_context(nc.sbuf_tensor(f"sd{layer}", [128, CT, B], F32))
    rstd = ctx.enter_context(nc.sbuf_tensor(f"rstd{layer}", [128, CT, B], F32))
    sums = ctx.enter_context(nc.psum_tensor(f"sums{layer}", [128, 2, 512], F32))
    x_in = [sem(f"x_in{layer}_{i}") for i in range(CT * B)]
    share_in = sem(f"share_in{layer}")
    chain = sem(f"gn_chain{layer}")
    second_ready = sem(f"second_ready{layer}")
    means_ready = sem(f"means_ready{layer}")
    mean_sum = sem(f"mean_sum{layer}")
    var_sum = sem(f"var_sum{layer}")
    var_ready = sem(f"var_ready{layer}")
    sd_ready = sem(f"sd_ready{layer}")

    with nc.Block() as block:
        @block.sync
        def _(sp):
            if layer == 0:
                for i in range(CT * B):
                    t, b = i // B, i % B
                    sp.dma_start(x[:, t, b * TOK:(b + 1) * TOK],
                                 dram["x"][t * 128:(t + 1) * 128, b * TOK:(b + 1) * TOK]).then_inc(x_in[i], 16)
            sp.dma_start(share[:, :, :], dram["share"]).then_inc(share_in, 16)

        @block.vector
        def _(dve):
            steps = [0]

            def link(ins):
                steps[0] += 1
                ins.then_inc(chain, 1)
                dve.wait_ge(chain, steps[0])

            for i in range(CT * B):
                t, b = i // B, i % B
                if layer == 0:
                    dve.wait_ge(x_in[i], 16)
                for a in range(NA):
                    at = b * TOK + a * UNIT
                    last = nc.vector.bn_stats(stats[:, i * NA + a, :], x[:, t, at:at + UNIT])
            link(last)
            for i in range(CT * B):
                last = nc.vector.bn_aggr(chan[:, i, :], stats[:, i * NA:(i + 1) * NA, :])
            link(last)
            by_chan = chan[:, :, :].rearrange("p (t b) s -> p t b s", b=B)
            nc.vector.tensor_copy(means[:, :, :], by_chan[:, :, :, 0]).then_inc(means_ready, 1)
            dve.wait_ge(mean_sum, 1)
            link(nc.vector.tensor_copy(gmean[:, :, :], sums[:, 0, 0:CT * B].rearrange("p (t b) -> p t b", b=B)))
            link(nc.vector.tensor_tensor(off[:, :, :], by_chan[:, :, :, 0], gmean[:, :, :], ALU.subtract))
            link(nc.vector.tensor_tensor(off[:, :, :], off[:, :, :], off[:, :, :], ALU.mult))
            nc.vector.tensor_tensor(second[:, :, :], off[:, :, :], by_chan[:, :, :, 1],
                                    ALU.add).then_inc(second_ready, 1)
            dve.wait_ge(var_sum, 1)
            nc.vector.tensor_scalar(gvar[:, :, :], sums[:, 1, 0:CT * B].rearrange("p (t b) -> p t b", b=B),
                                    EPS, None, ALU.add).then_inc(var_ready, 1)
            dve.wait_ge(sd_ready, 1)
            link(nc.vector.reciprocal(rstd[:, :, :], sd[:, :, :]))
            for i in range(CT * B):
                t, b = i // B, i % B
                nc.vector.tensor_scalar(x[:, t, b * TOK:(b + 1) * TOK], x[:, t, b * TOK:(b + 1) * TOK],
                                        gmean[:, t, b:b + 1], rstd[:, t, b:b + 1], ALU.subtract, ALU.mult)

        @block.tensor
        def _(pe):
            pe.wait_ge(share_in, 16)
            for ready, done, src, bank in ((means_ready, mean_sum, means, 0), (second_ready, var_sum, second, 1)):
                pe.wait_ge(ready, 1)
                for to in range(CT):
                    for t in range(CT):
                        last = nc.tensor.matmul(sums[:, bank, to * B:(to + 1) * B],
                                                share[:, t, to * 128:(to + 1) * 128], src[:, t, :],
                                                start=(t == 0), stop=(t == CT - 1))
                last.then_inc(done, 1)

        @block.scalar
        def _(act):
            act.wait_ge(var_ready, 1)
            nc.scalar.activation(sd[:, :, :], gvar[:, :, :], ACT.Sqrt).then_inc(sd_ready, 1)


def project(nc, ctx, x, values, layer, dram, sem):
    regs = REGS if layer == 0 else 0
    w = ctx.enter_context(nc.sbuf_tensor(f"w{layer}", [128, CT, 3 * C], F32))
    bias = ctx.enter_context(nc.sbuf_tensor(f"bias{layer}", [128, 2 * CT], F32))
    q_bias = ctx.enter_context(nc.sbuf_tensor(f"q_bias{layer}", [128, CT], F32))
    v_bias = ctx.enter_context(nc.sbuf_tensor(f"v_bias{layer}", [128, C], F32))
    full = ctx.enter_context(nc.sbuf_tensor(f"full{layer}", [128, 3, UNIT], F32))
    v_full = ctx.enter_context(nc.sbuf_tensor(f"v_full{layer}", [128, 3, C], F32))
    high = ctx.enter_context(nc.sbuf_tensor(f"high{layer}", [128, 2, TOK + REGS], F16))
    low = ctx.enter_context(nc.sbuf_tensor(f"low{layer}", [128, 2, TOK + REGS], F16))
    other = ctx.enter_context(nc.sbuf_tensor(f"other{layer}", [128, 2, TOK + REGS], F16))
    acc = ctx.enter_context(nc.psum_tensor(f"acc{layer}", [128, 8, 512], F32))
    w_in = sem(f"w_in{layer}")
    acc_ready = sem(f"acc_ready{layer}")
    full_ready = sem(f"full_ready{layer}")
    bias_ready = sem(f"bias_ready{layer}")
    high_ready = sem(f"high_ready{layer}")
    low_ready = sem(f"low_ready{layer}")
    other_ready = sem(f"other_ready{layer}")
    stored = [sem(f"stored{layer}_{i}") for i in range(2)]
    v_acc_ready = sem(f"v_acc_ready{layer}")
    v_full_ready = sem(f"v_full_ready{layer}")
    v_high_ready = sem(f"v_high_ready{layer}")
    v_low_ready = sem(f"v_low_ready{layer}")

    blocks = [(m, b) for m in range(2 * CT) for b in range(B)]

    def chunks(m, b):
        return NA + (1 if regs and m >= CT and b == 0 else 0)

    def width(a):
        return UNIT if a < NA else regs

    def source(b, a):
        return (b * TOK + a * UNIT) if a < NA else ALL

    def by_strip(buf, a):
        return buf[:, TOK:TOK + REGS] if a == NA else buf[:, a * UNIT:(a + 1) * UNIT]

    def by_row(buf, a):
        if a == NA:
            return buf[:, TOK:TOK + REGS]
        rows = UNIT // KC
        c, r = a * rows // SIDE, a * rows % SIDE
        return buf[:, 0:TOK].rearrange("p (r c s) -> p c r s", c=NS, s=KC)[:, c, r:r + rows]

    def as_rows(ap, a):
        return ap if a == NA else ap.rearrange("p (r s) -> p r s", s=KC)

    def targets(m, bufs):
        hi, lo, order = bufs
        if m < CT:
            q, other_q = dram["q_parts"], dram["q_other"]
            return [(q[:, 0], hi), (q[:, 1], hi), (q[:, 2], lo)] + ([(other_q, order)] if layer == 0 else [])
        k = dram["k_parts"]
        return [(k[:, 0], hi), (k[:, 1], lo), (k[:, 2], hi), (dram["k_other"], order)]

    def store_count(i):
        out = 0
        for j in range(i % 2, i + 1, 2):
            m, b = blocks[j]
            out += 16 * len(targets(m, (0, 1, 2))) * (2 if chunks(m, b) > NA else 1)
        return out

    v_tiles = [(b, j) for b in range(B) for j in range(TILES)] + ([(B, 0)] if regs else [])
    total = sum(chunks(m, b) for m, b in blocks)

    with nc.Block() as block:
        @block.sync
        def _(sp):
            sp.dma_start(w[:, :, :], dram[f"w{layer}"].rearrange("(t p) n -> p t n", p=128)).then_inc(w_in, 16)
            sp.dma_start(bias[:, :], dram[f"b{layer}"][:, 0:2 * CT]).then_inc(w_in, 16)
            sp.dma_start(v_bias[:, :], dram[f"vb{layer}"]).then_inc(w_in, 16)
            if regs:
                sp.dma_start(x[:, :, ALL:ALL + REGS],
                             dram["registers"].rearrange("(t p) n -> p t n", p=128)).then_inc(w_in, 16)
            done = 0
            for i, (m, b) in enumerate(blocks):
                done += chunks(m, b)
                sp.wait_ge(high_ready, done)
                sp.wait_ge(low_ready, done)
                par = i % 2
                heads = slice((m % CT) * HPT, (m % CT + 1) * HPT)
                n = TOK + (regs if chunks(m, b) > NA else 0)
                sp.wait_ge(other_ready, done)
                for dst, buf in targets(m, (high, low, other)):
                    sp.dma_start(dst[heads, :, b, 0:n], buf[:, par, 0:n]).then_inc(stored[par], 16)
                    if n > TOK:
                        sp.dma_start(dst[heads, :, 1, TOK:n], buf[:, par, TOK:n]).then_inc(stored[par], 16)
            for par in range(2):
                sp.wait_ge(stored[par], store_count(len(blocks) - 2 + par))

        @block.tensor
        def _(pe):
            pe.wait_ge(w_in, 16 * (4 if regs else 3))
            n = 0
            for m, b in blocks:
                for a in range(chunks(m, b)):
                    if n >= 4:
                        pe.wait_ge(full_ready, n - 3)
                    at = source(b, a)
                    for t in range(CT):
                        last = nc.tensor.matmul(acc[:, n % 4, 0:width(a)], w[:, t, m * 128:(m + 1) * 128],
                                                x[:, t, at:at + width(a)], start=(t == 0), stop=(t == CT - 1))
                    last.then_inc(acc_ready, 1)
                    n += 1
            for n, (b, j) in enumerate(v_tiles):
                if n >= 4:
                    pe.wait_ge(v_full_ready, n - 3)
                for t in range(CT):
                    if b < B:
                        at = b * TOK + j * 128
                        keys = x[:, t, at:at + 128]
                        dst = acc[:, 4 + n % 4, 0:C]
                    else:
                        keys = x[:, t, ALL:ALL + REGS]
                        dst = acc[0:REGS, 4 + n % 4, 0:C]
                    last = nc.tensor.matmul(dst, keys, w[:, t, 2 * C:3 * C], start=(t == 0), stop=(t == CT - 1))
                last.then_inc(v_acc_ready, 1)

        @block.scalar
        def _(act):
            act.wait_ge(w_in, 16 * (4 if regs else 3))
            nc.scalar.activation(q_bias[:, :], bias[:, 0:CT], ACT.Identity, scale=Q_SCALE).then_inc(bias_ready, 1)
            act.wait_ge(bias_ready, 1)
            n = 0
            for m, b in blocks:
                for a in range(chunks(m, b)):
                    act.wait_ge(acc_ready, n + 1)
                    if n >= 3:
                        act.wait_ge(low_ready, n - 2)
                        act.wait_ge(other_ready, n - 2)
                    col = q_bias[:, m:m + 1] if m < CT else bias[:, m:m + 1]
                    nc.scalar.activation(full[:, n % 3, 0:width(a)], acc[:, n % 4, 0:width(a)], ACT.Identity,
                                         bias=col, scale=Q_SCALE if m < CT else 1.0).then_inc(full_ready, 1)
                    n += 1
            for n, (b, j) in enumerate(v_tiles):
                act.wait_ge(v_full_ready, n + 1)
                p = 128 if b < B else REGS
                tile = b * TILES + j
                nc.scalar.activation(values[0:p, :, tile, 0:D],
                                     v_full[0:p, n % 3, :].rearrange("p (h d) -> p h d", d=D),
                                     ACT.Identity).then_inc(v_high_ready, 1)

        @block.vector
        def _(dve):
            n = 0
            for i, (m, b) in enumerate(blocks):
                par = i % 2
                if i >= 2:
                    dve.wait_ge(stored[par], store_count(i - 2))
                for a in range(chunks(m, b)):
                    src = full[:, n % 3, 0:width(a)]
                    if m < CT:
                        src = as_rows(src, a)
                        hi, lo = by_row(high[:, par, :], a), by_row(low[:, par, :], a)
                    else:
                        hi, lo = by_strip(high[:, par, :], a), by_strip(low[:, par, :], a)
                    dve.wait_ge(full_ready, n + 1)
                    nc.vector.tensor_copy(hi, src).then_inc(high_ready, 1)
                    dve.wait_ge(high_ready, n + 1)
                    nc.vector.tensor_tensor(lo, src, hi, ALU.subtract).then_inc(low_ready, 1)
                    n += 1
            for n, (b, j) in enumerate(v_tiles):
                p = 128 if b < B else REGS
                tile = b * TILES + j
                dve.wait_ge(v_acc_ready, n + 1)
                if n >= 3:
                    dve.wait_ge(v_low_ready, n - 2)
                nc.vector.tensor_tensor(v_full[0:p, n % 3, :], acc[0:p, 4 + n % 4, 0:C], v_bias[0:p, :],
                                        ALU.add).then_inc(v_full_ready, 1)

        @block.gpsimd
        def _(pool):
            nc.gpsimd.memset(values[:, :, :, 2 * D:VW], 1.0)
            n = 0
            for i, (m, b) in enumerate(blocks):
                par = i % 2
                for a in range(chunks(m, b)):
                    if a == 0 and i >= 2:
                        pool.wait_ge(stored[par], store_count(i - 2))
                    pool.wait_ge(full_ready, n + 1)
                    src = full[:, n % 3, 0:width(a)]
                    if m < CT:
                        dst = by_strip(other[:, par, :], a)
                    else:
                        dst, src = by_row(other[:, par, :], a), as_rows(src, a)
                    nc.gpsimd.tensor_copy(dst, src).then_inc(other_ready, 1)
                    n += 1
            for n, (b, j) in enumerate(v_tiles):
                p = 128 if b < B else REGS
                tile = b * TILES + j
                pool.wait_ge(v_high_ready, n + 1)
                nc.gpsimd.tensor_tensor(values[0:p, :, tile, D:2 * D],
                                        v_full[0:p, n % 3, :].rearrange("p (h d) -> p h d", d=D),
                                        values[0:p, :, tile, 0:D], ALU.subtract).then_inc(v_low_ready, 1)


def position_bias(nc, ctx, dram, sem):
    GQ = 4
    NG = SIDE // GQ
    table32 = ctx.enter_context(nc.sbuf_tensor("table32", [128, 2, 2 * SIDE], F32))
    table_hi = ctx.enter_context(nc.sbuf_tensor("table_hi", [128, 2, 2 * SIDE], F16))
    table = ctx.enter_context(nc.sbuf_tensor("table", [128, 2, 2 * SIDE], F16))
    q = ctx.enter_context(nc.sbuf_tensor("bias_q", [128, 2, B, TOK], F16))
    hi = ctx.enter_context(nc.sbuf_tensor("bias_hi", [SIDE, 2, B, TOK], F16))
    lo = ctx.enter_context(nc.sbuf_tensor("bias_lo", [SIDE, 2, B, TOK], F16))
    acc = ctx.enter_context(nc.psum_tensor("bias_acc", [128, 8, 512], F32))
    tables_in = sem("tables_in")
    table_hi_ready = sem("table_hi_ready")
    table_ready = sem("table_ready")
    q_in = [sem(f"q_in{i}") for i in range(2)]
    acc_ready = sem("bias_acc_ready")
    hi_ready = sem("bias_hi_ready")
    lo_ready = sem("bias_lo_ready")
    stored = [sem(f"bias_stored{i}") for i in range(2)]

    def groups():
        return [(axis, g) for axis in range(2) for g in range(NG)]

    def banked(n, axis):
        v = acc[0:SIDE, n % 8, 0:B * GQ * SIDE].rearrange("p (b g x) -> p b g x", b=B, g=GQ)
        return v if axis == 0 else v.rearrange("p b g x -> p b x g")

    def placed(buf, axis, g):
        if axis == 0:
            return buf[:, axis, :, g * GQ * SIDE:(g + 1) * GQ * SIDE].rearrange("p b (g x) -> p b g x", g=GQ)
        return buf[:, axis, :, :].rearrange("p b (x w) -> p b x w", w=SIDE)[:, :, :, g * GQ:(g + 1) * GQ]

    with nc.Block() as block:
        @block.sync
        def _(sp):
            for part in range(3):
                sp.dma_start(table32[part * D:(part + 1) * D, :, 0:2 * SIDE - 1], dram["tables"]).then_inc(tables_in, 16)

            def load(h, par):
                sp.dma_start(q[0:3 * D, par], dram["q_parts"][bass.ds(h, 1)].rearrange("o p d b n -> (o p d) b n")).then_inc(q_in[par], 16)

            def store(h, axis):
                sp.wait_ge(lo_ready, h * 2 * NG + (axis + 1) * NG)
                if axis == 0:
                    sp.dma_start(dram["row_bias"][bass.ds(h, 1), 0:SIDE].rearrange("o p b n -> (o p) b n"),
                                 hi[:, 0]).then_inc(stored[0], 16)
                    sp.dma_start(dram["row_bias"][bass.ds(h, 1), SIDE:2 * SIDE].rearrange("o p b n -> (o p) b n"),
                                 lo[:, 0]).then_inc(stored[0], 16)
                else:
                    for part, buf in enumerate((hi, lo)):
                        dst = dram["col_bias"][bass.ds(h, 1), part * KC:(part + 1) * KC]
                        sp.dma_start(dst.rearrange("o p c b n -> (o c) p b n"), buf[:, 1]).then_inc(stored[1], 16)

            def two_heads(h, more):
                if due(h):
                    sp.wait_ge(acc_ready, h * 2 * NG)
                load(h + 1, 1)
                for axis in range(2):
                    store(h, axis)
                if more:
                    load(h + 2, 0)
                for axis in range(2):
                    store(h + 1, axis)

            load(0, 0)
            two_heads(0, True)
            with sp.Fori(1, HEADS // 2 - 1) as pair:
                two_heads(pair * 2, True)
            two_heads(HEADS - 2, False)
            for axis in range(2):
                sp.wait_ge(stored[axis], 32 * HEADS)

        @block.tensor
        def _(pe):
            pe.wait_ge(table_ready, 2)

            def two_heads(pair):
                for par in range(2):
                    h = pair * 2 + par
                    pe.wait_ge(q_in[par], (pair + 1) * 16)
                    for n, (axis, g) in enumerate(groups()):
                        if due(h * 2 * NG + n - 7):
                            pe.wait_ge(lo_ready, h * 2 * NG + n - 7)
                        for j in range(GQ):
                            x = g * GQ + j
                            dst = acc[0:SIDE, n % 8, 0:B * GQ * SIDE] \
                                .rearrange("p (b g x) -> p b g x", b=B, g=GQ)[:, :, j]
                            src = q[0:3 * D, par].rearrange("p b (r w) -> p b r w", w=SIDE)
                            src = src[:, :, x, :] if axis == 0 else src[:, :, :, x]
                            last = nc.tensor.matmul(dst, table[0:3 * D, axis, SIDE - 1 - x:2 * SIDE - 1 - x], src,
                                                    start=True, stop=True)
                        last.then_inc(acc_ready, 1)

            two_heads(0)
            with pe.Fori(1, HEADS // 2) as pair:
                two_heads(pair)

        @block.scalar
        def _(act):
            def head(h):
                for n, (axis, g) in enumerate(groups()):
                    if g == 0 and due(h):
                        act.wait_ge(stored[axis], h * 32)
                    act.wait_ge(acc_ready, h * 2 * NG + n + 1)
                    nc.scalar.activation(placed(hi, axis, g), banked(n, axis), ACT.Identity).then_inc(hi_ready, 1)

            head(0)
            with act.Fori(1, HEADS) as h:
                head(h)

        @block.vector
        def _(dve):
            dve.wait_ge(tables_in, 48)
            used = table32[0:3 * D, :, 0:2 * SIDE - 1]
            parts = table_hi[0:3 * D, :, 0:2 * SIDE - 1]
            nc.vector.tensor_copy(parts, used).then_inc(table_hi_ready, 1)
            dve.wait_ge(table_hi_ready, 1)
            nc.vector.tensor_copy(table[0:3 * D, :, 0:2 * SIDE - 1], parts).then_inc(table_hi_ready, 1)
            dve.wait_ge(table_hi_ready, 2)
            nc.vector.tensor_tensor(table[D:2 * D, :, 0:2 * SIDE - 1], table32[D:2 * D, :, 0:2 * SIDE - 1],
                                    table_hi[D:2 * D, :, 0:2 * SIDE - 1], ALU.subtract).then_inc(table_ready, 2)
            with dve.Fori(0, HEADS) as h:
                for n, (axis, g) in enumerate(groups()):
                    dve.wait_ge(hi_ready, h * 2 * NG + n + 1)
                    nc.vector.tensor_tensor(placed(lo, axis, g), banked(n, axis), placed(hi, axis, g),
                                            ALU.subtract).then_inc(lo_ready, 1)


def attention(nc, ctx, x, values, layer, dram, sem):
    local = layer == 0
    keys_n = TOK + (REGS if local else 0)
    key_tiles = TILES + (1 if local else 0)
    PAIRS = TILES // 2
    PITCH = max(rect_width(a, c) for a in range(NA) for c in range(NS))
    SLOT = NS * PITCH + UNIT if local else 2 * UNIT
    RING = 3
    LAG = 2
    PER_UNIT = 1 if local else PAIRS
    STEPS = NA * PER_UNIT
    SCORES = STEPS * (NS + 1 if local else 1)
    BY_DVE = 512
    STEP_PIECES = QT if local else 2
    UNIT_PIECES = STEP_PIECES * PER_UNIT
    ROW_STEP = min(3, PER_UNIT - 1)
    BEFORE_ROW = ROW_STEP * STEP_PIECES
    LATE = NA - (2 if local else 1)
    UNIT_BANKS = UNIT_PIECES + 1

    q_a = ctx.enter_context(nc.sbuf_tensor(f"q_a{layer}", [128, 2, NS, TOK], F16))
    q_b = ctx.enter_context(nc.sbuf_tensor(f"q_b{layer}", [B_ROWS, 2, TOK], F16))
    k_a = ctx.enter_context(nc.sbuf_tensor(f"k_a{layer}", [128, 2, keys_n], F16))
    k_b = ctx.enter_context(nc.sbuf_tensor(f"k_b{layer}", [B_ROWS, NA + 1, 128], F16))
    q_m = ctx.enter_context(nc.sbuf_tensor(f"q_m{layer}", [128, 2, TOK], F16))
    k_m = ctx.enter_context(nc.sbuf_tensor(f"k_m{layer}", [128, 2, keys_n], F16))
    v = ctx.enter_context(nc.sbuf_tensor(f"v{layer}", [128, 2, key_tiles, VW], F16))
    ident = ctx.enter_context(nc.sbuf_tensor(f"ident{layer}", [128, 128], F16))
    prob = ctx.enter_context(nc.sbuf_tensor(f"prob{layer}", [128, RING, SLOT], F32))
    prob_low = ctx.enter_context(nc.sbuf_tensor(f"prob_low{layer}", [128, RING, SLOT], F16))
    part_max = ctx.enter_context(nc.sbuf_tensor(f"part_max{layer}", [128, QT, PIECES], F32))
    tile_max = ctx.enter_context(nc.sbuf_tensor(f"tile_max{layer}", [128, 2, QT], F32))
    neg_max = ctx.enter_context(nc.sbuf_tensor(f"neg_max{layer}", [128, QT], F16))
    max_row = ctx.enter_context(nc.sbuf_tensor(f"max_row{layer}", [QT, NA, 128], F16))
    warm = ctx.enter_context(nc.sbuf_tensor(f"warm{layer}", [1, 1], F32))
    result = x[0:VW].rearrange("p t n -> p (t n)")[:, 0:2 * TOK].rearrange("p (b n) -> p b n", b=B)
    scores = ctx.enter_context(nc.psum_tensor(f"scores{layer}", [128, 4, 512], F32))
    max_acc = ctx.enter_context(nc.psum_tensor(f"max_acc{layer}", [128, 2, 512], F32))
    out_acc = ctx.enter_context(nc.psum_tensor(f"out_acc{layer}", [128, 2, 512], F32))

    consts_in = sem(f"consts_in{layer}")
    main_in = [sem(f"main_in{layer}_{i}") for i in range(2)]
    max_in = [sem(f"max_in{layer}_{i}") for i in range(2)]
    score_ready = sem(f"score_ready{layer}")
    prob_ready = sem(f"prob_ready{layer}")
    low_by_dve = sem(f"low_by_dve{layer}")
    low_by_pool = sem(f"low_by_pool{layer}")
    prob_used = sem(f"prob_used{layer}")
    bank_filled = sem(f"bank_filled{layer}")
    bank_read = sem(f"bank_read{layer}")
    tile_max_ready = sem(f"tile_max_ready{layer}")
    neg_ready = sem(f"neg_ready{layer}")
    rows_in = [sem(f"rows_in{layer}_{i}") for i in range(2)]
    result_ready = sem(f"result_ready{layer}")
    result_out = [sem(f"result_out{layer}_{i}") for i in range(2)]

    CONSTS = 16 * (2 + 2 * (5 if local else 2))
    MAIN = 16 * (4 if local else 5)
    MAX = 16 * (2 if local else 4)
    RESULT = 16
    ROWS = 16 * QT

    def piece_use(stage, i):
        u, j = i // UNIT_PIECES, i % UNIT_PIECES
        if isinstance(stage, int) and stage == 0 and u == 0:
            return i, i % 2
        within = u * UNIT_BANKS - 1 + j + (1 if j >= BEFORE_ROW else 0)
        return stage * (NA * UNIT_BANKS) + within, within % 2

    def row_use(stage, u):
        within = (u + 1) * UNIT_BANKS - 1
        if not (isinstance(stage, int) and stage == STAGES - 1 and u == NA - 1):
            within += BEFORE_ROW
        return stage * (NA * UNIT_BANKS) + within, within % 2

    def near(a, c):
        return *window_of(a, KR, SIDE), *window_of(c, KC, SIDE)

    def is_first(n):
        return isinstance(n, int) and n == 0

    def is_last(n):
        return isinstance(n, int) and n == STAGES - 1

    with nc.Block() as block:
        @block.sync
        def _(sp):
            for par in range(2):
                sp.dma_start(k_m[32:128, par], dram[f"one_m{layer}"][:, 0:keys_n]).then_inc(consts_in, 16)
                if local:
                    sp.dma_start(q_m[32:128, par], dram["mask_m"]).then_inc(consts_in, 16)

            def load_main(h, b):
                src = dram["q_parts"][bass.ds(h, 1), :, :, b].rearrange("o p d n -> (o p d) n")
                src = src.unsqueeze(1).to_broadcast((3 * D, NS, TOK))
                sp.dma_start(q_a[0:3 * D, b], src).then_inc(main_in[b], 16)
                src = dram["k_parts"][bass.ds(h, 1), :, :, b, 0:keys_n].rearrange("o p d n -> (o p d) n")
                sp.dma_start(k_a[0:3 * D, b], src).then_inc(main_in[b], 16)
                own = values[:, bass.ds(h, 1), b * TILES:(b + 1) * TILES].rearrange("p o t n -> p (o t) n")
                sp.dma_start(v[:, b, 0:TILES], own).then_inc(main_in[b], 16)
                if local:
                    own = values[0:REGS, bass.ds(h, 1), B * TILES].rearrange("p o n -> p (o n)")
                    sp.dma_start(v[0:REGS, b, TILES], own).then_inc(main_in[b], 16)
                else:
                    sp.dma_start(q_a[96:128, b],
                                 dram["col_bias"][bass.ds(h, 1), :, :, b].rearrange("o p c n -> (o p) c n")) \
                        .then_inc(main_in[b], 16)
                    sp.dma_start(q_b[0:2 * SIDE, b],
                                 dram["row_bias"][bass.ds(h, 1), :, b].rearrange("o p n -> (o p) n")) \
                        .then_inc(main_in[b], 16)

            def load_max(h, b):
                src = dram["q_other"] if local else dram["q_parts"][:, 0]
                sp.dma_start(q_m[0:D, b], src[bass.ds(h, 1), :, b].rearrange("o d n -> (o d) n")) \
                    .then_inc(max_in[b], 16)
                src = dram["k_other"][bass.ds(h, 1), :, b, 0:keys_n]
                sp.dma_start(k_m[0:D, b], src.rearrange("o d n -> (o d) n")).then_inc(max_in[b], 16)
                if not local:
                    sp.dma_start(q_m[D:D + SIDE, b],
                                 dram["row_bias"][bass.ds(h, 1), 0:SIDE, b].rearrange("o p n -> (o p) n")) \
                        .then_inc(max_in[b], 16)
                    sp.dma_start(q_m[D + SIDE:128, b],
                                 dram["col_bias"][bass.ds(h, 1), 0:KC, :, b].rearrange("o p c n -> (o c) p n")) \
                        .then_inc(max_in[b], 16)

            def store(h, b):
                sp.wait_ge(result_ready, (h * B + b + 1) * NA)
                sp.dma_start(dram["sums"][:, bass.ds(h, 1), b].rearrange("p o n -> (p o) n"),
                             result[:, b]).then_inc(result_out[b], 16)

            def place_rows(stage, b, late):
                u0, u1 = (LATE, NA) if late else (0, LATE)
                sp.wait_ge(bank_read, row_use(stage, u1 - 1)[0] + 1)
                dst = q_b[M_ROW:M_ROW + 1, b, u0 * UNIT:u1 * UNIT]
                for t in range(QT):
                    src = max_row[t:t + 1, u0:u1]
                    if local:
                        to = dst.rearrange("o (r c s) -> o c r s", c=NS, s=KC)[:, t]
                        src = src.rearrange("o u (r s) -> o (u r) s", s=KC)
                    else:
                        to = dst.rearrange("o (u t n) -> o t u n", t=QT, n=128)[:, t]
                    sp.dma_start(to, src).then_inc(rows_in[late], 16)

            load_max(0, 0)
            sp.dma_start(ident[:, :], dram["ident"]).then_inc(consts_in, 16)
            load_main(0, 0)
            sp.dma_start(k_b[:, :, :], dram[f"one_b{layer}"]).then_inc(consts_in, 16)
            for par in range(2):
                sp.dma_start(k_a[96:128, par], dram[f"one_a{layer}"][:, 0:keys_n]).then_inc(consts_in, 16)
                if local:
                    sp.dma_start(q_a[96:128, par], dram["mask_a"]).then_inc(consts_in, 16)
                    sp.dma_start(q_b[0:2 * SIDE, par], dram["mask_b"]).then_inc(consts_in, 16)
            load_max(0, 1)
            place_rows(0, 0, False)

            def stage(h, b):
                n = h * B + b
                place_rows(n, b, True)
                if not is_last(n) and not is_last(n + 1 if isinstance(n, int) else n):
                    sp.wait_ge(bank_read, piece_use(n, NA * UNIT_PIECES - 1)[0] + 1)
                    load_max(h + 1, b)
                if not is_last(n):
                    if not is_first(n):
                        sp.wait_ge(prob_used, n * STEPS)
                    load_main(h + b, 1 - b)
                if not is_first(n):
                    store(h - (1 - b), 1 - b)
                if not is_last(n):
                    place_rows(n + 1, 1 - b, False)

            each_stage(sp, stage)
            store(HEADS - 1, 1)
            for b in range(B):
                sp.wait_ge(result_out[b], RESULT * HEADS)

        @block.tensor
        def _(pe):
            def max_pieces(stage, b, k, part):
                for i in range(k * STEP_PIECES + part, (k + 1) * STEP_PIECES if part else k * STEP_PIECES + 1):
                    use, bank = piece_use(stage, i)
                    if due(use - 1):
                        pe.wait_ge(bank_read, use - 1)
                    if local:
                        r0, r1, c0, c1 = near(k, i % QT)
                        n = (r1 - r0) * (c1 - c0)
                        at = i % QT * STRIP + k * 128
                        keys = k_m[:, b, 0:TOK].rearrange("p (r w) -> p r w", w=SIDE)[:, r0:r1, c0:c1]
                        nc.tensor.matmul(max_acc[:, bank, 0:n], q_m[:, b, at:at + 128], keys, start=True, stop=True)
                        last = nc.tensor.matmul(max_acc[:, bank, n:n + REGS], q_m[:, b, at:at + 128],
                                                k_m[:, b, TOK:keys_n], start=True, stop=True)
                    else:
                        tile, piece = i // PIECES, i % PIECES
                        last = nc.tensor.matmul(max_acc[:, bank, 0:PIECE], q_m[:, b, tile * 128:(tile + 1) * 128],
                                                k_m[:, b, piece * PIECE:(piece + 1) * PIECE],
                                                start=True, stop=True)
                    last.then_inc(bank_filled, 1)

            def row_of_max(stage, u):
                pe.wait_ge(neg_ready, stage * NA + u + 1)
                use, bank = row_use(stage, u)
                pe.wait_ge(bank_read, use - 1)
                nc.tensor.matmul(max_acc[0:QT, bank, 0:128], neg_max[:, :], ident[:, :],
                                 start=True, stop=True).then_inc(bank_filled, 1)

            def key_product(bank, tile, queries_a, queries_b, b):
                kind = tile % NA if tile < TILES else NA
                rows = 128 if tile < TILES else REGS
                nc.tensor.matmul(bank, k_a[:, b, tile * 128:tile * 128 + rows], queries_a, start=True, stop=False)
                return nc.tensor.matmul(bank, k_b[:, kind, 0:rows], queries_b, start=False, stop=True)

            def row_is_placed(n, a):
                if a in (0, LATE):
                    pe.wait_ge(rows_in[a == LATE], ROWS * (n + 1))

            def scores_full(n, b, p):
                a, k = p // PAIRS, p % PAIRS
                if k == 0:
                    row_is_placed(n, a)
                if due(n * STEPS + p - 1):
                    pe.wait_ge(prob_ready, n * STEPS + p - 1)
                for j in range(2):
                    tile = 2 * k + j
                    last = key_product(scores[:, 2 * (p % 2) + j, 0:UNIT], tile,
                                       q_a[:, b, tile // NA, a * UNIT:(a + 1) * UNIT],
                                       q_b[:, b, a * UNIT:(a + 1) * UNIT], b)
                last.then_inc(score_ready, 1)

            def weighted_full(n, b, p):
                a, k = p // PAIRS, p % PAIRS
                pe.wait_ge(low_by_dve, n * STEPS + p + 1)
                pe.wait_ge(low_by_pool, n * STEPS + p + 1)
                if k == 0 and due(n * NA + a - 1):
                    pe.wait_ge(result_ready, n * NA + a - 1)
                high = prob[:, p % RING, :].bitcast(BF16)[:, 1::2]
                low = prob_low[:, p % RING, :]
                for j in range(2):
                    tile = 2 * k + j
                    cut = slice(j * UNIT, (j + 1) * UNIT)
                    nc.tensor.matmul(out_acc[0:VW, a % 2, 0:UNIT], v[:, b, tile, :], high[:, cut],
                                     start=(tile == 0), stop=False)
                    last = nc.tensor.matmul(out_acc[0:VW, a % 2, 0:UNIT], v[:, b, tile, :], low[:, cut],
                                            start=False, stop=(tile == TILES - 1))
                last.then_inc(prob_used, 1)

            def scores_local(n, b, a):
                row_is_placed(n, a)
                cut = slice(a * UNIT, (a + 1) * UNIT)
                for c in range(NS + 1):
                    if due(n * SCORES + (a - 1) * (NS + 1) + c + 1):
                        pe.wait_ge(prob_ready, n * SCORES + (a - 1) * (NS + 1) + c + 1)
                    if c == NS:
                        last = key_product(scores[0:REGS, c, 0:UNIT], TILES, q_a[:, b, 0, cut], q_b[:, b, cut], b)
                        last.then_inc(score_ready, 1)
                        continue
                    qa = q_a[:, b, c, cut].rearrange("p (r w) -> p r w", w=SIDE)
                    qb = q_b[:, b, cut].rearrange("p (r w) -> p r w", w=SIDE)
                    for s, ka, r0, r1, lo, hi, at in rects(a):
                        if s == c:
                            w = (r1 - r0) * (hi - lo)
                            last = key_product(scores[:, c, at:at + w], c * NA + ka,
                                               qa[:, r0:r1, lo:hi], qb[:, r0:r1, lo:hi], b)
                    last.then_inc(score_ready, 1)

            def weighted_local(n, b, a):
                pe.wait_ge(low_by_dve, n * STEPS + a + 1)
                pe.wait_ge(low_by_pool, n * STEPS + a + 1)
                if due(n * NA + a - 1):
                    pe.wait_ge(result_ready, n * NA + a - 1)
                high = prob[:, a % RING, :].bitcast(BF16)[:, 1::2]
                low = prob_low[:, a % RING, :]
                sums = out_acc[0:VW, a % 2, 0:UNIT]
                cut = slice(NS * PITCH, NS * PITCH + UNIT)
                nc.tensor.matmul(sums, v[0:REGS, b, TILES, :], high[0:REGS, cut], start=True, stop=False)
                nc.tensor.matmul(sums, v[0:REGS, b, TILES, :], low[0:REGS, cut], start=False, stop=False)
                todo = rects(a)
                for i, (c, ka, r0, r1, lo, hi, at) in enumerate(todo):
                    w = (r1 - r0) * (hi - lo)
                    cut = slice(c * PITCH + at, c * PITCH + at + w)
                    dst = sums.rearrange("p (r w) -> p r w", w=SIDE)[:, r0:r1, lo:hi]
                    nc.tensor.matmul(dst, v[:, b, c * NA + ka, :], high[:, cut], start=False, stop=False)
                    last = nc.tensor.matmul(dst, v[:, b, c * NA + ka, :], low[:, cut],
                                            start=False, stop=(i == len(todo) - 1))
                last.then_inc(prob_used, 1)

            compute, use = (scores_local, weighted_local) if local else (scores_full, weighted_full)

            pe.wait_ge(consts_in, CONSTS)
            pe.wait_ge(max_in[0], MAX)
            for u in range(NA):
                for k in range(PER_UNIT):
                    if u > 0 and k == ROW_STEP:
                        row_of_max(0, u - 1)
                    max_pieces(0, 0, u * PER_UNIT + k, 0)
                    max_pieces(0, 0, u * PER_UNIT + k, 1)

            def stage(h, b):
                n = h * B + b
                pe.wait_ge(main_in[b], (h + 1) * MAIN)
                if not is_last(n):
                    pe.wait_ge(max_in[1 - b], (h + 1 + b) * MAX)
                for k in range(STEPS):
                    compute(n, b, k)
                    if k % PER_UNIT == ROW_STEP:
                        if k < PER_UNIT:
                            row_of_max(n, NA - 1)
                        elif not is_last(n):
                            row_of_max(n + 1, k // PER_UNIT - 1)
                    if not is_last(n):
                        max_pieces(n + 1, 1 - b, k, 0)
                    if k >= LAG:
                        use(n, b, k - LAG)
                    elif not is_first(n):
                        use(n - 1, 1 - b, k - LAG + STEPS)
                    if not is_last(n):
                        max_pieces(n + 1, 1 - b, k, 1)

            each_stage(pe, stage)
            for k in range(STEPS - LAG, STEPS):
                use(STAGES - 1, 1, k)

        @block.scalar
        def _(act):
            def take_result(h, b, a):
                n = h * B + b
                act.wait_ge(prob_used, n * STEPS + (a + 1) * PER_UNIT)
                if a == 0 and due(h):
                    act.wait_ge(result_out[b], h * RESULT)
                dst = result[:, b].rearrange("p (c r s) -> p c r s", c=NS, s=KC)
                nc.scalar.activation(dst[:, :, a * KR:(a + 1) * KR],
                                     out_acc[0:VW, a % 2, 0:UNIT].rearrange("p (r c s) -> p c r s", c=NS, s=KC),
                                     ACT.Identity).then_inc(result_ready, 1)

            act.wait_ge(consts_in, CONSTS)
            nc.scalar.activation(warm[:, :], ident[0:1, 0:1], ACT.Exp)

            def exps(n, k):
                free = n * STEPS + k - RING + 1
                for c in range(NS + 1 if local else 1):
                    act.wait_ge(score_ready, n * SCORES + k * (SCORES // STEPS) + c + 1)
                    if c == 0 and due(free):
                        act.wait_ge(prob_used, free)
                    if local:
                        p = 128 if c < NS else REGS
                        w = rect_width(k, c) if c < NS else UNIT
                        dst, src = prob[0:p, k % RING, c * PITCH:c * PITCH + w], scores[0:p, c, 0:w]
                    else:
                        dst = prob[:, k % RING, :].rearrange("p (j n) -> p j n", j=2)
                        src = scores[:, 2 * (k % 2):2 * (k % 2) + 2, 0:UNIT]
                    nc.scalar.activation(dst, src, ACT.Exp).then_inc(prob_ready, 1)

            def stage(h, b):
                n = h * B + b
                for k in range(STEPS):
                    exps(n, k)
                    u = (k - LAG) // PER_UNIT
                    if (k - LAG) % PER_UNIT == PER_UNIT - 1:
                        if u >= 0:
                            take_result(h, b, u)
                        elif not is_first(n):
                            take_result(h - (1 - b), 1 - b, NA + u)

            each_stage(act, stage)
            for a in range(NA - (LAG - 1) // PER_UNIT - 1, NA):
                take_result(HEADS - 1, 1, a)

        def low_part(engine, n, k, done):
            ours = engine is nc.vector
            if local:
                parts = (0, 2) if ours else (1, NS)
            else:
                parts = (0,)
            for c in parts:
                if local:
                    p = 128 if c < NS else REGS
                    cut = slice(c * PITCH, c * PITCH + (rect_width(k, c) if c < NS else UNIT))
                else:
                    p = 128
                    cut = slice(0, BY_DVE) if ours else slice(BY_DVE, SLOT)
                engine.wait_ge(prob_ready, n * SCORES + k * (SCORES // STEPS) + c + 1)
                last = engine.tensor_tensor(prob_low[0:p, k % RING, cut], prob[0:p, k % RING, cut],
                                            prob[0:p, k % RING, :].bitcast(BF16)[:, 1::2][:, cut], ALU.subtract)
            last.then_inc(done, 1)

        @block.vector
        def _(dve):
            def maxima(stage, k):
                for i in range(k * STEP_PIECES, (k + 1) * STEP_PIECES):
                    use, bank = piece_use(stage, i)
                    dve.wait_ge(bank_filled, use + 1)
                    if local:
                        r0, r1, c0, c1 = near(k, i % QT)
                        w = (r1 - r0) * (c1 - c0) + REGS
                        dst = tile_max[:, k % 2, i % QT:i % QT + 1]
                    else:
                        w, j = PIECE, i % UNIT_PIECES
                        dst = part_max[:, j // PIECES, j % PIECES:j % PIECES + 1]
                    nc.vector.reduce_max(dst, max_acc[:, bank, 0:w], axis=AX.X).then_inc(bank_read, 1)

            def unit_max(stage, u):
                unit = stage * NA + u
                dve.wait_ge(bank_read, piece_use(stage, (u + 1) * UNIT_PIECES - 1)[0] + 1)
                if not local:
                    nc.vector.reduce_max(tile_max[:, u % 2], part_max[:, :, :], axis=AX.X).then_inc(tile_max_ready, 1)
                    dve.wait_ge(tile_max_ready, unit + 1)
                nc.vector.tensor_scalar(neg_max[:, :], tile_max[:, u % 2], -1.0, None, ALU.mult).then_inc(neg_ready, 1)

            def take_row(stage, u):
                use, bank = row_use(stage, u)
                dve.wait_ge(bank_filled, use + 1)
                if u in (0, LATE) and due(stage):
                    dve.wait_ge(rows_in[u == LATE], ROWS * stage)
                nc.vector.tensor_copy(max_row[:, u], max_acc[0:QT, bank, 0:128]).then_inc(bank_read, 1)

            for u in range(NA):
                for k in range(PER_UNIT):
                    if u > 0 and k == ROW_STEP:
                        take_row(0, u - 1)
                    maxima(0, u * PER_UNIT + k)
                unit_max(0, u)

            def stage(h, b):
                n = h * B + b
                for k in range(STEPS):
                    if k >= 1:
                        low_part(nc.vector, n, k - 1, low_by_dve)
                    elif not is_first(n):
                        low_part(nc.vector, n - 1, STEPS - 1, low_by_dve)
                    if k % PER_UNIT == ROW_STEP:
                        if k < PER_UNIT:
                            take_row(n, NA - 1)
                        elif not is_last(n):
                            take_row(n + 1, k // PER_UNIT - 1)
                    if not is_last(n):
                        maxima(n + 1, k)
                    if not is_last(n) and k % PER_UNIT == PER_UNIT - 1:
                        unit_max(n + 1, k // PER_UNIT)

            each_stage(dve, stage)
            low_part(nc.vector, STAGES - 1, STEPS - 1, low_by_dve)

        @block.gpsimd
        def _(pool):
            def stage(h, b):
                for k in range(STEPS):
                    low_part(nc.gpsimd, h * B + b, k, low_by_pool)

            each_stage(pool, stage)


def mix(nc, ctx, x, layer, dram, sem):
    w = ctx.enter_context(nc.sbuf_tensor(f"ow{layer}", [128, CT, C], F32))
    bias = ctx.enter_context(nc.sbuf_tensor(f"ob{layer}", [128, CT], F32))
    spread = ctx.enter_context(nc.sbuf_tensor(f"spread{layer}", [HEADS, CT, 128], F32))
    totals = ctx.enter_context(nc.sbuf_tensor(f"totals{layer}", [128, HEADS * ALL // 128], F32))
    inverse = ctx.enter_context(nc.sbuf_tensor(f"inverse{layer}", [128, HEADS * ALL // 128], F32))
    by_head = ctx.enter_context(nc.sbuf_tensor(f"by_head{layer}", [HEADS, ALL], F32))
    parts = ctx.enter_context(nc.sbuf_tensor(f"parts{layer}", [128, 3, 2 * CT, UNIT], F32))
    heads = ctx.enter_context(nc.sbuf_tensor(f"heads{layer}", [128, 2, CT, UNIT], F32))
    normed = ctx.enter_context(nc.sbuf_tensor(f"normed{layer}", [128, 2, CT, UNIT], F32))
    acc = ctx.enter_context(nc.psum_tensor(f"mix_acc{layer}", [128, 4, 512], F32))
    factor = ctx.enter_context(nc.psum_tensor(f"factor{layer}", [128, 4, 512], F32))
    w_in = sem(f"ow_in{layer}")
    totals_in = sem(f"totals_in{layer}")
    inverse_ready = sem(f"inverse_ready{layer}")
    inverse_out = sem(f"inverse_out{layer}")
    by_head_in = sem(f"by_head_in{layer}")
    x_back = [sem(f"x_back{layer}_{b}") for b in range(B)]
    parts_in = [sem(f"parts_in{layer}_{i}") for i in range(3)]
    factor_ready = sem(f"factor_ready{layer}")
    heads_ready = sem(f"heads_ready{layer}")
    normed_ready = sem(f"normed_ready{layer}")
    mixed = sem(f"mixed{layer}")
    added = sem(f"added{layer}")
    out_done = sem(f"out_done{layer}")
    UNITS = B * NA
    src_x = dram["x"] if layer == 0 else dram["x1"]
    dst_x = dram["x1"] if layer == 0 else dram["out"]

    with nc.Block() as block:
        @block.sync
        def _(sp):
            sp.dma_start(totals[:, :], dram["sums"][2 * D].rearrange("h b n -> (h b n)")
                         .rearrange("(p n) -> p n", p=128)).then_inc(totals_in, 16)

            def load(u):
                b, a = u // NA, u % NA
                if u >= 3:
                    sp.wait_ge(heads_ready, u - 2)
                src = dram["sums"][0:2 * D, :, b, a * UNIT:(a + 1) * UNIT].rearrange("d h n -> (d h) n")
                sp.dma_start(parts[:, u % 3], src.rearrange("(t p) n -> p t n", p=128)).then_inc(parts_in[u % 3], 16)

            sp.dma_start(w[:, :, :], dram[f"ow{layer}"].rearrange("(t p) n -> p t n", p=128)).then_inc(w_in, 16)
            sp.dma_start(bias[:, :], dram[f"ob{layer}"]).then_inc(w_in, 16)
            sp.dma_start(spread[:, :, :], dram["spread"]).then_inc(w_in, 16)
            load(0)
            load(1)
            sp.wait_ge(inverse_ready, 1)
            sp.dma_start(dram["inverse"].rearrange("h n -> (h n)").rearrange("(p n) -> p n", p=128), inverse[:, :]) \
                .then_inc(inverse_out, 16)
            sp.wait_ge(inverse_out, 16)
            sp.dma_start(by_head[:, :], dram["inverse"]).then_inc(by_head_in, 16)
            for b in range(B):
                sp.dma_start(x[:, :, b * TOK:(b + 1) * TOK],
                             src_x[:, b * TOK:(b + 1) * TOK].rearrange("(t p) n -> p t n", p=128)) \
                    .then_inc(x_back[b], 16)
            for u in range(UNITS):
                if u + 2 < UNITS:
                    load(u + 2)
                at = u * UNIT
                sp.wait_ge(added, u + 1)
                sp.dma_start(dst_x[:, at:at + UNIT].rearrange("(t p) n -> p t n", p=128),
                             x[:, :, at:at + UNIT]).then_inc(out_done, 16)
            sp.wait_ge(out_done, 16 * UNITS)

        @block.gpsimd
        def _(pool):
            for u in range(UNITS):
                pool.wait_ge(parts_in[u % 3], 16 * (u // 3 + 1))
                if u >= 2:
                    pool.wait_ge(normed_ready, u - 1)
                nc.gpsimd.tensor_tensor(heads[:, u % 2], parts[:, u % 3, 0:CT], parts[:, u % 3, CT:2 * CT],
                                        ALU.add).then_inc(heads_ready, 1)

        @block.vector
        def _(dve):
            def add(u):
                if u % NA == 0:
                    dve.wait_ge(x_back[u // NA], 16)
                dve.wait_ge(mixed, u + 1)
                for to in range(CT):
                    dst = x[:, to, u * UNIT:(u + 1) * UNIT]
                    last = nc.vector.scalar_tensor_tensor(dst, acc[:, to, 0:UNIT], bias[:, to:to + 1], dst,
                                                          ALU.add, ALU.add)
                last.then_inc(added, 1)

            dve.wait_ge(totals_in, 16)
            nc.vector.reciprocal(inverse[:, :], totals[:, :]).then_inc(inverse_ready, 1)
            dve.wait_ge(w_in, 48)
            for u in range(UNITS):
                dve.wait_ge(heads_ready, u + 1)
                dve.wait_ge(factor_ready, u + 1)
                if u >= 2:
                    dve.wait_ge(mixed, u - 1)
                nc.vector.tensor_tensor(normed[:, u % 2], factor[:, 0:CT, 0:UNIT], heads[:, u % 2],
                                        ALU.mult).then_inc(normed_ready, 1)
                if u > 0:
                    add(u - 1)
            add(UNITS - 1)

        @block.tensor
        def _(pe):
            def factors(u):
                if u > 0:
                    pe.wait_ge(normed_ready, u)
                for t in range(CT):
                    last = nc.tensor.matmul(factor[:, t, 0:UNIT], spread[:, t, :], by_head[:, u * UNIT:(u + 1) * UNIT],
                                            start=True, stop=True)
                last.then_inc(factor_ready, 1)

            pe.wait_ge(w_in, 48)
            pe.wait_ge(by_head_in, 16)
            factors(0)
            for u in range(UNITS):
                pe.wait_ge(normed_ready, u + 1)
                if u + 1 < UNITS:
                    factors(u + 1)
                if u > 0:
                    pe.wait_ge(added, u)
                for to in range(CT):
                    for t in range(CT):
                        last = nc.tensor.matmul(acc[:, to, 0:UNIT], w[:, t, to * 128:(to + 1) * 128],
                                                normed[:, u % 2, t], start=(t == 0), stop=(t == CT - 1))
                last.then_inc(mixed, 1)


def build(nc, dram):
    def scratch(name, shape, dtype):
        dram[name] = nc.dram_tensor(name, shape, dtype, kind="Internal").ap()

    scratch("q_parts", (HEADS, 3, D, B, TOK), F16)
    scratch("k_parts", (HEADS, 3, D, B, TOK + REGS), F16)
    scratch("q_other", (HEADS, D, B, TOK), F16)
    scratch("k_other", (HEADS, D, B, TOK + REGS), F16)
    scratch("row_bias", (HEADS, 2 * SIDE, B, TOK), F16)
    scratch("col_bias", (HEADS, 2 * KC, NS, B, TOK), F16)
    scratch("sums", (VW, HEADS, B, TOK), F32)
    scratch("inverse", (HEADS, ALL), F32)
    scratch("x1", (C, ALL), F32)

    with ExitStack() as whole:
        x = whole.enter_context(nc.sbuf_tensor("x", [128, CT, ALL + REGS], F32))
        values = whole.enter_context(nc.sbuf_tensor("values", [128, HEADS, B * TILES + 1, VW], F16))

        for layer in range(2):
            def phase(work, *args):
                with ExitStack() as ctx:
                    def sem(name):
                        return ctx.enter_context(nc.semaphore(name))

                    work(nc, ctx, *args, dram, sem)

            phase(group_norm, x, layer)
            phase(project, x, values, layer)
            if layer == 1:
                phase(position_bias)
            phase(attention, x, values, layer)
            phase(mix, x, layer)


def kernel(**inputs):
    import concourse.bacc as bacc
    from concourse.bass_utils import run_bass_kernel_spmd

    def array(name):
        return np.asarray(inputs[name])

    def by_channel(w):
        return w.reshape(HEADS, D, C).transpose(1, 0, 2).reshape(C, C)

    reach = np.minimum(2 * SIDE - 2 - np.arange(2 * SIDE - 1), array("L1_conv_rel_pos_h").shape[0] - 1)
    arrays = {
        "x": array("x").reshape(B, SIDE, NS, KC, C).transpose(4, 0, 2, 1, 3).reshape(C, ALL),
        "registers": array("L0_conv_registers").T,
        "w0": array("L0_conv_qkv_w").T, "b0": array("L0_conv_qkv_b").reshape(3 * CT, 128).T,
        "vb0": np.broadcast_to(array("L0_conv_qkv_b")[2 * C:], (128, C)),
        "ow0": by_channel(array("L0_conv_out_w").T), "ob0": array("L0_conv_out_b").reshape(CT, 128).T,
        "w1": array("L1_conv_qkv_w").T, "b1": array("L1_conv_qkv_b").reshape(3 * CT, 128).T,
        "vb1": np.broadcast_to(array("L1_conv_qkv_b")[2 * C:], (128, C)),
        "ow1": by_channel(array("L1_conv_proj_w").T), "ob1": array("L1_conv_proj_b").reshape(CT, 128).T,
        "tables": np.stack([array("L1_conv_rel_pos_h")[reach].T, array("L1_conv_rel_pos_w")[reach].T], axis=1),
        **shape_constants(),
    }
    arrays = {name: np.ascontiguousarray(a) for name, a in arrays.items()}

    nc = bacc.Bacc("TRN2", target_bir_lowering=False, num_devices=1)
    dram = {name: nc.dram_tensor("in_" + name, a.shape, mybir.dt.from_np(a.dtype), kind="ExternalInput").ap()
            for name, a in arrays.items()}
    dram["out"] = nc.dram_tensor("out_x", (C, ALL), F32, kind="ExternalOutput").ap()
    build(nc, dram)
    r = run_bass_kernel_spmd(nc, [{"in_" + name: a for name, a in arrays.items()}], core_ids=[0])
    return np.ascontiguousarray(r.results[0]["out_x"].reshape(C, B, NS, SIDE, KC).transpose(1, 3, 2, 4, 0)
                                .reshape(B, SIDE, SIDE, C))
```

```python
from contextlib import ExitStack

import numpy as np
import concourse.bass as bass
from concourse import mybir

F32 = mybir.dt.float32
F16 = mybir.dt.float16
BF16 = mybir.dt.bfloat16
ACT = mybir.ActivationFunctionType
ALU = mybir.AluOpType
AX = mybir.AxisListType

B, SIDE, C = 2, 48, 384
TOK = SIDE * SIDE
ALL = B * TOK
HEADS, D = 12, 32
REGS, WINDOW = 16, 7
CT = C // 128
GROUPS = 32
HPT = 128 // D
EPS = 1e-5
W_SCALE = 64.0
INV_SCALE = 256.0
Q_SCALE = float(D) ** -0.5

KR, KC = 8, 16
NA, NS = SIDE // KR, SIDE // KC
TILES = NA * NS
STRIP = SIDE * KC
UNIT = KR * SIDE
PIECE = 384
PIECES = TOK // PIECE
QT = UNIT // 128
HALO = WINDOW // 2
VW = 2 * D + 1
BIG = 32768.0
STAGES = HEADS * B

B_ROWS = 2 * SIDE + 1
M_ROW = 2 * SIDE


def due(count):
    return not isinstance(count, int) or count > 0


def each_stage(engine, stage):
    for b in range(B):
        stage(0, b)
    with engine.Fori(1, HEADS - 1) as h:
        for b in range(B):
            stage(h, b)
    for b in range(B):
        stage(HEADS - 1, b)


def window_of(tile, size, limit):
    return max(0, tile * size - HALO), min(limit, (tile + 1) * size + HALO)


def rects(a):
    out = []
    for c in range(NS):
        lo, hi = window_of(c, KC, SIDE)
        at = 0
        for ka, r0, r1 in ((a, 0, KR), (a - 1, 0, HALO), (a + 1, KR - HALO, KR)):
            if 0 <= ka < NA:
                out.append((c, ka, r0, r1, lo, hi, at))
                at += (r1 - r0) * (hi - lo)
    return out


def rect_width(a, c):
    return sum((r1 - r0) * (hi - lo) for s, _, r0, r1, lo, hi, _ in rects(a) if s == c)


def shape_constants():
    t = np.arange(TOK)
    strip, row, col = t // STRIP, (t % STRIP) // KC, t % KC
    one_a = np.zeros((32, TOK + REGS), np.float16)
    for i in range(KC):
        one_a[i, :TOK] = one_a[KC + i, :TOK] = col == i
    one_b = np.zeros((B_ROWS, NA + 1, 128), np.float16)
    for a in range(NA):
        for k in range(128):
            one_b[a * KR + k // KC, a, k] = one_b[SIDE + a * KR + k // KC, a, k] = 1
    one_m = np.zeros((2 * SIDE, TOK + REGS), np.float16)
    one_m[t // SIDE, t] = 1
    one_m[SIDE + t % SIDE, t] = 1
    pos = np.arange(SIDE)
    start = np.clip(pos - HALO, 0, SIDE - WINDOW)
    outside = ~((pos[:, None] >= start[None]) & (pos[:, None] < start[None] + WINDOW))
    far = np.where(outside, -BIG, 0.0).astype(np.float16)
    far_row = far[:, t // SIDE]
    far_col = far[:, t % SIDE]
    mask_a = np.zeros((32, NS, TOK), np.float16)
    for c in range(NS):
        mask_a[:KC, c] = far_col[c * KC:(c + 1) * KC]
    mask_b = np.concatenate([far_row, np.zeros_like(far_row)])
    by_strip = row * SIDE + strip * KC + col
    mask_m = np.concatenate([far_row, far_col])[:, by_strip]
    ones_row = np.zeros((B_ROWS, NA + 1, 128), np.float16)
    ones_row[M_ROW] = 1
    group = np.arange(C) // (C // GROUPS)
    share = (group[:, None] == group[None]).astype(np.float32) / (C // GROUPS)
    share = share.reshape(CT, 128, C).transpose(1, 0, 2).copy()
    spread = (np.arange(2 * HEADS)[:, None] % HEADS == np.arange(C)[None] % HEADS) / INV_SCALE
    spread = spread.astype(np.float16).reshape(2 * HEADS, CT, 128)
    big = np.float16(BIG)
    return {
        "one_a0": one_a * big, "one_a1": one_a, "one_b0": one_b * big + ones_row,
        "one_b1": one_b + ones_row, "one_m0": one_m * big, "one_m1": one_m,
        "mask_a": mask_a, "mask_b": mask_b, "mask_m": mask_m, "share": share, "spread": spread,
        "ident": np.eye(128, dtype=np.float16),
    }


def split_halves(ap):
    halves = ap.bitcast(F16)
    return halves[:, 0::2], halves[:, 1::2]


def norm_and_project(nc, ctx, x, values, layer, dram, sem):
    w_hi = ctx.enter_context(nc.sbuf_tensor(f"w_hi{layer}", [128, CT, 3 * C], F16))
    w_lo = ctx.enter_context(nc.sbuf_tensor(f"w_lo{layer}", [128, CT, 3 * C], F16))
    with ExitStack() as own:
        group_norm(nc, own, x, w_hi, w_lo, layer, dram, sem)
    project(nc, ctx, x, w_hi, w_lo, values, layer, dram, sem)


def group_norm(nc, ctx, x, w_hi, w_lo, layer, dram, sem):
    w = ctx.enter_context(nc.sbuf_tensor(f"w{layer}", [128, CT, 3 * C], F32))
    regs = ctx.enter_context(nc.sbuf_tensor(f"regs{layer}", [128, CT * REGS], F32))
    normed = ctx.enter_context(nc.sbuf_tensor(f"gn_out{layer}", [128, 3, TOK // 3], F32))
    w_in = sem(f"w_in{layer}")
    w_steps = sem(f"w_steps{layer}")
    if layer == 0:
        regs_in = sem("regs_in")
        regs_hi_ready = sem("regs_hi_ready")
    normed_ready = sem(f"gn_out_ready{layer}")
    x_hi_ready = sem(f"x_hi_ready{layer}")
    x_lo_ready = [sem(f"x_lo_ready{layer}_{i}") for i in range(2)]
    pieces = [(t, b, b * TOK + i * TOK // 3) for b in range(B) for i in range(3) for t in range(CT)]
    stats = ctx.enter_context(nc.sbuf_tensor(f"stats{layer}", [128, CT * B * NA, 6], F32))
    chan = ctx.enter_context(nc.sbuf_tensor(f"chan{layer}", [128, CT * B, 2], F32))
    share = ctx.enter_context(nc.sbuf_tensor(f"share{layer}", [128, CT, C], F32))
    means = ctx.enter_context(nc.sbuf_tensor(f"means{layer}", [128, CT, B], F32))
    second = ctx.enter_context(nc.sbuf_tensor(f"second{layer}", [128, CT, B], F32))
    off = ctx.enter_context(nc.sbuf_tensor(f"off{layer}", [128, CT, B], F32))
    gmean = ctx.enter_context(nc.sbuf_tensor(f"gmean{layer}", [128, CT, B], F32))
    gvar = ctx.enter_context(nc.sbuf_tensor(f"gvar{layer}", [128, CT, B], F32))
    sd = ctx.enter_context(nc.sbuf_tensor(f"sd{layer}", [128, CT, B], F32))
    rstd = ctx.enter_context(nc.sbuf_tensor(f"rstd{layer}", [128, CT, B], F32))
    sums = ctx.enter_context(nc.psum_tensor(f"sums{layer}", [128, 2, 512], F32))
    x_in = [sem(f"x_in{layer}_{i}") for i in range(CT * B if layer == 0 else 0)]
    share_in = sem(f"share_in{layer}")
    chain = sem(f"gn_chain{layer}")
    second_ready = sem(f"second_ready{layer}")
    means_ready = sem(f"means_ready{layer}")
    mean_sum = sem(f"mean_sum{layer}")
    var_sum = sem(f"var_sum{layer}")
    var_ready = sem(f"var_ready{layer}")
    sd_ready = sem(f"sd_ready{layer}")

    def x_low(queue, engine, i):
        t, _, at = pieces[i]
        hi, lo = split_halves(x[:, t, at:at + TOK // 3])
        queue.wait_ge(x_hi_ready, i + 1)
        engine.tensor_tensor(lo, normed[:, i % 3, :], hi, ALU.subtract).then_inc(x_lo_ready[i % 2], 1)

    with nc.Block() as block:
        @block.sync
        def _(sp):
            if layer == 0:
                for i in range(CT * B):
                    t, b = i // B, i % B
                    sp.dma_start(x[:, t, b * TOK:(b + 1) * TOK],
                                 dram["x"][t * 128:(t + 1) * 128, b * TOK:(b + 1) * TOK]).then_inc(x_in[i], 16)
            sp.dma_start(share[:, :, :], dram["share"]).then_inc(share_in, 16)
            sp.dma_start(w[:, :, :], dram[f"w{layer}"].rearrange("(t p) n -> p t n", p=128)).then_inc(w_in, 16)
            if layer == 0:
                sp.dma_start(regs[:, :].rearrange("p (t n) -> p t n", n=REGS),
                             dram["registers"].rearrange("(t p) n -> p t n", p=128)).then_inc(regs_in, 16)

        @block.vector
        def _(dve):
            steps = [0]

            def link(ins):
                steps[0] += 1
                ins.then_inc(chain, 1)
                dve.wait_ge(chain, steps[0])

            for i in range(CT * B):
                t, b = i // B, i % B
                if layer == 0:
                    dve.wait_ge(x_in[i], 16)
                for a in range(NA):
                    at = b * TOK + a * UNIT
                    last = nc.vector.bn_stats(stats[:, i * NA + a, :], x[:, t, at:at + UNIT])
            link(last)
            for i in range(CT * B):
                last = nc.vector.bn_aggr(chan[:, i, :], stats[:, i * NA:(i + 1) * NA, :])
            link(last)
            by_chan = chan[:, :, :].rearrange("p (t b) s -> p t b s", b=B)
            nc.vector.tensor_copy(means[:, :, :], by_chan[:, :, :, 0]).then_inc(means_ready, 1)
            dve.wait_ge(mean_sum, 1)
            link(nc.vector.tensor_copy(gmean[:, :, :], sums[:, 0, 0:CT * B].rearrange("p (t b) -> p t b", b=B)))
            link(nc.vector.tensor_tensor(off[:, :, :], by_chan[:, :, :, 0], gmean[:, :, :], ALU.subtract))
            link(nc.vector.tensor_tensor(off[:, :, :], off[:, :, :], off[:, :, :], ALU.mult))
            nc.vector.tensor_tensor(second[:, :, :], off[:, :, :], by_chan[:, :, :, 1],
                                    ALU.add).then_inc(second_ready, 1)
            dve.wait_ge(var_sum, 1)
            nc.vector.tensor_scalar(gvar[:, :, :], sums[:, 1, 0:CT * B].rearrange("p (t b) -> p t b", b=B),
                                    EPS, None, ALU.add).then_inc(var_ready, 1)
            dve.wait_ge(sd_ready, 1)
            link(nc.vector.reciprocal(rstd[:, :, :], sd[:, :, :]))
            for i, (t, b, at) in enumerate(pieces):
                if i >= 3:
                    dve.wait_ge(x_lo_ready[(i - 3) % 2], (i - 3) // 2 + 1)
                nc.vector.tensor_scalar(normed[:, i % 3, :], x[:, t, at:at + TOK // 3], gmean[:, t, b:b + 1],
                                        rstd[:, t, b:b + 1], ALU.subtract, ALU.mult).then_inc(normed_ready, 1)
                if i % 2 == 0 and i > 0:
                    x_low(dve, nc.vector, i - 1)
            x_low(dve, nc.vector, len(pieces) - 1)

        @block.tensor
        def _(pe):
            pe.wait_ge(share_in, 16)
            for ready, done, src, bank in ((means_ready, mean_sum, means, 0), (second_ready, var_sum, second, 1)):
                pe.wait_ge(ready, 1)
                for to in range(CT):
                    for t in range(CT):
                        last = nc.tensor.matmul(sums[:, bank, to * B:(to + 1) * B],
                                                share[:, t, to * 128:(to + 1) * 128], src[:, t, :],
                                                start=(t == 0), stop=(t == CT - 1))
                last.then_inc(done, 1)

        @block.scalar
        def _(act):
            act.wait_ge(w_in, 16)
            nc.scalar.activation(w[:, :, :], w[:, :, :], ACT.Identity, scale=W_SCALE).then_inc(w_steps, 1)
            act.wait_ge(w_steps, 1)
            nc.scalar.activation(w_hi[:, :, :], w[:, :, :], ACT.Identity).then_inc(w_steps, 1)
            if layer == 0:
                act.wait_ge(regs_in, 16)
                for t in range(CT):
                    hi, _ = split_halves(x[:, t, ALL:ALL + REGS])
                    last = nc.scalar.activation(hi, regs[:, t * REGS:(t + 1) * REGS], ACT.Identity)
                last.then_inc(regs_hi_ready, 1)
            act.wait_ge(var_ready, 1)
            nc.scalar.activation(sd[:, :, :], gvar[:, :, :], ACT.Sqrt).then_inc(sd_ready, 1)
            for i, (t, b, at) in enumerate(pieces):
                act.wait_ge(normed_ready, i + 1)
                hi, _ = split_halves(x[:, t, at:at + TOK // 3])
                nc.scalar.activation(hi, normed[:, i % 3, :], ACT.Identity).then_inc(x_hi_ready, 1)

        @block.gpsimd
        def _(pool):
            pool.wait_ge(w_steps, 2)
            nc.gpsimd.tensor_tensor(w_lo[:, :, :], w[:, :, :], w_hi[:, :, :], ALU.subtract)
            if layer == 0:
                pool.wait_ge(regs_hi_ready, 1)
                for t in range(CT):
                    hi, lo = split_halves(x[:, t, ALL:ALL + REGS])
                    nc.gpsimd.tensor_tensor(lo, regs[:, t * REGS:(t + 1) * REGS], hi, ALU.subtract)
            for i in range(0, len(pieces), 2):
                x_low(pool, nc.gpsimd, i)


def project(nc, ctx, x, w_hi, w_lo, values, layer, dram, sem):
    regs = REGS if layer == 0 else 0
    bias = ctx.enter_context(nc.sbuf_tensor(f"bias{layer}", [128, 2 * CT], F32))
    q_bias = ctx.enter_context(nc.sbuf_tensor(f"q_bias{layer}", [128, CT], F32))
    v_bias = ctx.enter_context(nc.sbuf_tensor(f"v_bias{layer}", [128, C], F32))
    full = ctx.enter_context(nc.sbuf_tensor(f"full{layer}", [128, 3, UNIT], F32))
    v_full = ctx.enter_context(nc.sbuf_tensor(f"v_full{layer}", [128, 3, C], F32))
    high = ctx.enter_context(nc.sbuf_tensor(f"high{layer}", [128, 2, TOK + REGS], F16))
    low = ctx.enter_context(nc.sbuf_tensor(f"low{layer}", [128, 2, TOK + REGS], F16))
    other = ctx.enter_context(nc.sbuf_tensor(f"other{layer}", [128, 2, TOK + REGS], F16))
    acc = ctx.enter_context(nc.psum_tensor(f"acc{layer}", [128, 8, 512], F32))
    bias_in = sem(f"bias_in{layer}")
    acc_ready = sem(f"acc_ready{layer}")
    full_ready = sem(f"full_ready{layer}")
    bias_ready = sem(f"bias_ready{layer}")
    high_ready = sem(f"high_ready{layer}")
    low_ready = sem(f"low_ready{layer}")
    other_ready = sem(f"other_ready{layer}")
    stored = [sem(f"stored{layer}_{i}") for i in range(2)]
    v_acc_ready = sem(f"v_acc_ready{layer}")
    v_full_ready = sem(f"v_full_ready{layer}")
    v_high_ready = sem(f"v_high_ready{layer}")
    v_low_ready = sem(f"v_low_ready{layer}")

    blocks = [(m, b) for m in range(2 * CT) for b in range(B)]

    def chunks(m, b):
        return NA + (1 if regs and m >= CT and b == 0 else 0)

    def width(a):
        return UNIT if a < NA else regs

    def source(b, a):
        return (b * TOK + a * UNIT) if a < NA else ALL

    def by_strip(buf, a):
        return buf[:, TOK:TOK + REGS] if a == NA else buf[:, a * UNIT:(a + 1) * UNIT]

    def by_row(buf, a):
        if a == NA:
            return buf[:, TOK:TOK + REGS]
        rows = UNIT // KC
        c, r = a * rows // SIDE, a * rows % SIDE
        return buf[:, 0:TOK].rearrange("p (r c s) -> p c r s", c=NS, s=KC)[:, c, r:r + rows]

    def as_rows(ap, a):
        return ap if a == NA else ap.rearrange("p (r s) -> p r s", s=KC)

    def targets(m, bufs):
        hi, lo, order = bufs
        if m < CT:
            q, other_q = dram["q_parts"], dram["q_other"]
            return [(q[:, 0], hi), (q[:, 1], hi), (q[:, 2], lo)] + ([(other_q, order)] if layer == 0 else [])
        k = dram["k_parts"]
        return [(k[:, 0], hi), (k[:, 1], lo), (k[:, 2], hi), (dram["k_other"], order)]

    def reordered(n):
        return n if layer == 0 else max(0, n - CT * B * NA)

    def store_count(i):
        out = 0
        for j in range(i % 2, i + 1, 2):
            m, b = blocks[j]
            out += 16 * len(targets(m, (0, 1, 2))) * (2 if chunks(m, b) > NA else 1)
        return out

    v_tiles = [(b, j) for b in range(B) for j in range(TILES)] + ([(B, 0)] if regs else [])
    total = sum(chunks(m, b) for m, b in blocks)

    with nc.Block() as block:
        @block.sync
        def _(sp):
            sp.dma_start(bias[:, :], dram[f"b{layer}"][:, 0:2 * CT]).then_inc(bias_in, 16)
            sp.dma_start(v_bias[:, :], dram[f"vb{layer}"]).then_inc(bias_in, 16)
            done = 0
            for i, (m, b) in enumerate(blocks):
                done += chunks(m, b)
                sp.wait_ge(high_ready, done)
                sp.wait_ge(low_ready, done)
                par = i % 2
                heads = slice((m % CT) * HPT, (m % CT + 1) * HPT)
                n = TOK + (regs if chunks(m, b) > NA else 0)
                if reordered(done):
                    sp.wait_ge(other_ready, reordered(done))
                for dst, buf in targets(m, (high, low, other)):
                    sp.dma_start(dst[heads, :, b, 0:n], buf[:, par, 0:n]).then_inc(stored[par], 16)
                    if n > TOK:
                        sp.dma_start(dst[heads, :, 1, TOK:n], buf[:, par, TOK:n]).then_inc(stored[par], 16)
            for par in range(2):
                sp.wait_ge(stored[par], store_count(len(blocks) - 2 + par))

        @block.tensor
        def _(pe):
            n = 0
            for m, b in blocks:
                cols = slice(m * 128, (m + 1) * 128)
                for a in range(chunks(m, b)):
                    if n >= 4:
                        pe.wait_ge(full_ready, n - 3)
                    at = source(b, a)
                    dst = acc[:, n % 4, 0:width(a)]
                    for t in range(CT):
                        hi, lo = split_halves(x[:, t, at:at + width(a)])
                        nc.tensor.matmul(dst, w_hi[:, t, cols], hi, start=(t == 0), stop=False)
                        nc.tensor.matmul(dst, w_hi[:, t, cols], lo, start=False, stop=False)
                        last = nc.tensor.matmul(dst, w_lo[:, t, cols], hi, start=False, stop=(t == CT - 1))
                    last.then_inc(acc_ready, 1)
                    n += 1
            cols = slice(2 * C, 3 * C)
            for n, (b, j) in enumerate(v_tiles):
                if n >= 4:
                    pe.wait_ge(v_full_ready, n - 3)
                p = 128 if b < B else REGS
                at = b * TOK + j * 128 if b < B else ALL
                dst = acc[0:p, 4 + n % 4, 0:C]
                for t in range(CT):
                    hi, lo = split_halves(x[:, t, at:at + p])
                    nc.tensor.matmul(dst, hi, w_hi[:, t, cols], start=(t == 0), stop=False)
                    nc.tensor.matmul(dst, hi, w_lo[:, t, cols], start=False, stop=False)
                    last = nc.tensor.matmul(dst, lo, w_hi[:, t, cols], start=False, stop=(t == CT - 1))
                last.then_inc(v_acc_ready, 1)

        @block.scalar
        def _(act):
            act.wait_ge(bias_in, 32)
            nc.scalar.activation(q_bias[:, :], bias[:, 0:CT], ACT.Identity, scale=Q_SCALE).then_inc(bias_ready, 1)
            act.wait_ge(bias_ready, 1)
            n = 0
            for m, b in blocks:
                for a in range(chunks(m, b)):
                    act.wait_ge(acc_ready, n + 1)
                    if n >= 3:
                        act.wait_ge(low_ready, n - 2)
                        if reordered(n - 2):
                            act.wait_ge(other_ready, reordered(n - 2))
                    col = q_bias[:, m:m + 1] if m < CT else bias[:, m:m + 1]
                    nc.scalar.activation(full[:, n % 3, 0:width(a)], acc[:, n % 4, 0:width(a)], ACT.Identity,
                                         bias=col, scale=(Q_SCALE if m < CT else 1.0) / W_SCALE).then_inc(full_ready, 1)
                    n += 1
            for n, (b, j) in enumerate(v_tiles):
                act.wait_ge(v_full_ready, n + 1)
                p = 128 if b < B else REGS
                tile = b * TILES + j
                nc.scalar.activation(values[0:p, :, tile, 0:D],
                                     v_full[0:p, n % 3, :].rearrange("p (h d) -> p h d", d=D),
                                     ACT.Identity).then_inc(v_high_ready, 1)

        @block.vector
        def _(dve):
            n = 0
            for i, (m, b) in enumerate(blocks):
                par = i % 2
                if i >= 2:
                    dve.wait_ge(stored[par], store_count(i - 2))
                for a in range(chunks(m, b)):
                    src = full[:, n % 3, 0:width(a)]
                    if m < CT:
                        src = as_rows(src, a)
                        hi, lo = by_row(high[:, par, :], a), by_row(low[:, par, :], a)
                    else:
                        hi, lo = by_strip(high[:, par, :], a), by_strip(low[:, par, :], a)
                    dve.wait_ge(full_ready, n + 1)
                    nc.vector.tensor_copy(hi, src).then_inc(high_ready, 1)
                    dve.wait_ge(high_ready, n + 1)
                    nc.vector.tensor_tensor(lo, src, hi, ALU.subtract).then_inc(low_ready, 1)
                    n += 1
            for n, (b, j) in enumerate(v_tiles):
                p = 128 if b < B else REGS
                tile = b * TILES + j
                dve.wait_ge(v_acc_ready, n + 1)
                if n >= 3:
                    dve.wait_ge(v_low_ready, n - 2)
                nc.vector.scalar_tensor_tensor(v_full[0:p, n % 3, :], acc[0:p, 4 + n % 4, 0:C], 1.0 / W_SCALE,
                                               v_bias[0:p, :], ALU.mult, ALU.add).then_inc(v_full_ready, 1)

        @block.gpsimd
        def _(pool):
            nc.gpsimd.memset(values[:, :, :, 2 * D:VW], 1.0)
            n = 0
            for i, (m, b) in enumerate(blocks):
                par = i % 2
                for a in range(chunks(m, b)):
                    if reordered(n + 1) == reordered(n):
                        n += 1
                        continue
                    if a == 0 and i >= 2:
                        pool.wait_ge(stored[par], store_count(i - 2))
                    pool.wait_ge(full_ready, n + 1)
                    src = full[:, n % 3, 0:width(a)]
                    if m < CT:
                        dst = by_strip(other[:, par, :], a)
                    else:
                        dst, src = by_row(other[:, par, :], a), as_rows(src, a)
                    nc.gpsimd.tensor_copy(dst, src).then_inc(other_ready, 1)
                    n += 1
            for n, (b, j) in enumerate(v_tiles):
                p = 128 if b < B else REGS
                tile = b * TILES + j
                pool.wait_ge(v_high_ready, n + 1)
                nc.gpsimd.tensor_tensor(values[0:p, :, tile, D:2 * D],
                                        v_full[0:p, n % 3, :].rearrange("p (h d) -> p h d", d=D),
                                        values[0:p, :, tile, 0:D], ALU.subtract).then_inc(v_low_ready, 1)


def position_bias(nc, ctx, dram, sem):
    GQ = 4
    NG = SIDE // GQ
    table32 = ctx.enter_context(nc.sbuf_tensor("table32", [128, 2, 2 * SIDE], F32))
    table_hi = ctx.enter_context(nc.sbuf_tensor("table_hi", [128, 2, 2 * SIDE], F16))
    table = ctx.enter_context(nc.sbuf_tensor("table", [128, 2, 2 * SIDE], F16))
    q = ctx.enter_context(nc.sbuf_tensor("bias_q", [128, 2, B, TOK], F16))
    hi = ctx.enter_context(nc.sbuf_tensor("bias_hi", [SIDE, 2, B, TOK], F16))
    lo = ctx.enter_context(nc.sbuf_tensor("bias_lo", [SIDE, 2, B, TOK], F16))
    acc = ctx.enter_context(nc.psum_tensor("bias_acc", [128, 8, 512], F32))
    tables_in = sem("tables_in")
    table_hi_ready = sem("table_hi_ready")
    table_ready = sem("table_ready")
    q_in = [sem(f"q_in{i}") for i in range(2)]
    acc_ready = sem("bias_acc_ready")
    hi_ready = sem("bias_hi_ready")
    lo_ready = sem("bias_lo_ready")
    stored = [sem(f"bias_stored{i}") for i in range(2)]

    def groups():
        return [(axis, g) for axis in range(2) for g in range(NG)]

    def banked(n, axis):
        v = acc[0:SIDE, n % 8, 0:B * GQ * SIDE].rearrange("p (b g x) -> p b g x", b=B, g=GQ)
        return v if axis == 0 else v.rearrange("p b g x -> p b x g")

    def placed(buf, axis, g):
        if axis == 0:
            return buf[:, axis, :, g * GQ * SIDE:(g + 1) * GQ * SIDE].rearrange("p b (g x) -> p b g x", g=GQ)
        return buf[:, axis, :, :].rearrange("p b (x w) -> p b x w", w=SIDE)[:, :, :, g * GQ:(g + 1) * GQ]

    with nc.Block() as block:
        @block.sync
        def _(sp):
            for part in range(3):
                sp.dma_start(table32[part * D:(part + 1) * D, :, 0:2 * SIDE - 1], dram["tables"]).then_inc(tables_in, 16)

            def load(h, par):
                sp.dma_start(q[0:3 * D, par], dram["q_parts"][bass.ds(h, 1)].rearrange("o p d b n -> (o p d) b n")).then_inc(q_in[par], 16)

            def store(h, axis):
                sp.wait_ge(lo_ready, h * 2 * NG + (axis + 1) * NG)
                if axis == 0:
                    sp.dma_start(dram["row_bias"][bass.ds(h, 1), 0:SIDE].rearrange("o p b n -> (o p) b n"),
                                 hi[:, 0]).then_inc(stored[0], 16)
                    sp.dma_start(dram["row_bias"][bass.ds(h, 1), SIDE:2 * SIDE].rearrange("o p b n -> (o p) b n"),
                                 lo[:, 0]).then_inc(stored[0], 16)
                else:
                    for part, buf in enumerate((hi, lo)):
                        dst = dram["col_bias"][bass.ds(h, 1), part * KC:(part + 1) * KC]
                        sp.dma_start(dst.rearrange("o p c b n -> (o c) p b n"), buf[:, 1]).then_inc(stored[1], 16)

            def two_heads(h, more):
                if due(h):
                    sp.wait_ge(acc_ready, h * 2 * NG)
                load(h + 1, 1)
                for axis in range(2):
                    store(h, axis)
                if more:
                    load(h + 2, 0)
                for axis in range(2):
                    store(h + 1, axis)

            load(0, 0)
            two_heads(0, True)
            with sp.Fori(1, HEADS // 2 - 1) as pair:
                two_heads(pair * 2, True)
            two_heads(HEADS - 2, False)
            for axis in range(2):
                sp.wait_ge(stored[axis], 32 * HEADS)

        @block.tensor
        def _(pe):
            pe.wait_ge(table_ready, 2)

            def two_heads(pair):
                for par in range(2):
                    h = pair * 2 + par
                    pe.wait_ge(q_in[par], (pair + 1) * 16)
                    for n, (axis, g) in enumerate(groups()):
                        if due(h * 2 * NG + n - 7):
                            pe.wait_ge(lo_ready, h * 2 * NG + n - 7)
                        for j in range(GQ):
                            x = g * GQ + j
                            dst = acc[0:SIDE, n % 8, 0:B * GQ * SIDE] \
                                .rearrange("p (b g x) -> p b g x", b=B, g=GQ)[:, :, j]
                            src = q[0:3 * D, par].rearrange("p b (r w) -> p b r w", w=SIDE)
                            src = src[:, :, x, :] if axis == 0 else src[:, :, :, x]
                            last = nc.tensor.matmul(dst, table[0:3 * D, axis, SIDE - 1 - x:2 * SIDE - 1 - x], src,
                                                    start=True, stop=True)
                        last.then_inc(acc_ready, 1)

            two_heads(0)
            with pe.Fori(1, HEADS // 2) as pair:
                two_heads(pair)

        @block.scalar
        def _(act):
            def head(h):
                for n, (axis, g) in enumerate(groups()):
                    if g == 0 and due(h):
                        act.wait_ge(stored[axis], h * 32)
                    act.wait_ge(acc_ready, h * 2 * NG + n + 1)
                    nc.scalar.activation(placed(hi, axis, g), banked(n, axis), ACT.Identity).then_inc(hi_ready, 1)

            head(0)
            with act.Fori(1, HEADS) as h:
                head(h)

        @block.vector
        def _(dve):
            dve.wait_ge(tables_in, 48)
            used = table32[0:3 * D, :, 0:2 * SIDE - 1]
            parts = table_hi[0:3 * D, :, 0:2 * SIDE - 1]
            nc.vector.tensor_copy(parts, used).then_inc(table_hi_ready, 1)
            dve.wait_ge(table_hi_ready, 1)
            nc.vector.tensor_copy(table[0:3 * D, :, 0:2 * SIDE - 1], parts).then_inc(table_hi_ready, 1)
            dve.wait_ge(table_hi_ready, 2)
            nc.vector.tensor_tensor(table[D:2 * D, :, 0:2 * SIDE - 1], table32[D:2 * D, :, 0:2 * SIDE - 1],
                                    table_hi[D:2 * D, :, 0:2 * SIDE - 1], ALU.subtract).then_inc(table_ready, 2)
            with dve.Fori(0, HEADS) as h:
                for n, (axis, g) in enumerate(groups()):
                    dve.wait_ge(hi_ready, h * 2 * NG + n + 1)
                    nc.vector.tensor_tensor(placed(lo, axis, g), banked(n, axis), placed(hi, axis, g),
                                            ALU.subtract).then_inc(lo_ready, 1)


def attention(nc, ctx, x, values, layer, dram, sem):
    local = layer == 0
    keys_n = TOK + (REGS if local else 0)
    key_tiles = TILES + (1 if local else 0)
    PAIRS = TILES // 2
    PITCH = max(rect_width(a, c) for a in range(NA) for c in range(NS))
    SLOT = NS * PITCH + UNIT if local else 2 * UNIT
    RING = 3
    LAG = 2
    PER_UNIT = 1 if local else PAIRS
    STEPS = NA * PER_UNIT
    SCORES = STEPS * (NS + 1 if local else 1)
    BY_DVE = 208
    ADDITIONS = 1 if local else 2
    SUM_ROW = 2 * D if local else 3 * D
    STEP_PIECES = QT if local else 2
    UNIT_PIECES = STEP_PIECES * PER_UNIT
    ROW_STEP = min(6, PER_UNIT - 1)
    BEFORE_ROW = ROW_STEP * STEP_PIECES
    LATE = NA - (2 if local else 1)
    UNIT_BANKS = UNIT_PIECES + 1

    q_a = ctx.enter_context(nc.sbuf_tensor(f"q_a{layer}", [128, 2, NS, TOK], F16))
    q_b = ctx.enter_context(nc.sbuf_tensor(f"q_b{layer}", [B_ROWS, 2, TOK], F16))
    k_a = ctx.enter_context(nc.sbuf_tensor(f"k_a{layer}", [128, 2, keys_n], F16))
    k_b = ctx.enter_context(nc.sbuf_tensor(f"k_b{layer}", [B_ROWS, NA + 1, 128], F16))
    q_m = ctx.enter_context(nc.sbuf_tensor(f"q_m{layer}", [128, 2, TOK], F16))
    k_m = ctx.enter_context(nc.sbuf_tensor(f"k_m{layer}", [128, 2, keys_n], F16))
    v = ctx.enter_context(nc.sbuf_tensor(f"v{layer}", [128, 2, key_tiles, VW], F16))
    ident = ctx.enter_context(nc.sbuf_tensor(f"ident{layer}", [128, 128], F16))
    prob = ctx.enter_context(nc.sbuf_tensor(f"prob{layer}", [128, RING, SLOT], F32))
    prob_low = ctx.enter_context(nc.sbuf_tensor(f"prob_low{layer}", [128, RING, SLOT], F16))
    part_max = ctx.enter_context(nc.sbuf_tensor(f"part_max{layer}", [128, QT, PIECES], F32))
    tile_max = ctx.enter_context(nc.sbuf_tensor(f"tile_max{layer}", [128, 2, QT], F32))
    neg_max = ctx.enter_context(nc.sbuf_tensor(f"neg_max{layer}", [128, QT], F16))
    max_row = ctx.enter_context(nc.sbuf_tensor(f"max_row{layer}", [QT, NA, 128], F16))
    warm = ctx.enter_context(nc.sbuf_tensor(f"warm{layer}", [1, 1], F32))
    result = x[0:D + 1].rearrange("p t n -> p (t n)")[:, 0:2 * TOK].rearrange("p (b n) -> p b n", b=B)
    scores = ctx.enter_context(nc.psum_tensor(f"scores{layer}", [128, 4, 512], F32))
    max_acc = ctx.enter_context(nc.psum_tensor(f"max_acc{layer}", [128, 2, 512], F32))
    out_acc = ctx.enter_context(nc.psum_tensor(f"out_acc{layer}", [128, 2, 512], F32))

    first_in = sem(f"first_in{layer}")
    consts_in = sem(f"consts_in{layer}")
    main_in = [sem(f"main_in{layer}_{i}") for i in range(2)]
    max_in = [sem(f"max_in{layer}_{i}") for i in range(2)]
    score_ready = sem(f"score_ready{layer}")
    prob_ready = sem(f"prob_ready{layer}")
    low_by_dve = sem(f"low_by_dve{layer}")
    low_by_pool = sem(f"low_by_pool{layer}")
    prob_used = sem(f"prob_used{layer}")
    bank_filled = sem(f"bank_filled{layer}")
    bank_read = sem(f"bank_read{layer}")
    tile_max_ready = sem(f"tile_max_ready{layer}")
    neg_ready = sem(f"neg_ready{layer}")
    rows_in = [sem(f"rows_in{layer}_{i}") for i in range(2)]
    rows_copied = sem(f"rows_copied{layer}")
    first_added = sem(f"first_added{layer}")
    result_ready = sem(f"result_ready{layer}")
    result_out = [sem(f"result_out{layer}_{i}") for i in range(2)]

    FIRST = 16 * (3 if local else 2)
    CONSTS = 16 * (1 + (2 * 3 + 2 if local else 2 + 1))
    MAIN = 16 * (4 if local else 5)
    MAX = 16 * (2 if local else 4)
    RESULT = 16
    ROWS = 16 * QT

    def piece_use(stage, i):
        u, j = i // UNIT_PIECES, i % UNIT_PIECES
        if isinstance(stage, int) and stage == 0 and u == 0:
            return i, i % 2
        within = u * UNIT_BANKS - 1 + j + (1 if j >= BEFORE_ROW else 0)
        return stage * (NA * UNIT_BANKS) + within, within % 2

    def row_use(stage, u):
        within = (u + 1) * UNIT_BANKS - 1
        if not (isinstance(stage, int) and stage == STAGES - 1 and u == NA - 1):
            within += BEFORE_ROW
        return stage * (NA * UNIT_BANKS) + within, within % 2

    def near(a, c):
        return *window_of(a, KR, SIDE), *window_of(c, KC, SIDE)

    def in_rows(bank):
        return bank.rearrange("p (r c s) -> p r c s", c=NS, s=KC)

    def in_strips(rows, b, a):
        return result[rows, b].rearrange("p (c r s) -> p r c s", c=NS, s=KC)[:, a * KR:(a + 1) * KR]

    def is_first(n):
        return isinstance(n, int) and n == 0

    def is_last(n):
        return isinstance(n, int) and n == STAGES - 1

    with nc.Block() as block:
        @block.sync
        def _(sp):
            def max_consts(par, done):
                sp.dma_start(k_m[32:128, par], dram[f"one_m{layer}"][:, 0:keys_n]).then_inc(done, 16)
                if local:
                    sp.dma_start(q_m[32:128, par], dram["mask_m"]).then_inc(done, 16)

            def load_main(h, b):
                src = dram["q_parts"][bass.ds(h, 1), :, :, b].rearrange("o p d n -> (o p d) n")
                src = src.unsqueeze(1).to_broadcast((3 * D, NS, TOK))
                sp.dma_start(q_a[0:3 * D, b], src).then_inc(main_in[b], 16)
                src = dram["k_parts"][bass.ds(h, 1), :, :, b, 0:keys_n].rearrange("o p d n -> (o p d) n")
                sp.dma_start(k_a[0:3 * D, b], src).then_inc(main_in[b], 16)
                own = values[:, bass.ds(h, 1), b * TILES:(b + 1) * TILES].rearrange("p o t n -> p (o t) n")
                sp.dma_start(v[:, b, 0:TILES], own).then_inc(main_in[b], 16)
                if local:
                    own = values[0:REGS, bass.ds(h, 1), B * TILES].rearrange("p o n -> p (o n)")
                    sp.dma_start(v[0:REGS, b, TILES], own).then_inc(main_in[b], 16)
                else:
                    sp.dma_start(q_a[96:128, b],
                                 dram["col_bias"][bass.ds(h, 1), :, :, b].rearrange("o p c n -> (o p) c n")) \
                        .then_inc(main_in[b], 16)
                    sp.dma_start(q_b[0:2 * SIDE, b],
                                 dram["row_bias"][bass.ds(h, 1), :, b].rearrange("o p n -> (o p) n")) \
                        .then_inc(main_in[b], 16)

            def load_max(h, b):
                src = dram["q_other"] if local else dram["q_parts"][:, 0]
                sp.dma_start(q_m[0:D, b], src[bass.ds(h, 1), :, b].rearrange("o d n -> (o d) n")) \
                    .then_inc(max_in[b], 16)
                src = dram["k_other"][bass.ds(h, 1), :, b, 0:keys_n]
                sp.dma_start(k_m[0:D, b], src.rearrange("o d n -> (o d) n")).then_inc(max_in[b], 16)
                if not local:
                    sp.dma_start(q_m[D:D + SIDE, b],
                                 dram["row_bias"][bass.ds(h, 1), 0:SIDE, b].rearrange("o p n -> (o p) n")) \
                        .then_inc(max_in[b], 16)
                    sp.dma_start(q_m[D + SIDE:128, b],
                                 dram["col_bias"][bass.ds(h, 1), 0:KC, :, b].rearrange("o p c n -> (o c) p n")) \
                        .then_inc(max_in[b], 16)

            def store(h, b):
                sp.wait_ge(result_ready, (h * B + b + 1) * NA)
                sp.dma_start(dram["sums"][:, bass.ds(h, 1), b].rearrange("p o n -> (p o) n"),
                             result[:, b]).then_inc(result_out[b], 16)

            def place_rows(stage, b, late):
                u0, u1 = (LATE, NA) if late else (0, LATE)
                sp.wait_ge(bank_read, row_use(stage, u1 - 1)[0] + 1)
                dst = q_b[M_ROW:M_ROW + 1, b, u0 * UNIT:u1 * UNIT]
                for t in range(QT):
                    src = max_row[t:t + 1, u0:u1]
                    if local:
                        to = dst.rearrange("o (r c s) -> o c r s", c=NS, s=KC)[:, t]
                        src = src.rearrange("o u (r s) -> o (u r) s", s=KC)
                    else:
                        to = dst.rearrange("o (u t n) -> o t u n", t=QT, n=128)[:, t]
                    sp.dma_start(to, src).then_inc(rows_in[late], 16)

            load_max(0, 0)
            max_consts(0, first_in)
            sp.dma_start(ident[:, :], dram["ident"]).then_inc(first_in, 16)
            load_main(0, 0)
            sp.dma_start(k_b[:, :, :], dram[f"one_b{layer}"]).then_inc(consts_in, 16)
            for par in range(2):
                sp.dma_start(k_a[96:128, par], dram[f"one_a{layer}"][:, 0:keys_n]).then_inc(consts_in, 16)
                if local:
                    sp.dma_start(q_a[96:128, par], dram["mask_a"]).then_inc(consts_in, 16)
                    sp.dma_start(q_b[0:2 * SIDE, par], dram["mask_b"]).then_inc(consts_in, 16)
            load_max(0, 1)
            max_consts(1, consts_in)
            place_rows(0, 0, False)

            def stage(h, b):
                n = h * B + b
                place_rows(n, b, True)
                if not is_last(n) and not is_last(n + 1 if isinstance(n, int) else n):
                    sp.wait_ge(bank_read, piece_use(n, NA * UNIT_PIECES - 1)[0] + 1)
                    load_max(h + 1, b)
                if not is_last(n):
                    if not is_first(n):
                        sp.wait_ge(prob_used, n * STEPS)
                    load_main(h + b, 1 - b)
                if not is_first(n):
                    store(h - (1 - b), 1 - b)
                if not is_last(n):
                    place_rows(n + 1, 1 - b, False)

            each_stage(sp, stage)
            store(HEADS - 1, 1)
            for b in range(B):
                sp.wait_ge(result_out[b], RESULT * HEADS)

        @block.tensor
        def _(pe):
            def max_pieces(stage, b, k, part):
                for i in range(k * STEP_PIECES + part, (k + 1) * STEP_PIECES if part else k * STEP_PIECES + 1):
                    use, bank = piece_use(stage, i)
                    if due(use - 1):
                        pe.wait_ge(bank_read, use - 1)
                    if local:
                        r0, r1, c0, c1 = near(k, i % QT)
                        n = (r1 - r0) * (c1 - c0)
                        at = i % QT * STRIP + k * 128
                        keys = k_m[:, b, 0:TOK].rearrange("p (r w) -> p r w", w=SIDE)[:, r0:r1, c0:c1]
                        nc.tensor.matmul(max_acc[:, bank, 0:n], q_m[:, b, at:at + 128], keys, start=True, stop=True)
                        last = nc.tensor.matmul(max_acc[:, bank, n:n + REGS], q_m[:, b, at:at + 128],
                                                k_m[:, b, TOK:keys_n], start=True, stop=True)
                    else:
                        tile, piece = i // PIECES, i % PIECES
                        last = nc.tensor.matmul(max_acc[:, bank, 0:PIECE], q_m[:, b, tile * 128:(tile + 1) * 128],
                                                k_m[:, b, piece * PIECE:(piece + 1) * PIECE],
                                                start=True, stop=True)
                    last.then_inc(bank_filled, 1)

            def row_of_max(stage, u):
                pe.wait_ge(neg_ready, stage * NA + u + 1)
                use, bank = row_use(stage, u)
                pe.wait_ge(bank_read, use - 1)
                nc.tensor.matmul(max_acc[0:QT, bank, 0:128], neg_max[:, :], ident[:, :],
                                 start=True, stop=True).then_inc(bank_filled, 1)

            def key_product(bank, tile, queries_a, queries_b, b):
                kind = tile % NA if tile < TILES else NA
                rows = 128 if tile < TILES else REGS
                nc.tensor.matmul(bank, k_a[:, b, tile * 128:tile * 128 + rows], queries_a, start=True, stop=False)
                return nc.tensor.matmul(bank, k_b[:, kind, 0:rows], queries_b, start=False, stop=True)

            def row_is_placed(n, a):
                if a in (0, LATE):
                    pe.wait_ge(rows_in[a == LATE], ROWS * (n + 1))

            def scores_full(n, b, p):
                a, k = p // PAIRS, p % PAIRS
                if k == 0:
                    row_is_placed(n, a)
                if due(n * STEPS + p - 1):
                    pe.wait_ge(prob_ready, n * STEPS + p - 1)
                for j in range(2):
                    tile = 2 * k + j
                    last = key_product(scores[:, 2 * (p % 2) + j, 0:UNIT], tile,
                                       q_a[:, b, tile // NA, a * UNIT:(a + 1) * UNIT],
                                       q_b[:, b, a * UNIT:(a + 1) * UNIT], b)
                last.then_inc(score_ready, 1)

            def weighted_full(n, b, p):
                a, k = p // PAIRS, p % PAIRS
                pe.wait_ge(low_by_dve, n * STEPS + p + 1)
                pe.wait_ge(low_by_pool, n * STEPS + p + 1)
                if k == 0 and due(n * NA + a - 1):
                    pe.wait_ge(result_ready, n * NA + a - 1)
                high = prob[:, p % RING, :].bitcast(BF16)[:, 1::2]
                low = prob_low[:, p % RING, :]
                for j in range(2):
                    tile = 2 * k + j
                    cut = slice(j * UNIT, (j + 1) * UNIT)
                    last = value_products(out_acc[:, a % 2, 0:UNIT], v[:, b, tile, :], high[:, cut], low[:, cut],
                                          tile == 0, tile == TILES - 1)
                last.then_inc(prob_used, 1)

            def value_products(bank, values_of, high, low, start, stop):
                if local:
                    nc.tensor.matmul(bank[0:VW], values_of, high, start=start, stop=False)
                    return nc.tensor.matmul(bank[0:VW], values_of, low, start=False, stop=stop)
                nc.tensor.matmul(bank[0:2 * D], values_of[:, 0:2 * D], high, start=start, stop=stop)
                nc.tensor.matmul(bank[SUM_ROW:SUM_ROW + 1], values_of[:, 2 * D:VW], high, start=start, stop=False)
                nc.tensor.matmul(bank[2 * D:3 * D], values_of[:, 0:D], low, start=start, stop=stop)
                return nc.tensor.matmul(bank[SUM_ROW:SUM_ROW + 1], values_of[:, 2 * D:VW], low, start=False, stop=stop)

            def scores_local(n, b, a):
                row_is_placed(n, a)
                cut = slice(a * UNIT, (a + 1) * UNIT)
                for c in range(NS + 1):
                    if due(n * SCORES + (a - 1) * (NS + 1) + c + 1):
                        pe.wait_ge(prob_ready, n * SCORES + (a - 1) * (NS + 1) + c + 1)
                    if c == NS:
                        last = key_product(scores[0:REGS, c, 0:UNIT], TILES, q_a[:, b, 0, cut], q_b[:, b, cut], b)
                        last.then_inc(score_ready, 1)
                        continue
                    qa = q_a[:, b, c, cut].rearrange("p (r w) -> p r w", w=SIDE)
                    qb = q_b[:, b, cut].rearrange("p (r w) -> p r w", w=SIDE)
                    for s, ka, r0, r1, lo, hi, at in rects(a):
                        if s == c:
                            w = (r1 - r0) * (hi - lo)
                            last = key_product(scores[:, c, at:at + w], c * NA + ka,
                                               qa[:, r0:r1, lo:hi], qb[:, r0:r1, lo:hi], b)
                    last.then_inc(score_ready, 1)

            def weighted_local(n, b, a):
                pe.wait_ge(low_by_dve, n * STEPS + a + 1)
                pe.wait_ge(low_by_pool, n * STEPS + a + 1)
                if due(n * NA + a - 1):
                    pe.wait_ge(result_ready, n * NA + a - 1)
                high = prob[:, a % RING, :].bitcast(BF16)[:, 1::2]
                low = prob_low[:, a % RING, :]
                sums = out_acc[:, a % 2, 0:UNIT]
                cut = slice(NS * PITCH, NS * PITCH + UNIT)
                value_products(sums, v[0:REGS, b, TILES, :], high[0:REGS, cut], low[0:REGS, cut], True, False)
                todo = rects(a)
                for i, (c, ka, r0, r1, lo, hi, at) in enumerate(todo):
                    w = (r1 - r0) * (hi - lo)
                    cut = slice(c * PITCH + at, c * PITCH + at + w)
                    dst = sums.rearrange("p (r w) -> p r w", w=SIDE)[:, r0:r1, lo:hi]
                    last = value_products(dst, v[:, b, c * NA + ka, :], high[:, cut], low[:, cut],
                                          False, i == len(todo) - 1)
                last.then_inc(prob_used, 1)

            compute, use = (scores_local, weighted_local) if local else (scores_full, weighted_full)

            pe.wait_ge(first_in, FIRST)
            pe.wait_ge(max_in[0], MAX)
            for u in range(NA):
                for k in range(PER_UNIT):
                    if u > 0 and k == ROW_STEP:
                        row_of_max(0, u - 1)
                    max_pieces(0, 0, u * PER_UNIT + k, 0)
                    max_pieces(0, 0, u * PER_UNIT + k, 1)

            def stage(h, b):
                n = h * B + b
                pe.wait_ge(main_in[b], (h + 1) * MAIN)
                if not is_last(n):
                    pe.wait_ge(max_in[1 - b], (h + 1 + b) * MAX)
                for k in range(STEPS):
                    compute(n, b, k)
                    if k % PER_UNIT == ROW_STEP:
                        if k < PER_UNIT:
                            row_of_max(n, NA - 1)
                        elif not is_last(n):
                            row_of_max(n + 1, k // PER_UNIT - 1)
                    if not is_last(n):
                        max_pieces(n + 1, 1 - b, k, 0)
                    if k >= LAG:
                        use(n, b, k - LAG)
                    elif not is_first(n):
                        use(n - 1, 1 - b, k - LAG + STEPS)
                    if not is_last(n):
                        max_pieces(n + 1, 1 - b, k, 1)

            pe.wait_ge(consts_in, CONSTS)
            each_stage(pe, stage)
            for k in range(STEPS - LAG, STEPS):
                use(STAGES - 1, 1, k)

        @block.scalar
        def _(act):
            def take_result(h, b, a):
                n = h * B + b
                act.wait_ge(prob_used, n * STEPS + (a + 1) * PER_UNIT)
                if a == 0 and due(h):
                    act.wait_ge(result_out[b], h * RESULT)
                for bank, rows in ((out_acc[0:D, a % 2, 0:UNIT], slice(0, D)),
                                   (out_acc[SUM_ROW:SUM_ROW + 1, a % 2, 0:UNIT], slice(D, D + 1))):
                    nc.scalar.activation(in_strips(rows, b, a), in_rows(bank), ACT.Identity).then_inc(rows_copied, 1)

            act.wait_ge(first_in, FIRST)
            nc.scalar.activation(warm[:, :], ident[0:1, 0:1], ACT.Exp)

            def exps(n, k):
                free = n * STEPS + k - RING + 1
                for c in range(NS + 1 if local else 1):
                    act.wait_ge(score_ready, n * SCORES + k * (SCORES // STEPS) + c + 1)
                    if c == 0 and due(free):
                        act.wait_ge(prob_used, free)
                    if local:
                        p = 128 if c < NS else REGS
                        w = rect_width(k, c) if c < NS else UNIT
                        dst, src = prob[0:p, k % RING, c * PITCH:c * PITCH + w], scores[0:p, c, 0:w]
                    else:
                        dst = prob[:, k % RING, :].rearrange("p (j n) -> p j n", j=2)
                        src = scores[:, 2 * (k % 2):2 * (k % 2) + 2, 0:UNIT]
                    nc.scalar.activation(dst, src, ACT.Exp).then_inc(prob_ready, 1)

            def stage(h, b):
                n = h * B + b
                for k in range(STEPS):
                    exps(n, k)
                    u = (k - LAG) // PER_UNIT
                    if (k - LAG) % PER_UNIT == PER_UNIT - 1:
                        if u >= 0:
                            take_result(h, b, u)
                        elif not is_first(n):
                            take_result(h - (1 - b), 1 - b, NA + u)

            each_stage(act, stage)
            for a in range(NA - (LAG - 1) // PER_UNIT - 1, NA):
                take_result(HEADS - 1, 1, a)

        def add_rows(n, b, a, part):
            dst = in_strips(slice(0, D), b, a)
            if part == 0:
                nc.vector.wait_ge(rows_copied, 2 * (n * NA + a + 1))
            else:
                nc.vector.wait_ge(first_added, n * NA + a + 1)
            rows = slice((part + 1) * D, (part + 2) * D)
            nc.vector.tensor_tensor(dst, in_rows(out_acc[rows, a % 2, 0:UNIT]), dst, ALU.add) \
                .then_inc(result_ready if part == ADDITIONS - 1 else first_added, 1)

        def low_part(engine, n, k, done):
            ours = engine is nc.vector
            if local:
                of_dve = (0, 2) if k % 2 == 0 else (0,)
                parts = of_dve if ours else [c for c in range(NS + 1) if c not in of_dve]
            else:
                parts = (0,)
            for c in parts:
                if local:
                    p = 128 if c < NS else REGS
                    cut = slice(c * PITCH, c * PITCH + (rect_width(k, c) if c < NS else UNIT))
                else:
                    p = 128
                    cut = slice(0, BY_DVE) if ours else slice(BY_DVE, SLOT)
                engine.wait_ge(prob_ready, n * SCORES + k * (SCORES // STEPS) + c + 1)
                last = engine.tensor_tensor(prob_low[0:p, k % RING, cut], prob[0:p, k % RING, cut],
                                            prob[0:p, k % RING, :].bitcast(BF16)[:, 1::2][:, cut], ALU.subtract)
            last.then_inc(done, 1)

        @block.vector
        def _(dve):
            def maxima(stage, k):
                for i in range(k * STEP_PIECES, (k + 1) * STEP_PIECES):
                    use, bank = piece_use(stage, i)
                    dve.wait_ge(bank_filled, use + 1)
                    if local:
                        r0, r1, c0, c1 = near(k, i % QT)
                        w = (r1 - r0) * (c1 - c0) + REGS
                        dst = tile_max[:, k % 2, i % QT:i % QT + 1]
                    else:
                        w, j = PIECE, i % UNIT_PIECES
                        dst = part_max[:, j // PIECES, j % PIECES:j % PIECES + 1]
                    nc.vector.reduce_max(dst, max_acc[:, bank, 0:w], axis=AX.X).then_inc(bank_read, 1)

            def unit_max(stage, u):
                unit = stage * NA + u
                dve.wait_ge(bank_read, piece_use(stage, (u + 1) * UNIT_PIECES - 1)[0] + 1)
                if not local:
                    nc.vector.reduce_max(tile_max[:, u % 2], part_max[:, :, :], axis=AX.X).then_inc(tile_max_ready, 1)
                    dve.wait_ge(tile_max_ready, unit + 1)
                nc.vector.tensor_scalar(neg_max[:, :], tile_max[:, u % 2], -1.0, None, ALU.mult).then_inc(neg_ready, 1)

            def add_last_rows(n, b, k):
                for part in range(ADDITIONS):
                    u, rest = divmod(k - 1 - part - LAG, PER_UNIT)
                    if rest == PER_UNIT - 1:
                        if u >= 0:
                            add_rows(n, b, u, part)
                        elif not is_first(n):
                            add_rows(n - 1, 1 - b, NA + u, part)

            def take_row(stage, u):
                use, bank = row_use(stage, u)
                dve.wait_ge(bank_filled, use + 1)
                if u in (0, LATE) and due(stage):
                    dve.wait_ge(rows_in[u == LATE], ROWS * stage)
                nc.vector.tensor_copy(max_row[:, u], max_acc[0:QT, bank, 0:128]).then_inc(bank_read, 1)

            for u in range(NA):
                for k in range(PER_UNIT):
                    if u > 0 and k == ROW_STEP:
                        take_row(0, u - 1)
                    maxima(0, u * PER_UNIT + k)
                unit_max(0, u)

            def stage(h, b):
                n = h * B + b
                for k in range(STEPS):
                    if k >= 1:
                        low_part(nc.vector, n, k - 1, low_by_dve)
                    elif not is_first(n):
                        low_part(nc.vector, n - 1, STEPS - 1, low_by_dve)
                    if local:
                        add_last_rows(n, b, k)
                    if k % PER_UNIT == ROW_STEP:
                        if k < PER_UNIT:
                            take_row(n, NA - 1)
                        elif not is_last(n):
                            take_row(n + 1, k // PER_UNIT - 1)
                    if not is_last(n):
                        maxima(n + 1, k)
                    if not is_last(n) and k % PER_UNIT == PER_UNIT - 1:
                        unit_max(n + 1, k // PER_UNIT)
                    if not local:
                        add_last_rows(n, b, k)

            each_stage(dve, stage)
            low_part(nc.vector, STAGES - 1, STEPS - 1, low_by_dve)
            for a in range(NA - LAG // PER_UNIT - 1, NA):
                for part in range(ADDITIONS):
                    add_rows(STAGES - 1, 1, a, part)

        @block.gpsimd
        def _(pool):
            def stage(h, b):
                for k in range(STEPS):
                    low_part(nc.gpsimd, h * B + b, k, low_by_pool)

            each_stage(pool, stage)


def mix(nc, ctx, x, layer, dram, sem):
    w = ctx.enter_context(nc.sbuf_tensor(f"ow{layer}", [128, CT, C], F32))
    w_hi = ctx.enter_context(nc.sbuf_tensor(f"ow_hi{layer}", [128, CT, C], F16))
    w_lo = ctx.enter_context(nc.sbuf_tensor(f"ow_lo{layer}", [128, CT, C], F16))
    bias = ctx.enter_context(nc.sbuf_tensor(f"ob{layer}", [128, CT], F32))
    spread = ctx.enter_context(nc.sbuf_tensor(f"spread{layer}", [2 * HEADS, CT, 128], F16))
    totals = ctx.enter_context(nc.sbuf_tensor(f"totals{layer}", [128, HEADS * ALL // 128], F32))
    inverse = ctx.enter_context(nc.sbuf_tensor(f"inverse{layer}", [128, HEADS * ALL // 128], F32))
    scaled = ctx.enter_context(nc.sbuf_tensor(f"scaled{layer}", [128, HEADS * ALL // 128], F32))
    inverse_parts = ctx.enter_context(nc.sbuf_tensor(f"inverse_parts{layer}", [128, 2, HEADS * ALL // 128], F16))
    by_head = ctx.enter_context(nc.sbuf_tensor(f"by_head{layer}", [2 * HEADS, ALL], F16))
    heads = ctx.enter_context(nc.sbuf_tensor(f"heads{layer}", [128, 3, CT, UNIT], F32))
    normed = ctx.enter_context(nc.sbuf_tensor(f"normed{layer}", [128, CT, UNIT], F32))
    normed_hi = ctx.enter_context(nc.sbuf_tensor(f"normed_hi{layer}", [128, 2, CT, UNIT], F16))
    normed_lo = ctx.enter_context(nc.sbuf_tensor(f"normed_lo{layer}", [128, 2, CT, UNIT], F16))
    mixed = ctx.enter_context(nc.sbuf_tensor(f"mixed{layer}", [128, 2, CT, UNIT], F32))
    acc = ctx.enter_context(nc.psum_tensor(f"mix_acc{layer}", [128, 4, 512], F32))
    factor = ctx.enter_context(nc.psum_tensor(f"factor{layer}", [128, 4, 512], F32))
    w_in = sem(f"ow_in{layer}")
    w_steps = sem(f"ow_steps{layer}")
    w_lo_ready = sem(f"ow_lo_ready{layer}")
    consts_in = sem(f"mix_consts_in{layer}")
    totals_in = sem(f"totals_in{layer}")
    inverse_steps = sem(f"inverse_steps{layer}")
    inverse_out = sem(f"inverse_out{layer}")
    by_head_in = sem(f"by_head_in{layer}")
    unit_in = [sem(f"unit_in{layer}_{i}") for i in range(3)]
    factor_ready = sem(f"factor_ready{layer}")
    normed_ready = sem(f"normed_ready{layer}")
    normed_hi_ready = sem(f"normed_hi_ready{layer}")
    normed_lo_ready = sem(f"normed_lo_ready{layer}")
    acc_ready = sem(f"mix_acc_ready{layer}")
    mixed_ready = sem(f"mixed_ready{layer}")
    added = sem(f"added{layer}")
    out_done = sem(f"out_done{layer}")
    UNITS = B * NA
    src_x = dram["x"] if layer == 0 else dram["x1"]
    dst_x = dram["x1"] if layer == 0 else dram["out"]

    def columns(ap, u):
        return ap[:, u * UNIT:(u + 1) * UNIT].rearrange("(t p) n -> p t n", p=128)

    with nc.Block() as block:
        @block.sync
        def _(sp):
            sp.dma_start(totals[:, :], dram["sums"][D].rearrange("h b n -> (h b n)")
                         .rearrange("(p n) -> p n", p=128)).then_inc(totals_in, 16)

            def load(u):
                b, a = u // NA, u % NA
                if u >= 3:
                    sp.wait_ge(normed_ready, u - 2)
                src = dram["sums"][0:D, :, b, a * UNIT:(a + 1) * UNIT].rearrange("d h n -> (d h) n")
                sp.dma_start(heads[:, u % 3], src.rearrange("(t p) n -> p t n", p=128)).then_inc(unit_in[u % 3], 16)
                sp.dma_start(x[:, :, u * UNIT:(u + 1) * UNIT], columns(src_x, u)).then_inc(unit_in[u % 3], 16)

            sp.dma_start(w[:, :, :], dram[f"ow{layer}"].rearrange("(t p) n -> p t n", p=128)).then_inc(w_in, 16)
            load(0)
            sp.dma_start(bias[:, :], dram[f"ob{layer}"]).then_inc(consts_in, 16)
            sp.dma_start(spread[:, :, :], dram["spread"]).then_inc(consts_in, 16)
            sp.wait_ge(inverse_steps, 4)
            sp.dma_start(dram["inverse"].rearrange("k h n -> k (h n)").rearrange("k (p n) -> p k n", p=128),
                         inverse_parts[:, :, :]).then_inc(inverse_out, 16)
            sp.wait_ge(inverse_out, 16)
            sp.dma_start(by_head[:, :], dram["inverse"].rearrange("k h n -> (k h) n")).then_inc(by_head_in, 16)
            load(1)
            load(2)
            for u in range(UNITS):
                if u + 3 < UNITS:
                    load(u + 3)
                sp.wait_ge(added, u + 1)
                sp.dma_start(columns(dst_x, u), x[:, :, u * UNIT:(u + 1) * UNIT]).then_inc(out_done, 16)
            sp.wait_ge(out_done, 16 * UNITS)

        @block.gpsimd
        def _(pool):
            pool.wait_ge(w_steps, 2)
            nc.gpsimd.tensor_tensor(w_lo[:, :, :], w[:, :, :], w_hi[:, :, :], ALU.subtract).then_inc(w_lo_ready, 1)

        @block.vector
        def _(dve):
            dve.wait_ge(totals_in, 16)
            nc.vector.reciprocal(inverse[:, :], totals[:, :]).then_inc(inverse_steps, 1)
            dve.wait_ge(inverse_steps, 1)
            nc.vector.tensor_scalar(scaled[:, :], inverse[:, :], INV_SCALE, None, ALU.mult).then_inc(inverse_steps, 1)
            nc.vector.tensor_scalar(inverse_parts[:, 0], inverse[:, :], INV_SCALE, None,
                                    ALU.mult).then_inc(inverse_steps, 1)
            dve.wait_ge(inverse_steps, 3)
            nc.vector.tensor_tensor(inverse_parts[:, 1], scaled[:, :], inverse_parts[:, 0],
                                    ALU.subtract).then_inc(inverse_steps, 1)

            def normalise(u):
                dve.wait_ge(unit_in[u % 3], 32 * (u // 3 + 1))
                dve.wait_ge(factor_ready, u + 1)
                if u > 0:
                    dve.wait_ge(normed_lo_ready, u)
                nc.vector.tensor_tensor(normed[:, :, :], factor[:, 0:CT, 0:UNIT], heads[:, u % 3],
                                        ALU.mult).then_inc(normed_ready, 1)
                dve.wait_ge(normed_hi_ready, u + 1)
                if u >= 2:
                    dve.wait_ge(acc_ready, (u - 1) * CT)
                nc.vector.tensor_tensor(normed_lo[:, u % 2], normed[:, :, :], normed_hi[:, u % 2],
                                        ALU.subtract).then_inc(normed_lo_ready, 1)

            normalise(0)
            for u in range(UNITS):
                if u + 1 < UNITS:
                    normalise(u + 1)
                dve.wait_ge(mixed_ready, (u + 1) * CT)
                dst = x[:, :, u * UNIT:(u + 1) * UNIT]
                nc.vector.tensor_tensor(dst, mixed[:, u % 2], dst, ALU.add).then_inc(added, 1)

        @block.scalar
        def _(act):
            act.wait_ge(w_in, 16)
            nc.scalar.activation(w[:, :, :], w[:, :, :], ACT.Identity, scale=W_SCALE).then_inc(w_steps, 1)
            act.wait_ge(w_steps, 1)
            nc.scalar.activation(w_hi[:, :, :], w[:, :, :], ACT.Identity).then_inc(w_steps, 1)

            def high(u):
                act.wait_ge(normed_ready, u + 1)
                if u >= 2:
                    act.wait_ge(acc_ready, (u - 1) * CT)
                nc.scalar.activation(normed_hi[:, u % 2], normed[:, :, :], ACT.Identity).then_inc(normed_hi_ready, 1)

            high(0)
            act.wait_ge(consts_in, 32)
            for u in range(UNITS):
                if u + 1 < UNITS:
                    high(u + 1)
                if u >= 2:
                    act.wait_ge(added, u - 1)
                for to in range(CT):
                    n = u * CT + to
                    act.wait_ge(acc_ready, n + 1)
                    nc.scalar.activation(mixed[:, u % 2, to], acc[:, n % 4, 0:UNIT], ACT.Identity,
                                         bias=bias[:, to:to + 1], scale=1.0 / W_SCALE).then_inc(mixed_ready, 1)

        @block.tensor
        def _(pe):
            def factors(u):
                if u > 0:
                    pe.wait_ge(normed_ready, u)
                for t in range(CT):
                    last = nc.tensor.matmul(factor[:, t, 0:UNIT], spread[:, t, :], by_head[:, u * UNIT:(u + 1) * UNIT],
                                            start=True, stop=True)
                last.then_inc(factor_ready, 1)

            pe.wait_ge(consts_in, 32)
            pe.wait_ge(by_head_in, 16)
            factors(0)
            pe.wait_ge(w_lo_ready, 1)
            for u in range(UNITS):
                if u + 1 < UNITS:
                    factors(u + 1)
                pe.wait_ge(normed_lo_ready, u + 1)
                for to in range(CT):
                    n = u * CT + to
                    cols = slice(to * 128, (to + 1) * 128)
                    dst = acc[:, n % 4, 0:UNIT]
                    if n >= 4:
                        pe.wait_ge(mixed_ready, n - 3)
                    for t in range(CT):
                        hi, lo = normed_hi[:, u % 2, t], normed_lo[:, u % 2, t]
                        nc.tensor.matmul(dst, w_hi[:, t, cols], hi, start=(t == 0), stop=False)
                        nc.tensor.matmul(dst, w_hi[:, t, cols], lo, start=False, stop=False)
                        last = nc.tensor.matmul(dst, w_lo[:, t, cols], hi, start=False, stop=(t == CT - 1))
                    last.then_inc(acc_ready, 1)


def build(nc, dram):
    def scratch(name, shape, dtype):
        dram[name] = nc.dram_tensor(name, shape, dtype, kind="Internal").ap()

    scratch("q_parts", (HEADS, 3, D, B, TOK), F16)
    scratch("k_parts", (HEADS, 3, D, B, TOK + REGS), F16)
    scratch("q_other", (HEADS, D, B, TOK), F16)
    scratch("k_other", (HEADS, D, B, TOK + REGS), F16)
    scratch("row_bias", (HEADS, 2 * SIDE, B, TOK), F16)
    scratch("col_bias", (HEADS, 2 * KC, NS, B, TOK), F16)
    scratch("sums", (D + 1, HEADS, B, TOK), F32)
    scratch("inverse", (2, HEADS, ALL), F16)
    scratch("x1", (C, ALL), F32)

    with ExitStack() as whole:
        x = whole.enter_context(nc.sbuf_tensor("x", [128, CT, ALL + REGS], F32))
        values = whole.enter_context(nc.sbuf_tensor("values", [128, HEADS, B * TILES + 1, VW], F16))

        for layer in range(2):
            def phase(work, *args):
                with ExitStack() as ctx:
                    def sem(name):
                        return ctx.enter_context(nc.semaphore(name))

                    work(nc, ctx, *args, dram, sem)

            phase(norm_and_project, x, values, layer)
            if layer == 1:
                phase(position_bias)
            phase(attention, x, values, layer)
            phase(mix, x, layer)


def kernel(**inputs):
    import concourse.bacc as bacc
    from concourse.bass_utils import run_bass_kernel_spmd

    def array(name):
        return np.asarray(inputs[name])

    def by_channel(w):
        return w.reshape(HEADS, D, C).transpose(1, 0, 2).reshape(C, C)

    reach = np.minimum(2 * SIDE - 2 - np.arange(2 * SIDE - 1), array("L1_conv_rel_pos_h").shape[0] - 1)
    arrays = {
        "x": array("x").reshape(B, SIDE, NS, KC, C).transpose(4, 0, 2, 1, 3).reshape(C, ALL),
        "registers": array("L0_conv_registers").T,
        "w0": array("L0_conv_qkv_w").T, "b0": array("L0_conv_qkv_b").reshape(3 * CT, 128).T,
        "vb0": np.broadcast_to(array("L0_conv_qkv_b")[2 * C:], (128, C)),
        "ow0": by_channel(array("L0_conv_out_w").T), "ob0": array("L0_conv_out_b").reshape(CT, 128).T,
        "w1": array("L1_conv_qkv_w").T, "b1": array("L1_conv_qkv_b").reshape(3 * CT, 128).T,
        "vb1": np.broadcast_to(array("L1_conv_qkv_b")[2 * C:], (128, C)),
        "ow1": by_channel(array("L1_conv_proj_w").T), "ob1": array("L1_conv_proj_b").reshape(CT, 128).T,
        "tables": np.stack([array("L1_conv_rel_pos_h")[reach].T, array("L1_conv_rel_pos_w")[reach].T], axis=1),
        **shape_constants(),
    }
    arrays = {name: np.ascontiguousarray(a) for name, a in arrays.items()}

    nc = bacc.Bacc("TRN2", target_bir_lowering=False, num_devices=1)
    dram = {name: nc.dram_tensor("in_" + name, a.shape, mybir.dt.from_np(a.dtype), kind="ExternalInput").ap()
            for name, a in arrays.items()}
    dram["out"] = nc.dram_tensor("out_x", (C, ALL), F32, kind="ExternalOutput").ap()
    build(nc, dram)
    r = run_bass_kernel_spmd(nc, [{"in_" + name: a for name, a in arrays.items()}], core_ids=[0])
    return np.ascontiguousarray(r.results[0]["out_x"].reshape(C, B, NS, SIDE, KC).transpose(1, 3, 2, 4, 0)
                                .reshape(B, SIDE, SIDE, C))
```
